# Optimizing a Trainium2 kernel written in Bass

```python
import numpy as np
import jax
import jax.numpy as jnp

def _softmax(x, axis=-1):
    return jax.nn.softmax(x, axis=axis)

def _gelu(x):
    return jax.nn.gelu(x, approximate=True)

def _silu(x):
    return jax.nn.silu(x)

def _sigmoid(x):
    return jax.nn.sigmoid(x)

def _layernorm(x, axis=-1, eps=1e-05):
    m = jnp.mean(x, axis=axis, keepdims=True)
    v = jnp.var(x, axis=axis, keepdims=True)
    return (x - m) / jnp.sqrt(v + eps)

def _scatter_add(tgt, idx, src, axis=0):
    return tgt.at[idx].add(src)

def _segment_sum(src, seg, n):
    return jax.ops.segment_sum(src, seg, n)
kernel_name = 'mk_lm_tower_d2_tok_ids512_r4_74ded7'

def setup_inputs(seed: int=0):
    np.random.seed(seed)
    _w = jnp.asarray

    def _rec_inputs():
        import jax
        import jax.numpy as jnp
        _rk = jax.random.key(seed)
        x = jax.random.randint(jax.random.fold_in(_rk, 1), (32, 512), 0, 50257, jnp.int32)
        return x
    x = _rec_inputs()

    def _L0_tok_setup():
        import jax, jax.numpy as jnp
        import numpy as np
        D_MODEL = 128
        VOCAB = 50257
        BATCH = 8
        SEQ = 512

        def _positional_encoding(seq_len, d_model, dtype):
            pos = jnp.arange(1, seq_len + 1, dtype=jnp.float32)[:, None]
            i = jnp.arange(d_model)
            exponent = jnp.where(i % 2 == 0, i, i + 1).astype(jnp.float32) / d_model
            angle = pos / 10000.0 ** exponent
            pe = jnp.where(i % 2 == 0, jnp.cos(angle), jnp.sin(angle))
            return pe.astype(dtype)
        key = jax.random.key(seed)
        k1, k2, k3 = jax.random.split(key, 3)
        x = jax.random.randint(k1, (BATCH, SEQ), 0, VOCAB)
        W = jax.random.normal(k2, (D_MODEL, VOCAB), dtype=jnp.float32) * 0.02
        b = jax.random.normal(k3, (D_MODEL,), dtype=jnp.float32) * 0.02
        return {'x': x, 'W': W, 'b': b}
    _L0_tok_all = _L0_tok_setup()
    _L0_tok_in = {k: v for k, v in _L0_tok_all.items() if k in ('W', 'b')}
    del _L0_tok_all

    def _L0_attn_setup():
        import jax, jax.numpy as jnp
        import numpy as np
        B, T, D_MODEL, N_HEADS, D_FF = (2, 512, 128, 8, 512)
        D_HEAD = D_MODEL // N_HEADS
        EPS_LN = 1e-05
        DEN_MIN = 1e-06

        def layer_norm(x, g, b):
            mu = jnp.mean(x, axis=-1, keepdims=True)
            var = jnp.var(x, axis=-1, keepdims=True)
            return (x - mu) * jax.lax.rsqrt(var + EPS_LN) * g + b

        def causal_linear_attention(Q, K, V):
            KV = jnp.cumsum(K[..., :, None] * V[..., None, :], axis=2)
            z = jnp.cumsum(K, axis=2)
            num = jnp.einsum('bhtd,bhtdm->bhtm', Q, KV)
            den = jnp.maximum(jnp.einsum('bhtd,bhtd->bht', Q, z), DEN_MIN)[..., None]
            return num / den
        key = jax.random.key(seed)
        ks = jax.random.split(key, 12)

        def lin_w(k, din, dout):
            return jax.random.normal(k, (din, dout), jnp.float32) / np.sqrt(din).astype(np.float32)
        return {'x': jax.random.normal(ks[0], (B, T, D_MODEL), jnp.float32), 'ln1_g': jnp.ones((D_MODEL,), jnp.float32), 'ln1_b': jnp.zeros((D_MODEL,), jnp.float32), 'Wq': lin_w(ks[1], D_MODEL, D_MODEL), 'bq': jnp.zeros((D_MODEL,), jnp.float32), 'Wk': lin_w(ks[2], D_MODEL, D_MODEL), 'bk': jnp.zeros((D_MODEL,), jnp.float32), 'Wv': lin_w(ks[3], D_MODEL, D_MODEL), 'bv': jnp.zeros((D_MODEL,), jnp.float32), 'Wo': lin_w(ks[4], D_MODEL, D_MODEL), 'bo': jnp.zeros((D_MODEL,), jnp.float32), 'ln2_g': jnp.ones((D_MODEL,), jnp.float32), 'ln2_b': jnp.zeros((D_MODEL,), jnp.float32), 'W1': lin_w(ks[5], D_MODEL, D_FF), 'b1': jnp.zeros((D_FF,), jnp.float32), 'W2': lin_w(ks[6], D_FF, D_MODEL), 'b2': jnp.zeros((D_MODEL,), jnp.float32)}
    _L0_attn_all = _L0_attn_setup()
    _L0_attn_in = {k: v for k, v in _L0_attn_all.items() if k in ('ln1_g', 'ln1_b', 'Wq', 'bq', 'Wk', 'bk', 'Wv', 'bv', 'Wo', 'bo', 'ln2_g', 'ln2_b', 'W1', 'b1', 'W2', 'b2')}
    del _L0_attn_all

    def _L0_ffn_setup():
        import jax, jax.numpy as jnp
        import numpy as np
        D_MODEL = 128
        D_FF = 128
        N_EXPERTS = 16
        TOP_K = 3
        BATCH, SEQ = (1, 512)

        def _swiglu(combined):
            gate, up = jnp.split(combined, 2, axis=-1)
            return jax.nn.silu(gate) * up
        key = jax.random.key(seed)
        ks = jax.random.split(key, 6)
        x = jax.random.normal(ks[0], (BATCH, SEQ, D_MODEL), dtype=jnp.float32)
        gate_w = 0.01 * jax.random.normal(ks[1], (N_EXPERTS, D_MODEL), dtype=jnp.float32)
        expert_bias = jnp.zeros((N_EXPERTS,), dtype=jnp.float32)
        shared_gate_up = 0.02 * jax.random.normal(ks[2], (2 * D_FF, D_MODEL), dtype=jnp.float32)
        shared_down = 0.02 * jax.random.normal(ks[3], (D_MODEL, D_FF), dtype=jnp.float32)
        expert_gate_up = 0.02 * jax.random.normal(ks[4], (N_EXPERTS, 2 * D_FF, D_MODEL), dtype=jnp.float32)
        expert_down = 0.02 * jax.random.normal(ks[5], (N_EXPERTS, D_MODEL, D_FF), dtype=jnp.float32)
        return {'x': x, 'gate_w': gate_w, 'expert_bias': expert_bias, 'shared_gate_up': shared_gate_up, 'shared_down': shared_down, 'expert_gate_up': expert_gate_up, 'expert_down': expert_down}
    _L0_ffn_all = _L0_ffn_setup()
    _L0_ffn_in = {k: v for k, v in _L0_ffn_all.items() if k in ('gate_w', 'expert_bias', 'shared_gate_up', 'shared_down', 'expert_gate_up', 'expert_down')}
    del _L0_ffn_all

    def _L1_attn_setup():
        import jax, jax.numpy as jnp
        import numpy as np
        NUM_HEADS = 8
        key = jax.random.key(seed)
        k1, k2, k3 = jax.random.split(key, 3)
        B, N, C = (4, 512, 128)
        x = jax.random.normal(k1, (B, N, C), dtype=jnp.float32)
        q_w = jax.random.normal(k2, (C, C), dtype=jnp.float32) * 0.02
        kv_w = jax.random.normal(k3, (2 * C, C), dtype=jnp.float32) * 0.02
        return {'x': x, 'q_w': q_w, 'kv_w': kv_w}
    _L1_attn_all = _L1_attn_setup()
    _L1_attn_in = {k: v for k, v in _L1_attn_all.items() if k in ('q_w', 'kv_w')}
    del _L1_attn_all

    def _L1_ffn_setup():
        import jax, jax.numpy as jnp
        import numpy as np
        B, S, D, F, E = (8, 1024, 128, 512, 8)
        INIT_LAMBDA = 0.2
        LN_EPS = 1e-05
        LN_MERGE = 0.03
        key = jax.random.key(seed)
        ks = jax.random.split(key, 12)
        n = lambda k, shp, s=1.0: jax.random.normal(k, shp, dtype=jnp.float32) * s
        return {'hidden_states': n(ks[0], (B, S, D)), 'gfc1_w': n(ks[1], (D, D), 0.01), 'gfc1_b': jnp.zeros((D,), jnp.float32), 'gfc2_w': n(ks[2], (E, D), 0.01), 'gfc2_b': jnp.full((E,), INIT_LAMBDA, dtype=jnp.float32), 'W1': n(ks[3], (F, D), 0.02), 'b1': jnp.zeros((F,), jnp.float32), 'W2': n(ks[4], (D, F), 0.02), 'b2': jnp.zeros((D,), jnp.float32), 'ln_g': jnp.ones((D,), jnp.float32), 'ln_b': jnp.zeros((D,), jnp.float32), 'tv_W1': n(ks[5], (E, F, D), 0.02), 'tv_b1': n(ks[6], (E, F), 0.02), 'tv_W2': n(ks[7], (E, D, F), 0.02), 'tv_b2': n(ks[8], (E, D), 0.02), 'tv_ln_g': n(ks[9], (E, D), 0.02), 'tv_ln_b': n(ks[10], (E, D), 0.02)}
    _L1_ffn_all = _L1_ffn_setup()
    _L1_ffn_in = {k: v for k, v in _L1_ffn_all.items() if k in ('gfc1_w', 'gfc1_b', 'gfc2_w', 'gfc2_b', 'W1', 'b1', 'W2', 'b2', 'ln_g', 'ln_b', 'tv_W1', 'tv_b1', 'tv_W2', 'tv_b2', 'tv_ln_g', 'tv_ln_b')}
    del _L1_ffn_all
    return {'x': x, 'L0_tok_W': _L0_tok_in['W'], 'L0_tok_b': _L0_tok_in['b'], 'L0_attn_ln1_g': _L0_attn_in['ln1_g'], 'L0_attn_ln1_b': _L0_attn_in['ln1_b'], 'L0_attn_Wq': _L0_attn_in['Wq'], 'L0_attn_bq': _L0_attn_in['bq'], 'L0_attn_Wk': _L0_attn_in['Wk'], 'L0_attn_bk': _L0_attn_in['bk'], 'L0_attn_Wv': _L0_attn_in['Wv'], 'L0_attn_bv': _L0_attn_in['bv'], 'L0_attn_Wo': _L0_attn_in['Wo'], 'L0_attn_bo': _L0_attn_in['bo'], 'L0_attn_ln2_g': _L0_attn_in['ln2_g'], 'L0_attn_ln2_b': _L0_attn_in['ln2_b'], 'L0_attn_W1': _L0_attn_in['W1'], 'L0_attn_b1': _L0_attn_in['b1'], 'L0_attn_W2': _L0_attn_in['W2'], 'L0_attn_b2': _L0_attn_in['b2'], 'L0_ffn_gate_w': _L0_ffn_in['gate_w'], 'L0_ffn_expert_bias': _L0_ffn_in['expert_bias'], 'L0_ffn_shared_gate_up': _L0_ffn_in['shared_gate_up'], 'L0_ffn_shared_down': _L0_ffn_in['shared_down'], 'L0_ffn_expert_gate_up': _L0_ffn_in['expert_gate_up'], 'L0_ffn_expert_down': _L0_ffn_in['expert_down'], 'L1_attn_q_w': _L1_attn_in['q_w'], 'L1_attn_kv_w': _L1_attn_in['kv_w'], 'L1_ffn_gfc1_w': _L1_ffn_in['gfc1_w'], 'L1_ffn_gfc1_b': _L1_ffn_in['gfc1_b'], 'L1_ffn_gfc2_w': _L1_ffn_in['gfc2_w'], 'L1_ffn_gfc2_b': _L1_ffn_in['gfc2_b'], 'L1_ffn_W1': _L1_ffn_in['W1'], 'L1_ffn_b1': _L1_ffn_in['b1'], 'L1_ffn_W2': _L1_ffn_in['W2'], 'L1_ffn_b2': _L1_ffn_in['b2'], 'L1_ffn_ln_g': _L1_ffn_in['ln_g'], 'L1_ffn_ln_b': _L1_ffn_in['ln_b'], 'L1_ffn_tv_W1': _L1_ffn_in['tv_W1'], 'L1_ffn_tv_b1': _L1_ffn_in['tv_b1'], 'L1_ffn_tv_W2': _L1_ffn_in['tv_W2'], 'L1_ffn_tv_b2': _L1_ffn_in['tv_b2'], 'L1_ffn_tv_ln_g': _L1_ffn_in['tv_ln_g'], 'L1_ffn_tv_ln_b': _L1_ffn_in['tv_ln_b']}

def reference(x, L0_tok_W, L0_tok_b, L0_attn_ln1_g, L0_attn_ln1_b, L0_attn_Wq, L0_attn_bq, L0_attn_Wk, L0_attn_bk, L0_attn_Wv, L0_attn_bv, L0_attn_Wo, L0_attn_bo, L0_attn_ln2_g, L0_attn_ln2_b, L0_attn_W1, L0_attn_b1, L0_attn_W2, L0_attn_b2, L0_ffn_gate_w, L0_ffn_expert_bias, L0_ffn_shared_gate_up, L0_ffn_shared_down, L0_ffn_expert_gate_up, L0_ffn_expert_down, L1_attn_q_w, L1_attn_kv_w, L1_ffn_gfc1_w, L1_ffn_gfc1_b, L1_ffn_gfc2_w, L1_ffn_gfc2_b, L1_ffn_W1, L1_ffn_b1, L1_ffn_W2, L1_ffn_b2, L1_ffn_ln_g, L1_ffn_ln_b, L1_ffn_tv_W1, L1_ffn_tv_b1, L1_ffn_tv_W2, L1_ffn_tv_b2, L1_ffn_tv_ln_g, L1_ffn_tv_ln_b):
    import jax
    import jax.numpy as jnp

    def _L0_tok_ref(x, W, b):
        import jax, jax.numpy as jnp
        import numpy as np
        D_MODEL = 128
        VOCAB = 50257
        BATCH = 8
        SEQ = 512

        def _positional_encoding(seq_len, d_model, dtype):
            pos = jnp.arange(1, seq_len + 1, dtype=jnp.float32)[:, None]
            i = jnp.arange(d_model)
            exponent = jnp.where(i % 2 == 0, i, i + 1).astype(jnp.float32) / d_model
            angle = pos / 10000.0 ** exponent
            pe = jnp.where(i % 2 == 0, jnp.cos(angle), jnp.sin(angle))
            return pe.astype(dtype)
        emb = jnp.take(W.T, x, axis=0) + b
        pe = _positional_encoding(x.shape[1], W.shape[0], emb.dtype)
        return emb + pe[None, :, :]

    def _L0_attn_ref(x, ln1_g, ln1_b, Wq, bq, Wk, bk, Wv, bv, Wo, bo, ln2_g, ln2_b, W1, b1, W2, b2):
        import jax, jax.numpy as jnp
        import numpy as np
        B, T, D_MODEL, N_HEADS, D_FF = (2, 512, 128, 8, 512)
        D_HEAD = D_MODEL // N_HEADS
        EPS_LN = 1e-05
        DEN_MIN = 1e-06

        def layer_norm(x, g, b):
            mu = jnp.mean(x, axis=-1, keepdims=True)
            var = jnp.var(x, axis=-1, keepdims=True)
            return (x - mu) * jax.lax.rsqrt(var + EPS_LN) * g + b

        def causal_linear_attention(Q, K, V):
            KV = jnp.cumsum(K[..., :, None] * V[..., None, :], axis=2)
            z = jnp.cumsum(K, axis=2)
            num = jnp.einsum('bhtd,bhtdm->bhtm', Q, KV)
            den = jnp.maximum(jnp.einsum('bhtd,bhtd->bht', Q, z), DEN_MIN)[..., None]
            return num / den
        Bx, Tx, _ = x.shape
        h = layer_norm(x, ln1_g, ln1_b)

        def heads(y):
            return y.reshape(Bx, Tx, N_HEADS, D_HEAD).transpose(0, 2, 1, 3)
        Q = jax.nn.elu(heads(h @ Wq + bq)) + 1.0
        K = jax.nn.elu(heads(h @ Wk + bk)) + 1.0
        V = heads(h @ Wv + bv)
        attn = causal_linear_attention(Q, K, V)
        attn = attn.transpose(0, 2, 1, 3).reshape(Bx, Tx, D_MODEL)
        x = x + (attn @ Wo + bo)
        h2 = layer_norm(x, ln2_g, ln2_b)
        ffn = jax.nn.relu(h2 @ W1 + b1) @ W2 + b2
        return x + ffn

    def _L0_ffn_ref(x, gate_w, expert_bias, shared_gate_up, shared_down, expert_gate_up, expert_down):
        import jax, jax.numpy as jnp
        import numpy as np
        D_MODEL = 128
        D_FF = 128
        N_EXPERTS = 16
        TOP_K = 3
        BATCH, SEQ = (1, 512)

        def _swiglu(combined):
            gate, up = jnp.split(combined, 2, axis=-1)
            return jax.nn.silu(gate) * up
        B, S, D = x.shape
        xf = x.reshape(-1, D)
        shared_out = _swiglu(xf @ shared_gate_up.T) @ shared_down.T
        logits = xf @ gate_w.T
        affinity = jax.nn.sigmoid(logits)
        routing_scores = affinity + expert_bias
        _, sel = jax.lax.top_k(routing_scores, TOP_K)
        sel_aff = jnp.take_along_axis(affinity, sel, axis=1)
        gating = sel_aff / (sel_aff.sum(axis=-1, keepdims=True) + 1e-09)
        combined = jnp.einsum('td,efd->tef', xf, expert_gate_up)
        hidden = _swiglu(combined)
        expert_out = jnp.einsum('tef,edf->ted', hidden, expert_down)
        sel_out = jnp.take_along_axis(expert_out, sel[:, :, None], axis=1)
        routed_out = jnp.einsum('tk,tkd->td', gating, sel_out)
        out = shared_out + routed_out
        return out.reshape(B, S, D)

    def _L1_attn_ref(x, q_w, kv_w):
        import jax, jax.numpy as jnp
        import numpy as np
        NUM_HEADS = 8
        B, N, C = x.shape
        H = NUM_HEADS
        D = C // H
        halfB = B // 2
        q = (x @ q_w.T).reshape(B, N, H, D)
        kv = (x @ kv_w.T).reshape(B, N, 2, H, D)
        k, v = (kv[:, :, 0], kv[:, :, 1])
        k = jnp.concatenate([k[halfB:], k[:halfB]], axis=0)
        v = jnp.concatenate([v[halfB:], v[:halfB]], axis=0)
        scores = jnp.einsum('bnhd,bmhd->bhnm', q, k) / jnp.sqrt(jnp.float32(C))
        prob = jax.nn.softmax(scores, axis=-1)
        out = jnp.einsum('bhnm,bmhd->bndh', prob, v).reshape(B, N, C)
        return out

    def _L1_ffn_ref(hidden_states, gfc1_w, gfc1_b, gfc2_w, gfc2_b, W1, b1, W2, b2, ln_g, ln_b, tv_W1, tv_b1, tv_W2, tv_b2, tv_ln_g, tv_ln_b):
        import jax, jax.numpy as jnp
        import numpy as np
        B, S, D, F, E = (8, 1024, 128, 512, 8)
        INIT_LAMBDA = 0.2
        LN_EPS = 1e-05
        LN_MERGE = 0.03
        x = hidden_states
        gh = jax.nn.relu(jnp.einsum('bsd,hd->bsh', x, gfc1_w) + gfc1_b)
        g = (jnp.einsum('bsh,eh->bse', gh, gfc2_w) + gfc2_b).mean(axis=1)
        W1m = W1 + jnp.einsum('be,efd->bfd', g, tv_W1)
        b1m = b1 + g @ tv_b1
        W2m = W2 + jnp.einsum('be,edf->bdf', g, tv_W2)
        b2m = b2 + g @ tv_b2
        lng = ln_g + LN_MERGE * (tv_ln_g - ln_g).sum(axis=0)
        lnb = ln_b + LN_MERGE * (tv_ln_b - ln_b).sum(axis=0)
        h = jax.nn.relu(jnp.einsum('bsd,bfd->bsf', x, W1m) + b1m[:, None, :])
        out = jnp.einsum('bsf,bdf->bsd', h, W2m) + b2m[:, None, :]
        res = x + out
        mu = res.mean(axis=-1, keepdims=True)
        var = res.var(axis=-1, keepdims=True)
        return (res - mu) * jax.lax.rsqrt(var + LN_EPS) * lng + lnb
    h = _L0_tok_ref(x, L0_tok_W, L0_tok_b)
    h = h + _L0_attn_ref(_layernorm(h, axis=-1), L0_attn_ln1_g, L0_attn_ln1_b, L0_attn_Wq, L0_attn_bq, L0_attn_Wk, L0_attn_bk, L0_attn_Wv, L0_attn_bv, L0_attn_Wo, L0_attn_bo, L0_attn_ln2_g, L0_attn_ln2_b, L0_attn_W1, L0_attn_b1, L0_attn_W2, L0_attn_b2)
    h = h + _L0_ffn_ref(_layernorm(h, axis=-1), L0_ffn_gate_w, L0_ffn_expert_bias, L0_ffn_shared_gate_up, L0_ffn_shared_down, L0_ffn_expert_gate_up, L0_ffn_expert_down)
    h = h + _L1_attn_ref(_layernorm(h, axis=-1), L1_attn_q_w, L1_attn_kv_w)
    h = h + _L1_ffn_ref(_layernorm(h, axis=-1), L1_ffn_gfc1_w, L1_ffn_gfc1_b, L1_ffn_gfc2_w, L1_ffn_gfc2_b, L1_ffn_W1, L1_ffn_b1, L1_ffn_W2, L1_ffn_b2, L1_ffn_ln_g, L1_ffn_ln_b, L1_ffn_tv_W1, L1_ffn_tv_b1, L1_ffn_tv_W2, L1_ffn_tv_b2, L1_ffn_tv_ln_g, L1_ffn_tv_ln_b)
    return h

_drawn_inputs = setup_inputs


def setup_inputs(seed=0):
    import zlib

    import numpy as np

    out = dict(_drawn_inputs(seed))
    spreads = {'L0_attn_ln1_g': (1.0, 0.2),
     'L0_attn_ln1_b': (0.0, 0.1),
     'L0_attn_bq': (0.0, 2.0),
     'L0_attn_bk': (0.0, 2.0),
     'L0_attn_bv': (0.0, 0.1),
     'L0_attn_bo': (0.0, 0.1),
     'L0_attn_ln2_g': (1.0, 0.2),
     'L0_attn_ln2_b': (0.0, 0.1),
     'L0_attn_b1': (0.0, 0.1),
     'L0_attn_b2': (0.0, 0.1),
     'L0_ffn_expert_bias': (0.0, 0.8),
     'L1_ffn_gfc1_b': (0.0, 0.8),
     'L1_ffn_gfc2_b': (0.20000000298023224, 0.6),
     'L1_ffn_b1': (0.0, 0.775),
     'L1_ffn_b2': (0.0, 0.8),
     'L1_ffn_ln_g': (1.0, 0.533),
     'L1_ffn_ln_b': (0.0, 0.274)}
    factors = {'L0_attn_Wq': 5.338,
     'L0_attn_Wk': 2.851,
     'L0_ffn_gate_w': 8.0,
     'L0_ffn_shared_gate_up': 8.0,
     'L0_ffn_shared_down': 8.0,
     'L0_ffn_expert_gate_up': 8.0,
     'L0_ffn_expert_down': 8.0,
     'L1_attn_q_w': 200.0,
     'L1_ffn_gfc1_w': 8.0,
     'L1_ffn_gfc2_w': 8.0,
     'L1_ffn_W1': 2.706,
     'L1_ffn_tv_W1': 4.34,
     'L1_ffn_tv_b1': 37.111,
     'L1_ffn_tv_W2': 3.484,
     'L1_ffn_tv_b2': 46.687,
     'L1_ffn_tv_ln_g': 200.0,
     'L1_ffn_tv_ln_b': 200.0}
    for name, (base, spread) in spreads.items():
        noise = np.random.default_rng([zlib.crc32(name.encode()), seed]).standard_normal(out[name].shape)
        drawn = base * np.exp(spread * noise) if base else spread * noise
        out[name] = jnp.asarray(drawn.astype(out[name].dtype))
    for name, factor in factors.items():
        out[name] = (out[name] * factor).astype(out[name].dtype)
    return out
```

```python
from contextlib import ExitStack

import numpy as np

import concourse.bass as bass
from concourse import mybir

F32 = mybir.dt.float32
I32 = mybir.dt.int32
BF16 = mybir.dt.bfloat16
U32 = mybir.dt.uint32
ALU = mybir.AluOpType
ACT = mybir.ActivationFunctionType
AX_X = mybir.AxisListType.X

P = 128
SEQS, SEQ = 32, 512
CH = SEQ // P
HEADS, DH = 8, 16
STRIPS = 4
GROUPS = HEADS // STRIPS
VW = DH + 1
FF = 512
FB = FF // P
EXPERTS, TOP_K = 16, 3
TASKS = 8
EPS = 1e-5
DEN_MIN = 1e-6
GATE_EPS = 1e-9
MERGE = 0.03


def makers(nc, ctx):
    def sb(name, shape, dt=F32):
        return ctx.enter_context(nc.sbuf_tensor(name, shape, dt))

    def ps(name, shape):
        return ctx.enter_context(nc.psum_tensor(name, shape, F32))

    def sem(name):
        return ctx.enter_context(nc.semaphore(name))

    return sb, ps, sem


def wait_apart(engine, sem, value, passed):
    engine.wait_ge(sem, value)
    engine.sem_inc(passed, 1)


def chunk(c):
    return slice(c * P, (c + 1) * P)


def layer_norm(sb, sem, name, passed):
    return {
        "stats": [sb(f"{name}_stats{p}", [P, CH, 6]) for p in range(2)],
        "mv": [sb(f"{name}_mv{p}", [P, CH, 2]) for p in range(2)],
        "ve": [sb(f"{name}_ve{p}", [P, CH]) for p in range(2)],
        "rstd": [sb(f"{name}_rstd{p}", [P, CH]) for p in range(2)],
        "stats_done": sem(f"{name}_stats_done"),
        "mv_done": sem(f"{name}_mv_done"),
        "ve_done": sem(f"{name}_ve_done"),
        "rstd_done": sem(f"{name}_rstd_done"),
        "passed": passed,
    }


def ln_measure(dve, ln, x, n, p):
    for c in range(CH):
        last = dve.bn_stats(ln["stats"][p][:, c, :], x[:, c, :])
    last.then_inc(ln["stats_done"], 1)
    wait_apart(dve, ln["stats_done"], n + 1, ln["passed"])
    for c in range(CH):
        last = dve.bn_aggr(ln["mv"][p][:, c, :], ln["stats"][p][:, c, :])
    last.then_inc(ln["mv_done"], 1)


def ln_power(pool, ln, minus_half, n, p):
    wait_apart(pool, ln["mv_done"], n + 1, ln["passed"])
    pool.tensor_scalar(ln["ve"][p][:, :], ln["mv"][p][:, :, 1], EPS, None, ALU.add).then_inc(ln["ve_done"], 1)
    pool.wait_ge(ln["ve_done"], n + 1)
    pool.tensor_tensor(ln["rstd"][p][:, :], ln["ve"][p][:, :], minus_half, ALU.pow).then_inc(ln["rstd_done"], 1)


def ln_normalise(dve, ln, out, x, n, p):
    dve.wait_ge(ln["rstd_done"], n + 1)
    for c in range(CH):
        last = dve.tensor_scalar(out[:, c, :], x[:, c, :], ln["mv"][p][:, c, 0:1], ln["rstd"][p][:, c:c + 1],
                                 ALU.subtract, ALU.mult)
    return last


def pairs(engine):
    with engine.Fori(0, SEQS // 2) as i:
        yield [2 * i, 2 * i + 1]


def linear_attention_phase(nc, a, H, consts):
    ident, minus_half, ones_row = consts["ident"], consts["minus_half"], consts["ones_row"]
    with ExitStack() as ctx:
        sb, ps, sem = makers(nc, ctx)
        passed = consts["passed"]
        two = lambda name, shape: [sb(f"a_{name}_{p}", shape) for p in range(2)]
        w4 = sb("a_w4", [P, 4, P])
        w1 = sb("a_w1", [P, FF])
        w2 = sb("a_w2", [P, FB, P])
        cols = sb("a_cols", [P, 6 + FB])
        BQ, BK, G1, B1, G2, B2, BF = range(7)
        rows = sb("a_rows", [1, 3, CH, P])
        tok_ids = sb("a_tok_ids", [P, SEQS * CH], I32)
        posb = sb("a_posb", [P, CH, P])
        tokb = sb("a_tokb", [P, P])
        even = sb("a_even", [P, 2])
        causal = sb("a_causal", [P, P])
        bdiag = sb("a_bdiag", [P, HEADS * VW])

        ids = two("ids", [P, CH])
        ids = [sb(f"a_idx{p}", [P, CH], I32) for p in range(2)]
        E = two("emb", [P, CH, P])
        X0 = two("x0", [P, CH, P])
        X1 = two("x1", [P, CH, P])
        XN = two("xn", [P, CH, P])
        HT = two("ht", [P, SEQ])
        TE = two("te", [P, SEQ])
        TK = two("tk", [P, SEQ])
        QT = two("qt", [P, SEQ])
        KT = two("kt", [P, SEQ])
        Q2 = two("q2", [P, 2, SEQ])
        KK = two("kk", [P, CH, P])
        V = two("v", [P, CH, HEADS, VW])
        S = two("s", [P, CH - 1, HEADS * VW])
        AT = two("at", [P, STRIPS, 4 * P])
        DN = two("dn", [P, 2, HEADS])
        RD = two("rd", [P, 2, HEADS])
        AN = two("an", [P, CH, P])
        ANT = two("ant", [P, SEQ])
        r1 = two("r1", [P, CH])
        t1 = two("t1", [P, CH])
        B = [ps(f"a_ps{p}", [P, 4, 512]) for p in range(2)]

        ln1, ln2 = layer_norm(sb, sem, "a_ln1", passed), layer_norm(sb, sem, "a_ln2", passed)
        loaded = sem("a_loaded")
        consts_set = sem("a_consts_set")
        masks_zero = sem("a_masks_zero")
        bdiag_done = sem("a_bdiag_done")
        posb_done = sem("a_posb_done")
        idx_ready = sem("a_idx_ready")
        emb_landed = [sem(f"a_emb_landed{p}") for p in range(2)]
        h_ready = sem("a_h_ready")
        x1_ready = sem("a_x1_ready")
        r1_steps = sem("a_r1_steps")
        xn_ready = sem("a_xn_ready")
        xnT_ready = sem("a_xnT_ready")
        ht_ready = sem("a_ht_ready")
        qkv_ready = sem("a_qkv_ready")
        exp_ready = sem("a_exp_ready")
        pos_ready = sem("a_pos_ready")
        qk_done = sem("a_qk_done")
        q2_ready = sem("a_q2_ready")
        v_ready = sem("a_v_ready")
        kT_ready = sem("a_kT_ready")
        kk_ready = sem("a_kk_ready")
        state_ready = sem("a_state_ready")
        s_ready = sem("a_s_ready")
        at_ready = [sem(f"a_at_ready{half}") for half in range(2)]
        mask_done = [sem(f"a_mask_done{half}") for half in range(2)]
        o_ready = [sem(f"a_o_ready{half}") for half in range(2)]
        dn_ready = [sem(f"a_dn_ready{half}") for half in range(2)]
        rd_ready = [sem(f"a_rd_ready{half}") for half in range(2)]
        an_ready = [sem(f"a_an_ready{half}") for half in range(2)]
        anT_ready = sem("a_anT_ready")
        ant_ready = sem("a_ant_ready")
        wo_ready = sem("a_wo_ready")
        x2_ready = sem("a_x2_ready")
        xn2_ready = sem("a_xn2_ready")
        xn2T_ready = sem("a_xn2T_ready")
        h2t_ready = sem("a_h2t_ready")
        hid_ready = sem("a_hid_ready")
        relu_act = sem("a_relu_act")
        relu_dve = sem("a_relu_dve")
        y_ready = sem("a_y_ready")
        x3_ready = sem("a_x3_ready")

        block = ctx.enter_context(nc.Block())

        @block.sync
        def _(sp):
            sp.dma_start(tok_ids[:, :], a["ids"]).then_inc(loaded, 16)
            sp.dma_start(tokb[:, :], a["L0_tok_b"].rearrange("(o d) -> o d", o=1).broadcast_to([P, P]))\
              .then_inc(loaded, 16)
            sp.dma_start(posb[:, :, :], a["pos"].rearrange("(c p) d -> p c d", p=P)).then_inc(loaded, 16)
            for j, name in enumerate(("L0_attn_bq", "L0_attn_bk", "L0_attn_ln1_g", "L0_attn_ln1_b",
                                      "L0_attn_ln2_g", "L0_attn_ln2_b")):
                sp.dma_start(cols[:, j:j + 1], a[name].rearrange("(d o) -> d o", o=1)).then_inc(loaded, 16)
            for j, name in enumerate(("L0_attn_Wq", "L0_attn_Wk", "L0_attn_Wv", "L0_attn_Wo")):
                sp.dma_start(w4[:, j, :], a[name]).then_inc(loaded, 16)
            sp.dma_start(w1[:, :], a["L0_attn_W1"]).then_inc(loaded, 16)
            sp.dma_start(w2[:, :, :], a["L0_attn_W2"].rearrange("(b p) d -> p b d", p=P)).then_inc(loaded, 16)
            sp.wait_ge(loaded, 16 * 19)

        @block.gpsimd
        def _(pool):
            pool.memset(causal[:, :], 1.0).then_inc(masks_zero, 1)
            pool.memset(bdiag[:, :], 1.0).then_inc(masks_zero, 1)
            pool.memset(even[:, :], 0.0).then_inc(masks_zero, 1)
            pool.wait_ge(masks_zero, 3)
            pool.affine_select(out=causal[:, :], in_=causal[:, :], compare_op=ALU.is_ge, fill=0.0, base=0,
                               pattern=[[1, P]], channel_multiplier=-1).then_inc(consts_set, 1)
            heads_view = bdiag[:, :].rearrange("p (h v) -> p h v", h=HEADS)
            pool.affine_select(out=heads_view, in_=heads_view, compare_op=ALU.is_ge, fill=0.0, base=0,
                               pattern=[[-DH, HEADS], [0, VW]], channel_multiplier=1).then_inc(bdiag_done, 1)
            pool.wait_ge(bdiag_done, 1)
            pool.affine_select(out=heads_view, in_=heads_view, compare_op=ALU.is_ge, fill=0.0, base=DH - 1,
                               pattern=[[DH, HEADS], [0, VW]], channel_multiplier=-1).then_inc(bdiag_done, 1)
            pool.wait_ge(bdiag_done, 2)
            for odd in range(2):
                for i in range(STRIPS):
                    pool.wait_ge(bdiag_done, 2 + odd * STRIPS + i)
                    h = 2 * i + odd
                    pool.tensor_tensor(even[:, odd:odd + 1], even[:, odd:odd + 1],
                                       bdiag[:, h * VW:h * VW + 1], ALU.add).then_inc(bdiag_done, 1)
            pool.wait_ge(bdiag_done, 2 + HEADS)
            pool.wait_ge(loaded, 16 * 19)
            for ns in pairs(pool):
                for p, n in enumerate(ns):
                    pool.wait_ge(h_ready, n + 1)
                    pool.tensor_copy(ids[p][:, :], tok_ids[:, bass.ds(n * CH, CH)]).then_inc(idx_ready, 1)
                    wait_apart(pool, idx_ready, n + 1, passed)
                    for c in range(CH):
                        pool.indirect_dma_start(
                            out=E[p][:, c, :], out_offset=None, in_=a["table"],
                            in_offset=bass.IndirectOffsetOnAxis(ap=ids[p][:, c:c + 1], axis=0),
                        ).then_inc(emb_landed[p], 16)
                for p, n in enumerate(ns):
                    ln_power(pool, ln1, minus_half, n, p)
                    pool.wait_ge(ln1["rstd_done"], n + 1)
                    pool.tensor_tensor(t1[p][:, :], ln1["rstd"][p][:, :], ln1["rstd"][p][:, :], ALU.mult)\
                        .then_inc(r1_steps, 1)
                    pool.wait_ge(r1_steps, n * 4 + 1)
                    pool.tensor_tensor(t1[p][:, :], t1[p][:, :], ln1["mv"][p][:, :, 1], ALU.mult)\
                        .then_inc(r1_steps, 1)
                    wait_apart(pool, r1_steps, n * 4 + 2, passed)
                    pool.tensor_scalar(t1[p][:, :], t1[p][:, :], EPS, None, ALU.add).then_inc(r1_steps, 1)
                    pool.wait_ge(r1_steps, n * 4 + 3)
                    pool.tensor_tensor(r1[p][:, :], t1[p][:, :], minus_half, ALU.pow).then_inc(r1_steps, 1)
                for p, n in enumerate(ns):
                    ln_power(pool, ln2, minus_half, n, p)

        @block.scalar
        def _(act):
            for j, name in enumerate(("L0_attn_bv", "L0_attn_bo", "L0_attn_b2")):
                act.dma_start(rows[:, j, :, :],
                              a[name].rearrange("(o c d) -> o c d", o=1, c=1).broadcast_to([1, CH, P]))\
                    .then_inc(loaded, 16)
            act.dma_start(cols[:, BF:BF + FB], a["L0_attn_b1"]).then_inc(loaded, 16)
            act.wait_ge(loaded, 16 * 19)
            act.activation(TE[0][:, 0:1], cols[:, 0:1], ACT.Exp, scale=0.0)
            for ns in pairs(act):
                for p, n in enumerate(ns):
                    act.wait_ge(x1_ready, n + 1)
                    act.wait_ge(r1_steps, n * 4 + 4)
                    for c in range(CH):
                        last = act.activation(XN[p][:, c, :], X1[p][:, c, :], ACT.Copy, scale=r1[p][:, c:c + 1])
                    last.then_inc(xn_ready, 1)
                for p, n in enumerate(ns):
                    act.wait_ge(xnT_ready, n + 1)
                    act.activation(HT[p][:, :], B[p][:, 0, :], ACT.Identity, bias=cols[:, B1:B1 + 1],
                                   scale=cols[:, G1:G1 + 1]).then_inc(ht_ready, 1)
                for p, n in enumerate(ns):
                    act.wait_ge(qkv_ready, n * 3 + 1)
                    act.activation(TE[p][:, :], B[p][:, 1, :], ACT.Exp, bias=cols[:, BQ:BQ + 1])\
                        .then_inc(exp_ready, 1)
                    act.wait_ge(qkv_ready, n * 3 + 2)
                    act.activation(TK[p][:, :], B[p][:, 2, :], ACT.Exp, bias=cols[:, BK:BK + 1])\
                        .then_inc(exp_ready, 1)
                    act.wait_ge(qkv_ready, n * 3 + 3)
                    act.activation(V[p][:, :, :, 0:DH],
                                   B[p][:, 3, :].rearrange("p (c h d) -> p c h d", c=CH, h=HEADS), ACT.Copy)\
                        .then_inc(v_ready, 1)
                for p, n in enumerate(ns):
                    act.wait_ge(kT_ready, n + 1)
                    act.activation(KK[p][:, :, :], B[p][:, 0, :].rearrange("p (c d) -> p c d", c=CH), ACT.Copy)\
                        .then_inc(kk_ready, 1)
                for p, n in enumerate(ns):
                    act.wait_ge(anT_ready, n + 1)
                    act.activation(ANT[p][:, :], B[p][:, 1, :], ACT.Copy).then_inc(ant_ready, 1)
                for p, n in enumerate(ns):
                    act.wait_ge(xn2T_ready, n + 1)
                    act.activation(HT[p][:, :], B[p][:, 3, :], ACT.Identity, bias=cols[:, B2:B2 + 1],
                                   scale=cols[:, G2:G2 + 1]).then_inc(h2t_ready, 1)
                for p, n in enumerate(ns):
                    for fb in range(0, FB, 2):
                        act.wait_ge(hid_ready, n * FB + fb + 1)
                        act.activation(AT[p][:, fb, :], B[p][:, fb, :], ACT.Relu, bias=cols[:, BF + fb:BF + fb + 1])\
                            .then_inc(relu_act, 1)

        @block.vector
        def _(dve):
            for p in range(2):
                dve.memset(V[p][:, :, :, DH:VW], 1.0)
            dve.sem_inc(h_ready, 2)
            dve.wait_ge(loaded, 16 * 19)
            dve.tensor_tensor(posb[:, :, :], posb[:, :, :], tokb[:, :].unsqueeze(1).broadcast_to([P, CH, P]), ALU.add)\
               .then_inc(posb_done, 1)
            dve.wait_ge(posb_done, 1)
            dve.wait_ge(consts_set, 1)
            dve.wait_ge(bdiag_done, 2 + HEADS)
            for ns in pairs(dve):
                for p, n in enumerate(ns):
                    dve.wait_ge(emb_landed[p], (ns[0] + 1) * 8 * CH + 8 * CH)
                    dve.tensor_tensor(X0[p][:, :, :], E[p][:, :, :], posb[:, :, :], ALU.add)\
                       .then_inc(h_ready, 1)
                    dve.wait_ge(h_ready, n + 3)
                    ln_measure(dve, ln1, X0[p], n, p)
                for p, n in enumerate(ns):
                    ln_normalise(dve, ln1, X1[p], X0[p], n, p).then_inc(x1_ready, 1)
                for p, n in enumerate(ns):
                    for j, (out, e, b) in enumerate(((QT, TE, BQ), (KT, TK, BK))):
                        dve.wait_ge(exp_ready, n * 2 + j + 1)
                        dve.tensor_scalar(out[p][:, :], B[p][:, 1 + j, :], cols[:, b:b + 1], 0.0, ALU.add, ALU.max)\
                           .then_inc(pos_ready, 1)
                    for j, (out, e) in enumerate(((QT, TE), (KT, TK))):
                        dve.wait_ge(pos_ready, n * 2 + j + 1)
                        dve.scalar_tensor_tensor(out=out[p][:, :], in0=e[p][:, :], scalar=1.0, in1=out[p][:, :],
                                                 op0=ALU.min, op1=ALU.add).then_inc(qk_done, 1)
                    dve.wait_ge(qk_done, n * 2 + 1)
                    for odd in range(2):
                        last = dve.tensor_scalar(Q2[p][:, odd, :], QT[p][:, :], even[:, odd:odd + 1], None, ALU.mult)
                    last.then_inc(q2_ready, 1)
                for p, n in enumerate(ns):
                    dve.wait_ge(state_ready, n + 1)
                    dve.tensor_tensor(
                        S[p][:, :, :], B[p][:, 1, 0:(CH - 1) * HEADS * VW].rearrange("p (c v) -> p c v", c=CH - 1),
                        bdiag[:, :].unsqueeze(1).broadcast_to([P, CH - 1, HEADS * VW]), ALU.mult)\
                       .then_inc(s_ready, 1)
                for half in range(2):
                    for p, n in enumerate(ns):
                        dve.wait_ge(at_ready[half], n + 1)
                        dve.tensor_tensor(
                            AT[p][:, :, :].rearrange("p i (k t) -> p (i k) t", k=4),
                            B[p][:, :, :].rearrange("p i (k t) -> p (i k) t", k=4),
                            causal[:, :].unsqueeze(1).broadcast_to([P, 16, P]), ALU.mult)\
                           .then_inc(mask_done[half], 1)
                    for p, n in enumerate(ns):
                        dve.wait_ge(o_ready[half], n + 1)
                        o = B[p][:, 0, 0:2 * HEADS * VW].rearrange("p (c h v) -> p c h v", c=2, h=HEADS)
                        dve.tensor_scalar(DN[p][:, :, :], o[:, :, :, DH], DEN_MIN, None, ALU.max)\
                           .then_inc(dn_ready[half], 1)
                        dve.wait_ge(dn_ready[half], n + 1)
                        dve.reciprocal(RD[p][:, :, :], DN[p][:, :, :]).then_inc(rd_ready[half], 1)
                        dve.wait_ge(rd_ready[half], n + 1)
                        dve.tensor_tensor(
                            AN[p][:, 2 * half:2 * half + 2, :].rearrange("p c (h d) -> p c h d", h=HEADS),
                            o[:, :, :, 0:DH],
                            RD[p][:, :, :].unsqueeze(3).broadcast_to([P, 2, HEADS, DH]), ALU.mult)\
                           .then_inc(an_ready[half], 1)
                for p, n in enumerate(ns):
                    dve.wait_ge(wo_ready, n + 1)
                    dve.tensor_tensor(X1[p][:, :, :], X1[p][:, :, :],
                                      B[p][:, 2, :].rearrange("p (c d) -> p c d", c=CH), ALU.add)\
                       .then_inc(x2_ready, 1)
                    dve.wait_ge(x2_ready, n + 1)
                    ln_measure(dve, ln2, X1[p], n, p)
                for p, n in enumerate(ns):
                    ln_normalise(dve, ln2, XN[p], X1[p], n, p).then_inc(xn2_ready, 1)
                for p, n in enumerate(ns):
                    for fb in range(1, FB, 2):
                        dve.wait_ge(hid_ready, n * FB + fb + 1)
                        dve.tensor_scalar(AT[p][:, fb, :], B[p][:, fb, :], cols[:, BF + fb:BF + fb + 1], 0.0,
                                          ALU.add, ALU.max).then_inc(relu_dve, 1)
                for p, n in enumerate(ns):
                    dve.wait_ge(y_ready, n + 1)
                    dve.tensor_tensor(X1[p][:, :, :], X1[p][:, :, :],
                                      B[p][:, 0, :].rearrange("p (c d) -> p c d", c=CH), ALU.add)\
                       .then_inc(x3_ready, 1)
                    dve.wait_ge(x3_ready, n + 1)
                    dve.tensor_tensor(H[:, bass.ds(n, 1), :], X1[p][:, :, :].rearrange("p c d -> p (c d)").unsqueeze(1),
                                      X0[p][:, :, :].rearrange("p c d -> p (c d)").unsqueeze(1), ALU.add)

        @block.tensor
        def _(pe):
            pe.wait_ge(loaded, 16 * 19)
            for ns in pairs(pe):
                for p, n in enumerate(ns):
                    pe.wait_ge(xn_ready, n + 1)
                    for c in range(CH):
                        last = pe.transpose(B[p][:, 0, chunk(c)], XN[p][:, c, :], ident)
                    last.then_inc(xnT_ready, 1)
                for p, n in enumerate(ns):
                    pe.wait_ge(ht_ready, n + 1)
                    for j in range(2):
                        pe.matmul(B[p][:, 1 + j, :], w4[:, j, :], HT[p][:, :], start=True, stop=True)\
                          .then_inc(qkv_ready, 1)
                    pe.matmul(B[p][:, 3, :], ones_row, rows[:, 0, :, :].rearrange("o c d -> o (c d)"),
                              start=True, stop=False, skip_group_check=True)
                    for c in range(CH):
                        last = pe.matmul(B[p][:, 3, chunk(c)], HT[p][:, chunk(c)], w4[:, 2, :], start=False,
                                         stop=(c == CH - 1), skip_group_check=True)
                    last.then_inc(qkv_ready, 1)
                for p, n in enumerate(ns):
                    pe.wait_ge(qk_done, n * 2 + 2)
                    for c in range(CH):
                        last = pe.transpose(B[p][:, 0, chunk(c)], KT[p][:, chunk(c)], ident)
                    last.then_inc(kT_ready, 1)
                for p, n in enumerate(ns):
                    pe.wait_ge(kk_ready, n + 1)
                    pe.wait_ge(v_ready, n + 1)
                    for c in range(1, CH):
                        for b in range(c):
                            last = pe.matmul(B[p][:, 1, (c - 1) * HEADS * VW:c * HEADS * VW], KK[p][:, b, :],
                                             V[p][:, b, :, :].rearrange("p h v -> p (h v)"),
                                             start=(c == 1 and b == 0), stop=(b == c - 1), skip_group_check=True)
                    last.then_inc(state_ready, 1)
                for half in range(2):
                    for p, n in enumerate(ns):
                        if half == 0:
                            pe.wait_ge(s_ready, n + 1)
                            pe.wait_ge(q2_ready, n + 1)
                        else:
                            pe.wait_ge(an_ready[0], n + 1)
                        for odd in range(2):
                            for cc in range(2):
                                c = 2 * half + cc
                                for i in range(STRIPS):
                                    rows32 = slice(32 * i, 32 * i + 32)
                                    last = pe.matmul(B[p][:, i, (2 * odd + cc) * P:(2 * odd + cc + 1) * P],
                                                     KT[p][rows32, chunk(c)], Q2[p][rows32, odd, chunk(c)],
                                                     start=True, stop=True)
                        last.then_inc(at_ready[half], 1)
                    for p, n in enumerate(ns):
                        pe.wait_ge(mask_done[half], n + 1)
                        for cc in range(2):
                            c = 2 * half + cc
                            first = cc == 0
                            if c:
                                pe.matmul(B[p][:, 0, cc * HEADS * VW:(cc + 1) * HEADS * VW], QT[p][:, chunk(c)],
                                          S[p][:, c - 1, :], start=first, stop=False, skip_group_check=True)
                                first = False
                            for h in range(HEADS):
                                i, odd = h // 2, h % 2
                                at = (cc * HEADS + h) * VW
                                last = pe.matmul(B[p][:, 0, at:at + VW],
                                                 AT[p][:, i, (2 * odd + cc) * P:(2 * odd + cc + 1) * P],
                                                 V[p][:, c, h, :], start=first, stop=True, skip_group_check=True)
                                first = False
                        last.then_inc(o_ready[half], 1)
                for p, n in enumerate(ns):
                    pe.wait_ge(an_ready[1], n + 1)
                    for c in range(CH):
                        last = pe.transpose(B[p][:, 1, chunk(c)], AN[p][:, c, :], ident)
                    last.then_inc(anT_ready, 1)
                for p, n in enumerate(ns):
                    pe.wait_ge(ant_ready, n + 1)
                    pe.matmul(B[p][:, 2, :], ones_row, rows[:, 1, :, :].rearrange("o c d -> o (c d)"),
                              start=True, stop=False, skip_group_check=True)
                    for c in range(CH):
                        last = pe.matmul(B[p][:, 2, chunk(c)], ANT[p][:, chunk(c)], w4[:, 3, :], start=False,
                                         stop=(c == CH - 1), skip_group_check=True)
                    last.then_inc(wo_ready, 1)
                for p, n in enumerate(ns):
                    pe.wait_ge(xn2_ready, n + 1)
                    for c in range(CH):
                        last = pe.transpose(B[p][:, 3, chunk(c)], XN[p][:, c, :], ident)
                    last.then_inc(xn2T_ready, 1)
                for p, n in enumerate(ns):
                    pe.wait_ge(h2t_ready, n + 1)
                    for fb in range(FB):
                        pe.matmul(B[p][:, fb, :], w1[:, chunk(fb)], HT[p][:, :], start=True, stop=True)\
                          .then_inc(hid_ready, 1)
                for p, n in enumerate(ns):
                    pe.wait_ge(relu_act, n * FB // 2 + FB // 2)
                    pe.wait_ge(relu_dve, n * FB // 2 + FB // 2)
                    pe.matmul(B[p][:, 0, :], ones_row, rows[:, 2, :, :].rearrange("o c d -> o (c d)"),
                              start=True, stop=False, skip_group_check=True)
                    for c in range(CH):
                        for fb in range(FB):
                            last = pe.matmul(B[p][:, 0, chunk(c)], AT[p][:, fb, chunk(c)], w2[:, fb, :],
                                             start=False, stop=(c == CH - 1 and fb == FB - 1),
                                             skip_group_check=True)
                    last.then_inc(y_ready, 1)


def expert_phase(nc, a, H, consts):
    ident, minus_half = consts["ident"], consts["minus_half"]
    LAST = EXPERTS
    UNITS = EXPERTS + 1
    with ExitStack() as ctx:
        sb, ps, sem = makers(nc, ctx)
        passed = consts["passed"]
        two = lambda name, shape, dt=F32: [sb(f"e_{name}_{p}", shape, dt) for p in range(2)]
        wgu = sb("e_wgu", [P, UNITS, 2 * P])
        wdn = sb("e_wdn", [P, UNITS, P])
        wr = sb("e_wr", [P, EXPERTS])
        ebias = sb("e_bias", [P, EXPERTS])
        iota = sb("e_iota", [P, EXPERTS])
        XN = two("xn", [P, CH, P])
        XT = two("xt", [P, SEQ])
        EX = two("ex", [P, CH, EXPERTS])
        AF = two("af", [P, CH, EXPERTS])
        SC = two("sc", [P, CH, EXPERTS])
        T8 = two("t8", [P, CH, 8])
        I8 = two("i8", [P, CH, 8], U32)
        IF = two("if", [P, CH, 8])
        OH = two("oh", [P, CH, EXPERTS, TOP_K])
        GS = two("gs", [P, CH])
        GATE = two("gate", [P, CH, EXPERTS])
        ACC = two("acc", [P, CH, P])
        SIL = two("sil", [P, SEQ])
        HID = [sb(f"e_hid_{j}", [P, SEQ]) for j in range(3)]
        GP = [ps(f"e_gp{p}", [P, 512]) for p in range(2)]
        UP = [ps(f"e_up{p}", [P, 512]) for p in range(2)]
        DP = [ps(f"e_dp{p}", [P, 512]) for p in range(2)]
        TP = [ps(f"e_tp{p}", [P, 512]) for p in range(2)]

        ln = layer_norm(sb, sem, "e_ln", passed)
        loaded = sem("e_loaded")
        iota_done = sem("e_iota_done")
        xn_ready = sem("e_xn_ready")
        xnT_ready = sem("e_xnT_ready")
        xt_ready = sem("e_xt_ready")
        logit_ready = sem("e_logit_ready")
        ex_ready = sem("e_ex_ready")
        steps = sem("e_route_steps")
        gate_steps = sem("e_gate_steps")
        gu_ready = sem("e_gu_ready")
        sil_ready = sem("e_sil_ready")
        hid_ready = sem("e_hid_ready")
        dn_ready = sem("e_dn_ready")
        acc_ready = sem("e_acc_ready")
        h_ready = sem("e_h_ready")
        LOADS = 16 * 6

        block = ctx.enter_context(nc.Block())

        @block.sync
        def _(sp):
            sp.dma_start(wr[:, :], a["L0_ffn_gate_w"]).then_inc(loaded, 16)
            sp.dma_start(ebias[:, :], a["L0_ffn_expert_bias"].rearrange("(o d) -> o d", o=1)
                         .broadcast_to([P, EXPERTS])).then_inc(loaded, 16)
            sp.dma_start(wgu[:, 0, :], a["L0_ffn_shared_gate_up"]).then_inc(loaded, 16)
            sp.dma_start(wdn[:, 0, :], a["L0_ffn_shared_down"]).then_inc(loaded, 16)
            sp.dma_start(wgu[:, 1:UNITS, :], a["L0_ffn_expert_gate_up"].rearrange("e d f -> d e f"))\
              .then_inc(loaded, 16)
            sp.dma_start(wdn[:, 1:UNITS, :], a["L0_ffn_expert_down"].rearrange("e f d -> f e d"))\
              .then_inc(loaded, 16)
            sp.wait_ge(loaded, LOADS)

        @block.gpsimd
        def _(pool):
            pool.sem_inc(h_ready, 1)
            pool.iota(iota[:, :], pattern=[[1, EXPERTS]], base=0, channel_multiplier=0,
                      allow_small_or_imprecise_dtypes=True).then_inc(iota_done, 1)
            for ns in pairs(pool):
                for p, n in enumerate(ns):
                    ln_power(pool, ln, minus_half, n, p)
                for p, n in enumerate(ns):
                    pool.wait_ge(acc_ready, n * UNITS + UNITS + 1)
                    pool.tensor_copy(H[:, bass.ds(n, 1), :],
                                     ACC[p][:, :, :].rearrange("p c d -> p (c d)").unsqueeze(1)).then_inc(h_ready, 1)

        @block.scalar
        def _(act):
            for ns in pairs(act):
                for p, n in enumerate(ns):
                    act.wait_ge(xnT_ready, n + 1)
                    act.activation(XT[p][:, :], TP[p][:, :], ACT.Copy).then_inc(xt_ready, 1)
                for p, n in enumerate(ns):
                    act.wait_ge(logit_ready, n + 1)
                    act.activation(EX[p][:, :, :], TP[p][:, 0:CH * EXPERTS].rearrange("p (c e) -> p c e", c=CH),
                                   ACT.Exp, scale=-1.0).then_inc(ex_ready, 1)
                for p, n in enumerate(ns):
                    for e in range(UNITS):
                        act.wait_ge(gu_ready, n * UNITS + e + 1)
                        act.wait_ge(hid_ready, n * UNITS + max(e - 1, 0) + 1)
                        act.activation(SIL[e % 2][:, :], GP[e % 2][:, :], ACT.Silu).then_inc(sil_ready, 1)

        @block.vector
        def _(dve):
            dve.sem_inc(hid_ready, 1)
            dve.sem_inc(acc_ready, 1)
            dve.wait_ge(loaded, LOADS)
            dve.wait_ge(iota_done, 1)
            for ns in pairs(dve):
                for p, n in enumerate(ns):
                    x = H[:, bass.ds(n, 1), :].rearrange("p o (c d) -> p (o c) d", c=CH)
                    wait_apart(dve, h_ready, ns[0] + 1, passed)
                    dve.tensor_copy(ACC[p][:, :, :], x).then_inc(steps, 1)
                    dve.wait_ge(steps, ns[0] * 10 + p + 1)
                    ln_measure(dve, ln, ACC[p], n, p)
                for p, n in enumerate(ns):
                    ln_normalise(dve, ln, XN[p], ACC[p], n, p).then_inc(xn_ready, 1)
                for p, n in enumerate(ns):
                    done = [2 + 9 * p]

                    def step(ins):
                        ins.then_inc(steps, 1)
                        done[0] += 1
                        wait_apart(dve, steps, ns[0] * 10 + done[0], passed)

                    dve.wait_ge(ex_ready, n + 1)
                    step(dve.tensor_scalar(EX[p][:, :, :], EX[p][:, :, :], 1.0, None, ALU.add))
                    step(dve.reciprocal(AF[p][:, :, :], EX[p][:, :, :]))
                    step(dve.tensor_tensor(SC[p][:, :, :], AF[p][:, :, :],
                                           ebias[:, :].unsqueeze(1).broadcast_to([P, CH, EXPERTS]), ALU.add))
                    for c in range(CH):
                        last = dve.max(T8[p][:, c, :], SC[p][:, c, :])
                    last.then_inc(steps, 1)
                    done[0] += 1
                    wait_apart(dve, steps, ns[0] * 10 + done[0], passed)
                    for c in range(CH):
                        last = dve.max_index(I8[p][:, c, :], T8[p][:, c, :], SC[p][:, c, :])
                    step(last)
                    step(dve.tensor_copy(IF[p][:, :, :], I8[p][:, :, :]))
                    step(dve.tensor_tensor(
                        OH[p][:, :, :, :], IF[p][:, :, 0:TOP_K].unsqueeze(2).broadcast_to([P, CH, EXPERTS, TOP_K]),
                        iota[:, :].unsqueeze(1).unsqueeze(3).broadcast_to([P, CH, EXPERTS, TOP_K]), ALU.is_equal))
                    step(dve.tensor_reduce(SC[p][:, :, :], OH[p][:, :, :, :], AX_X, ALU.add))
                    step(dve.tensor_tensor(AF[p][:, :, :], AF[p][:, :, :], SC[p][:, :, :], ALU.mult))
                for p, n in enumerate(ns):
                    dve.tensor_reduce(GS[p][:, :], AF[p][:, :, :], AX_X, ALU.add).then_inc(gate_steps, 1)
                    dve.wait_ge(gate_steps, n * 4 + 1)
                    dve.tensor_scalar(GS[p][:, :], GS[p][:, :], GATE_EPS, None, ALU.add).then_inc(gate_steps, 1)
                    dve.wait_ge(gate_steps, n * 4 + 2)
                    dve.reciprocal(GS[p][:, :], GS[p][:, :]).then_inc(gate_steps, 1)
                    dve.wait_ge(gate_steps, n * 4 + 3)
                    dve.tensor_tensor(GATE[p][:, :, :], AF[p][:, :, :],
                                      GS[p][:, :].unsqueeze(2).broadcast_to([P, CH, EXPERTS]), ALU.mult)\
                       .then_inc(gate_steps, 1)
                for p, n in enumerate(ns):
                    def add(e):
                        dve.wait_ge(dn_ready, n * UNITS + e + 1 + 1)
                        if e == 0:
                            dve.tensor_tensor(ACC[p][:, :, :], ACC[p][:, :, :],
                                              DP[0][:, :].rearrange("p (c d) -> p c d", c=CH), ALU.add)\
                               .then_inc(acc_ready, 1)
                            return
                        dve.wait_ge(acc_ready, n * UNITS + e + 1)
                        if e == 1:
                            dve.wait_ge(gate_steps, n * 4 + 4)
                        for c in range(CH):
                            last = dve.scalar_tensor_tensor(
                                out=ACC[p][:, c, :], in0=DP[e % 2][:, chunk(c)], scalar=GATE[p][:, c, e - 1:e],
                                in1=ACC[p][:, c, :], op0=ALU.mult, op1=ALU.add)
                        last.then_inc(acc_ready, 1)

                    for e in range(UNITS):
                        dve.wait_ge(sil_ready, n * UNITS + e + 1)
                        dve.wait_ge(dn_ready, n * UNITS + max(e - 2, 0) + 1)
                        dve.tensor_tensor(HID[e % 3][:, :], SIL[e % 2][:, :], UP[e % 2][:, :], ALU.mult)\
                           .then_inc(hid_ready, 1)
                        if e >= 2:
                            add(e - 2)
                    add(LAST - 1)
                    add(LAST)

        @block.tensor
        def _(pe):
            pe.sem_inc(dn_ready, 1)
            pe.wait_ge(loaded, LOADS)
            for ns in pairs(pe):
                for p, n in enumerate(ns):
                    pe.wait_ge(xn_ready, n + 1)
                    for c in range(CH):
                        last = pe.transpose(TP[p][:, chunk(c)], XN[p][:, c, :], ident)
                    last.then_inc(xnT_ready, 1)
                for p, n in enumerate(ns):
                    pe.wait_ge(xt_ready, n + 1)
                    for c in range(CH):
                        last = pe.matmul(TP[p][:, c * EXPERTS:(c + 1) * EXPERTS], XT[p][:, chunk(c)], wr[:, :],
                                         start=(c == 0), stop=(c == CH - 1), skip_group_check=True)
                    last.then_inc(logit_ready, 1)
                for p, n in enumerate(ns):
                    def down(e):
                        pe.wait_ge(hid_ready, n * UNITS + e + 1 + 1)
                        pe.wait_ge(acc_ready, n * UNITS + max(e - 1, 0) + 1)
                        for c in range(CH):
                            last = pe.matmul(DP[e % 2][:, chunk(c)], HID[e % 3][:, chunk(c)], wdn[:, e, :],
                                             start=(c == 0), stop=(c == CH - 1), skip_group_check=True)
                        last.then_inc(dn_ready, 1)

                    for e in range(UNITS):
                        pe.wait_ge(hid_ready, n * UNITS + max(e - 1, 0) + 1)
                        pe.matmul(GP[e % 2][:, :], wgu[:, e, 0:P], XT[p][:, :], start=True, stop=True)
                        pe.matmul(UP[e % 2][:, :], wgu[:, e, P:2 * P], XT[p][:, :], start=True, stop=True)\
                          .then_inc(gu_ready, 1)
                        if e >= 2:
                            down(e - 2)
                    down(LAST - 1)
                    down(LAST)


def cross_attention_phase(nc, a, H, consts):
    ident, minus_half = consts["ident"], consts["minus_half"]
    SCALE = float(P) ** -0.5
    TILES = CH * GROUPS * STRIPS
    ROUNDS = TILES // 2
    PARTS = 3
    Q_PARTS, K_PARTS = (0, 0, 1, 0, 2, 1), (0, 1, 0, 2, 0, 1)
    ROWS = DH * len(Q_PARTS)
    LEAD = 8
    tiles = [(c, g, i) for c in range(CH) for g in range(GROUPS) for i in range(STRIPS)]
    with ExitStack() as ctx:
        sb, ps, sem = makers(nc, ctx)
        passed = consts["passed"]
        two = lambda name, shape, dt=F32: [sb(f"c_{name}_{p}", shape, dt) for p in range(2)]
        wq = sb("c_wq", [P, P])
        wk = sb("c_wk", [P, P])
        wv = sb("c_wv", [P, P])
        X = two("x", [P, CH, P])
        XN = two("xn", [P, CH, P])
        XT = two("xt", [P, SEQ])
        SPLIT = two("split", [P, 2, PARTS, SEQ], BF16)
        R1 = two("r1", [P, 2, SEQ])
        QS = two("qs", [P, HEADS, SEQ], BF16)
        KS = two("ks", [P, HEADS, SEQ], BF16)
        MF = two("mf", [HEADS, SEQ])
        MR = two("mr", [HEADS, SEQ])
        MS = two("ms", [HEADS, PARTS, SEQ], BF16)
        V = two("v", [P, CH, HEADS, 32])
        NM = two("nm", [P, CH, HEADS])
        PT = two("pt", [P, 2, SEQ])
        OS = sb("c_os", [P, GROUPS, SEQ])
        RD = sb("c_rd", [P, GROUPS, CH, STRIPS])
        AO = two("ao", [P, CH, P])
        S1 = [ps(f"c_s1_{p}", [P, 512]) for p in range(2)]
        S2 = [ps(f"c_s2_{p}", [P, 2, 512]) for p in range(2)]
        O = ps("c_o", [P, GROUPS, 512])

        ln = layer_norm(sb, sem, "c_ln", passed)
        split_dram = [nc.dram_tensor(f"c_split_dram{p}", (P, 2, PARTS, SEQ), BF16).ap() for p in range(2)]
        max_dram = [nc.dram_tensor(f"c_max_dram{p}", (HEADS, PARTS, SEQ), BF16).ap() for p in range(2)]
        zeroed = sem("c_zeroed")
        loaded = sem("c_loaded")
        ones_set = sem("c_ones_set")
        x_ready = sem("c_x_ready")
        xn_ready = sem("c_xn_ready")
        xnT_ready = sem("c_xnT_ready")
        xt_ready = sem("c_xt_ready")
        qk_ps = sem("c_qk_ps")
        v_ps = sem("c_v_ps")
        part1_ready = sem("c_part1_ready")
        rest_ready = sem("c_rest_ready")
        part2_ready = sem("c_part2_ready")
        part3_ready = sem("c_part3_ready")
        v_ready = sem("c_v_ready")
        to_dram = [sem(f"c_to_dram{p}") for p in range(2)]
        from_dram = [sem(f"c_from_dram{p}") for p in range(2)]
        STACKED = 16 * 2 * len(Q_PARTS)
        BACK = STACKED + 16
        mf_ready = sem("c_mf_ready")
        m_steps = sem("c_m_steps")
        s1_ready = sem("c_s1_ready")
        s1_read = sem("c_s1_read")
        nmT_ready = sem("c_nmT_ready")
        s2_ready = sem("c_s2_ready")
        pt_ready = sem("c_pt_ready")
        pv_done = sem("c_pv_done")
        os_ready = sem("c_os_ready")
        oT_ready = sem("c_oT_ready")
        rd_ready = sem("c_rd_ready")
        ao_ready = sem("c_ao_ready")
        LOADS = 16 * 3

        def twins(engine):
            with engine.Fori(0, SEQS // 2) as i:
                yield [(2 * i, i), (2 * i + 1, i + SEQS // 2)]

        block = ctx.enter_context(nc.Block())

        @block.sync
        def _(sp):
            sp.dma_start(wq[:, :], a["L1_attn_q_w"]).then_inc(loaded, 16)
            sp.dma_start(wk[:, :], a["L1_attn_kv_w"][:, 0:P]).then_inc(loaded, 16)
            sp.dma_start(wv[:, :], a["L1_attn_kv_w"][:, P:2 * P]).then_inc(loaded, 16)
            sp.wait_ge(loaded, LOADS)
            for ns in twins(sp):
                for p, (n, place) in enumerate(ns):
                    sp.wait_ge(part3_ready, n + 1)
                    sp.dma_start(split_dram[p], SPLIT[p][:, :, :, :]).then_inc(to_dram[p], 16)
                for p, (n, place) in enumerate(ns):
                    sp.wait_ge(to_dram[p], 16 * ns[0][0] + 16)
                    for stack, qk, parts in ((QS, 0, Q_PARTS), (KS, 1, K_PARTS)):
                        for b, part in enumerate(parts):
                            sp.dma_start(stack[p][DH * b:DH * (b + 1), :, :],
                                         split_dram[p][:, qk, part, :].rearrange("(h d) n -> d h n", h=HEADS))\
                              .then_inc(from_dram[p], 16)
                for p, (n, place) in enumerate(ns):
                    sp.wait_ge(m_steps, n * 4 + 4)
                    sp.dma_start(max_dram[p], MS[p][:, :, :]).then_inc(to_dram[p], 16)
                    sp.wait_ge(to_dram[p], 16 * ns[0][0] + 32)
                    sp.dma_start(QS[p][ROWS:ROWS + PARTS, :, :], max_dram[p].rearrange("h j n -> j h n"))\
                      .then_inc(from_dram[p], 16)

        @block.gpsimd
        def _(pool):
            for p in range(2):
                pool.memset(V[p][:, :, :, :], 0.0).then_inc(zeroed, 1)
            for p in range(2):
                pool.wait_ge(zeroed, 1 + p)
                pool.memset(V[p][:, :, :, DH:VW], 1.0).then_inc(ones_set, 1)
            for ns in twins(pool):
                for p, (n, place) in enumerate(ns):
                    ln_power(pool, ln, minus_half, n, p)
                for p, (n, place) in enumerate(ns):
                    pool.wait_ge(part2_ready, n + 1)
                    pool.tensor_tensor(SPLIT[p][:, :, 2, :], R1[p][:, :, :], SPLIT[p][:, :, 1, :], ALU.subtract)\
                        .then_inc(part3_ready, 1)

        @block.scalar
        def _(act):
            act.wait_ge(ones_set, 4)
            act.activation(RD[:, 0, 0, 0:1], ident[:, 0:1], ACT.Exp)

            def split_maxima(p, n):
                act.wait_ge(nmT_ready, n + 1)
                act.activation(MF[p][:, :], S1[0][0:HEADS, :], ACT.Copy).then_inc(mf_ready, 1)
                act.wait_ge(mf_ready, n + 1)
                act.activation(MS[p][:, 0, :], MF[p][:, :], ACT.Copy).then_inc(m_steps, 1)
                act.wait_ge(m_steps, n * 4 + 2)
                act.activation(MS[p][:, 1, :], MR[p][:, :], ACT.Copy).then_inc(m_steps, 1)

            def softmax(p, n):
                for r in range(ROUNDS):
                    act.wait_ge(s2_ready, n * ROUNDS + r + 1)
                    if r >= 2:
                        act.wait_ge(pv_done, n * ROUNDS + r - 1)
                    act.activation(PT[r % 2][:, :, :], S2[r % 2][:, :, :], ACT.Exp, scale=SCALE)\
                        .then_inc(pt_ready, 1)
                act.wait_ge(pv_done, n * ROUNDS + ROUNDS)
                act.activation(OS[:, :, :], O[:, :, :], ACT.Copy).then_inc(os_ready, 1)

            for ns in twins(act):
                for p, (n, place) in enumerate(ns):
                    act.wait_ge(xnT_ready, n + 1)
                    act.activation(XT[p][:, :], S1[p][:, :], ACT.Copy).then_inc(xt_ready, 1)
                for p, (n, place) in enumerate(ns):
                    act.wait_ge(qk_ps, n + 1)
                    act.activation(SPLIT[p][:, :, 0, :], S2[p][:, :, :], ACT.Copy).then_inc(part1_ready, 1)
                    act.wait_ge(rest_ready, n + 1)
                    act.activation(SPLIT[p][:, :, 1, :], R1[p][:, :, :], ACT.Copy).then_inc(part2_ready, 1)
                for p, (n, place) in enumerate(ns):
                    act.wait_ge(v_ps, n + 1)
                    act.activation(V[p][:, :, :, 0:DH], S1[p][:, :].rearrange("p (c h d) -> p c h d", c=CH, h=HEADS),
                                   ACT.Copy).then_inc(v_ready, 1)
                (n0, _), (n1, _) = ns
                split_maxima(0, n0)
                softmax(0, n0)
                split_maxima(1, n1)
                softmax(1, n1)

        @block.vector
        def _(dve):
            for p in range(2):
                dve.memset(KS[p][ROWS:ROWS + PARTS, :, :], 1.0).then_inc(ones_set, 1)

            def maxima(p, n):
                for r, (c, g, i) in enumerate(tiles):
                    dve.wait_ge(s1_ready, n * TILES + r + 1)
                    dve.tensor_reduce(NM[p][:, c, g * STRIPS + i:g * STRIPS + i + 1], S1[r % 2][:, :], AX_X, ALU.max, negate=True)\
                       .then_inc(s1_read, 1)

            def split_maxima(p, n):
                dve.wait_ge(m_steps, n * 4 + 1)
                dve.tensor_tensor(MR[p][:, :], MF[p][:, :], MS[p][:, 0, :], ALU.subtract).then_inc(m_steps, 1)
                dve.wait_ge(m_steps, n * 4 + 3)
                dve.tensor_tensor(MS[p][:, 2, :], MR[p][:, :], MS[p][:, 1, :], ALU.subtract).then_inc(m_steps, 1)

            def finish(p, n, place):
                dve.wait_ge(oT_ready, n + 1)
                for g in range(GROUPS):
                    sums = S1[g][:, :].rearrange("p (c i v) -> p c i v", c=CH, i=STRIPS)
                    last = dve.reciprocal(RD[:, g, :, :], sums[:, :, :, DH])
                last.then_inc(rd_ready, 1)
                dve.wait_ge(rd_ready, n + 1)
                for g in range(GROUPS):
                    o = S1[g][:, :].rearrange("p (c i v) -> p c i v", c=CH, i=STRIPS)
                    out = AO[p][:, :, :].rearrange("p c (d h) -> p c h d", h=HEADS)[:, :, g * STRIPS:(g + 1) * STRIPS, :]
                    last = dve.tensor_tensor(out, o[:, :, :, 0:DH],
                                             RD[:, g, :, :].unsqueeze(3).broadcast_to([P, CH, STRIPS, DH]), ALU.mult)
                last.then_inc(ao_ready, 1)
                dve.wait_ge(ao_ready, n + 1)
                dve.tensor_tensor(H[:, bass.ds(place, 1), :], X[p][:, :, :].rearrange("p c d -> p (c d)").unsqueeze(1),
                                  AO[p][:, :, :].rearrange("p c d -> p (c d)").unsqueeze(1), ALU.add)

            for ns in twins(dve):
                for p, (n, place) in enumerate(ns):
                    x = H[:, bass.ds(place, 1), :].rearrange("p o (c d) -> p (o c) d", c=CH)
                    dve.tensor_copy(X[p][:, :, :], x).then_inc(x_ready, 1)
                    dve.wait_ge(x_ready, n + 1)
                    ln_measure(dve, ln, X[p], n, p)
                for p, (n, place) in enumerate(ns):
                    ln_normalise(dve, ln, XN[p], X[p], n, p).then_inc(xn_ready, 1)
                for p, (n, place) in enumerate(ns):
                    dve.wait_ge(part1_ready, n + 1)
                    dve.tensor_tensor(R1[p][:, :, :], S2[p][:, :, :], SPLIT[p][:, :, 0, :], ALU.subtract)\
                       .then_inc(rest_ready, 1)
                (n0, place0), (n1, place1) = ns
                maxima(0, n0)
                split_maxima(0, n0)
                maxima(1, n1)
                split_maxima(1, n1)
                finish(0, n0, place0)
                finish(1, n1, place1)

        @block.tensor
        def _(pe):
            pe.wait_ge(loaded, LOADS)

            def score_for_max(p, n, r):
                c, g, i = tiles[r]
                h = g * STRIPS + i
                if r >= 2:
                    pe.wait_ge(s1_read, n * TILES + r - 1)
                pe.matmul(S1[r % 2][:, :], QS[p][0:ROWS, h, chunk(c)], KS[1 - p][0:ROWS, h, :], start=True, stop=True)\
                  .then_inc(s1_ready, 1)

            def turn_maxima(p, n):
                pe.wait_ge(s1_read, (n + 1) * TILES)
                for c in range(CH):
                    last = pe.transpose(S1[0][0:HEADS, chunk(c)], NM[p][:, c, :], ident)
                last.then_inc(nmT_ready, 1)
                pe.wait_ge(mf_ready, n + 1)

            def scores(p, n, r):
                for j in range(2):
                    c, g, i = tiles[2 * r + j]
                    h = g * STRIPS + i
                    last = pe.matmul(S2[r % 2][:, j, :], KS[1 - p][0:ROWS + PARTS, h, chunk(c)], QS[p][0:ROWS + PARTS, h, :],
                                     start=True, stop=True)
                last.then_inc(s2_ready, 1)

            def values(p, n, r):
                pe.wait_ge(pt_ready, n * ROUNDS + r + 1)
                for j in range(2):
                    c, g, i = tiles[2 * r + j]
                    strip = slice(32 * i, 32 * i + 32)
                    last = pe.matmul(O[strip, g, :], V[1 - p][:, c, g * STRIPS + i, :], PT[r % 2][:, j, :],
                                     start=(c == 0), stop=(c == CH - 1), skip_group_check=True)
                last.then_inc(pv_done, 1)

            def turn_output(p, n):
                pe.wait_ge(os_ready, n + 1)
                for g in range(GROUPS):
                    for c in range(CH):
                        last = pe.transpose(S1[g][:, chunk(c)], OS[:, g, chunk(c)], ident)
                last.then_inc(oT_ready, 1)

            for ns in twins(pe):
                for p, (n, place) in enumerate(ns):
                    pe.wait_ge(xn_ready, n + 1)
                    for c in range(CH):
                        last = pe.transpose(S1[p][:, chunk(c)], XN[p][:, c, :], ident)
                    last.then_inc(xnT_ready, 1)
                for p, (n, place) in enumerate(ns):
                    pe.wait_ge(xt_ready, n + 1)
                    pe.matmul(S2[p][:, 0, :], wq[:, :], XT[p][:, :], start=True, stop=True)
                    pe.matmul(S2[p][:, 1, :], wk[:, :], XT[p][:, :], start=True, stop=True).then_inc(qk_ps, 1)
                    for c in range(CH):
                        last = pe.matmul(S1[p][:, chunk(c)], XT[p][:, chunk(c)], wv[:, :], start=(c == 0),
                                         stop=(c == CH - 1), skip_group_check=True)
                    last.then_inc(v_ps, 1)
                (n0, _), (n1, _) = ns
                pe.wait_ge(v_ready, n1 + 1)
                pe.wait_ge(rest_ready, n1 + 1)
                for p in range(2):
                    pe.wait_ge(from_dram[p], n0 * (BACK // 2) + STACKED)
                for r in range(TILES):
                    score_for_max(0, n0, r)
                turn_maxima(0, n0)
                for r in range(LEAD):
                    score_for_max(1, n1, r)
                pe.wait_ge(from_dram[0], n0 * (BACK // 2) + BACK)
                for r in range(ROUNDS):
                    scores(0, n0, r)
                    for t in range(LEAD + 2 * r, min(LEAD + 2 * r + 2, TILES)):
                        score_for_max(1, n1, t)
                    if r:
                        values(0, n0, r - 1)
                values(0, n0, ROUNDS - 1)
                turn_maxima(1, n1)
                turn_output(0, n0)
                pe.wait_ge(from_dram[1], n0 * (BACK // 2) + BACK)
                for r in range(ROUNDS):
                    scores(1, n1, r)
                    if r:
                        values(1, n1, r - 1)
                values(1, n1, ROUNDS - 1)
                pe.wait_ge(ao_ready, n0 + 1)
                turn_output(1, n1)


def merged_ffn_phase(nc, a, H, out, consts):
    ident, minus_half, ones_row = consts["ident"], consts["minus_half"], consts["ones_row"]
    with ExitStack() as ctx:
        sb, ps, sem = makers(nc, ctx)
        passed = consts["passed"]
        two = lambda name, shape, dt=F32: [sb(f"f_{name}_{p}", shape, dt) for p in range(2)]
        wg1 = sb("f_wg1", [P, P])
        wg2 = sb("f_wg2", [P, TASKS])
        gb1 = sb("f_gb1", [P, 1])
        gb2 = sb("f_gb2", [1, TASKS])
        w1 = sb("f_w1", [P, FF])
        w2 = sb("f_w2", [P, FB * P])
        tw1 = sb("f_tw1", [P, TASKS, FF])
        tw2 = sb("f_tw2", [P, TASKS, FB, P])
        b1 = sb("f_b1", [P, FB])
        tb1 = sb("f_tb1", [P, FB, TASKS])
        b2 = sb("f_b2", [1, CH, P])
        tb2 = sb("f_tb2", [TASKS, CH, P])
        tln = sb("f_tln", [TASKS, 2, P])
        ln8 = sb("f_ln8", [TASKS, 2, P])
        lnp = sb("f_lnp", [P, 2, P])
        merge = sb("f_merge", [TASKS, P])
        ones = sb("f_ones", [P, P])
        X = two("x", [P, CH, P])
        XN = two("xn", [P, CH, P])
        XT = two("xt", [P, SEQ])
        GH = two("gh", [P, SEQ])
        GS = two("gs", [P, 1])
        GM = two("gm", [P, 1])
        GR = two("gr", [P, P])
        GB = two("gb", [P, TASKS])
        GC = two("gc", [TASKS, P])
        DG = two("dg", [P, TASKS, P])
        WM1 = two("wm1", [P, FF])
        WM2 = two("wm2", [P, FB * P])
        BT = two("bt", [P, FB, TASKS])
        BS = two("bs", [P, FB])
        B1 = two("b1m", [P, FB])
        F = two("hid", [P, FB, SEQ])
        B = [ps(f"f_ps{p}", [P, 4, 512]) for p in range(2)]

        ln, ln_out = layer_norm(sb, sem, "f_ln", passed), layer_norm(sb, sem, "f_lno", passed)
        loaded = sem("f_loaded")
        set_ = sem("f_set")
        tln_ready = sem("f_tln_ready")
        lnp_ps = sem("f_lnp_ps")
        lnp_ready = sem("f_lnp_ready")
        stored = [sem(f"f_stored{p}") for p in range(2)]
        x_ready = sem("f_x_ready")
        xn_ready = sem("f_xn_ready")
        xnT_ready = sem("f_xnT_ready")
        xt_ready = sem("f_xt_ready")
        gh_ps = sem("f_gh_ps")
        gs_ready = sem("f_gs_ready")
        gm_ready = sem("f_gm_ready")
        gr_ready = sem("f_gr_ready")
        g_ps = sem("f_g_ps")
        gb_ready = sem("f_gb_ready")
        gc_ready = sem("f_gc_ready")
        dg_ready = sem("f_dg_ready")
        w1_ps = sem("f_w1_ps")
        wm1_ready = sem("f_wm1_ready")
        wm2_steps = sem("f_wm2_steps")
        b1_steps = sem("f_b1_steps")
        hid_ready = sem("f_hid_ready")
        relu_act = sem("f_relu_act")
        relu_dve = sem("f_relu_dve")
        y_ready = sem("f_y_ready")
        r_ready = sem("f_r_ready")
        nr_ready = sem("f_nr_ready")
        gain_done = sem("f_gain_done")
        xb_ready = sem("f_xb_ready")
        out_ready = sem("f_out_ready")
        LOADS = 16 * 16

        block = ctx.enter_context(nc.Block())

        @block.sync
        def _(sp):
            row = lambda name: a[name].rearrange("(o d) -> o d", o=1)
            for tile, src in (
                (wg1[:, :], a["L1_ffn_gfc1_w"]),
                (wg2[:, :], a["L1_ffn_gfc2_w"]),
                (gb1[:, :], a["L1_ffn_gfc1_b"].rearrange("(d o) -> d o", o=1)),
                (gb2[:, :], row("L1_ffn_gfc2_b")),
                (tln[:, 0, :], a["L1_ffn_tv_ln_g"]),
                (tln[:, 1, :], a["L1_ffn_tv_ln_b"]),
                (ln8[:, 0, :], row("L1_ffn_ln_g").broadcast_to([TASKS, P])),
                (ln8[:, 1, :], row("L1_ffn_ln_b").broadcast_to([TASKS, P])),
                (lnp[:, 0, :], row("L1_ffn_ln_g").broadcast_to([P, P])),
                (lnp[:, 1, :], row("L1_ffn_ln_b").broadcast_to([P, P])),
                (tw1[:, :, :], a["L1_ffn_tv_W1"].rearrange("e d f -> d e f")),
                (w1[:, :], a["L1_ffn_W1"]),
                (b1[:, :], a["L1_ffn_b1"]),
                (tb1[:, :, :], a["L1_ffn_tv_b1"]),
                (b2[:, :, :], a["L1_ffn_b2"].rearrange("(o c d) -> o c d", o=1, c=1).broadcast_to([1, CH, P])),
                (tb2[:, :, :], a["L1_ffn_tv_b2"].unsqueeze(1).broadcast_to([TASKS, CH, P])),
            ):
                sp.dma_start(tile, src).then_inc(loaded, 16)
            for ns in pairs(sp):
                for p, n in enumerate(ns):
                    sp.wait_ge(out_ready, n + 1)
                    sp.dma_start(out[bass.ds(n, 1), :, :].rearrange("o (c p) d -> p (o c) d", p=P), XN[p][:, :, :])\
                      .then_inc(stored[p], 16)
            for p in range(2):
                sp.wait_ge(stored[p], SEQS * 8 + 16)

        @block.gpsimd
        def _(pool):
            pool.memset(ones[:, :], 1.0).then_inc(set_, 1)
            pool.memset(merge[:, :], MERGE).then_inc(set_, 1)
            pool.wait_ge(lnp_ready, 1)
            for ns in pairs(pool):
                for p, n in enumerate(ns):
                    ln_power(pool, ln, minus_half, n, p)
                for p, n in enumerate(ns):
                    pool.wait_ge(xn_ready, n + 1)
                    pool.tensor_tensor(X[p][:, :, :], X[p][:, :, :],
                                       lnp[:, 1, :].unsqueeze(1).broadcast_to([P, CH, P]), ALU.add)\
                        .then_inc(xb_ready, 1)
                for p, n in enumerate(ns):
                    ln_power(pool, ln_out, minus_half, n, p)

        @block.scalar
        def _(act):
            act.dma_start(tw2[:, :, :, :], a["L1_ffn_tv_W2"].rearrange("e (b p) d -> p e b d", p=P))\
               .then_inc(loaded, 16)
            act.dma_start(w2[:, :].rearrange("p (b d) -> p b d", b=FB), a["L1_ffn_W2"].rearrange("(b p) d -> p b d", p=P))\
               .then_inc(loaded, 16)
            act.wait_ge(loaded, LOADS + 32)
            for ns in pairs(act):
                for p, n in enumerate(ns):
                    act.wait_ge(xnT_ready, n + 1)
                    act.activation(XT[p][:, :], B[p][:, 0, :], ACT.Copy).then_inc(xt_ready, 1)
                for p, n in enumerate(ns):
                    act.wait_ge(gh_ps, n + 1)
                    act.activation(GH[p][:, :], B[p][:, 1, :], ACT.Relu, bias=gb1[:, :], accum_out=GS[p][:, :])\
                       .then_inc(gs_ready, 1)
                for p, n in enumerate(ns):
                    act.wait_ge(g_ps, n + 1)
                    act.activation(GB[p][:, :], B[p][:, 1, 0:TASKS], ACT.Copy).then_inc(gb_ready, 1)
                    act.activation(GC[p][:, :], B[p][0:TASKS, 1, P:2 * P], ACT.Copy).then_inc(gc_ready, 1)
                for p, n in enumerate(ns):
                    act.wait_ge(gb_ready, n + 1)
                    for e in range(TASKS):
                        last = act.activation(DG[p][:, e, :], ident, ACT.Copy, scale=GB[p][:, e:e + 1])
                    last.then_inc(dg_ready, 1)
                for p, n in enumerate(ns):
                    act.wait_ge(b1_steps, n * 3 + 3)
                    for fb in range(0, FB, 2):
                        act.wait_ge(hid_ready, n * FB + fb + 1)
                        act.activation(F[p][:, fb, :], B[p][:, fb, :], ACT.Relu, bias=B1[p][:, fb:fb + 1])\
                           .then_inc(relu_act, 1)

        @block.vector
        def _(dve):
            for p in range(2):
                dve.sem_inc(stored[p], 16)
            dve.wait_ge(loaded, LOADS + 32)
            dve.wait_ge(set_, 2)
            dve.tensor_tensor(tln[:, :, :], tln[:, :, :], ln8[:, :, :], ALU.subtract).then_inc(tln_ready, 1)
            dve.wait_ge(lnp_ps, 1)
            dve.tensor_tensor(lnp[:, :, :], lnp[:, :, :], B[0][:, 0, 0:2 * P].rearrange("p (o d) -> p o d", o=2), ALU.add)\
               .then_inc(lnp_ready, 1)
            dve.wait_ge(lnp_ready, 1)
            for ns in pairs(dve):
                for p, n in enumerate(ns):
                    x = H[:, bass.ds(n, 1), :].rearrange("p o (c d) -> p (o c) d", c=CH)
                    dve.tensor_copy(X[p][:, :, :], x).then_inc(x_ready, 1)
                    dve.wait_ge(x_ready, n + 1)
                    ln_measure(dve, ln, X[p], n, p)
                for p, n in enumerate(ns):
                    wait_apart(dve, stored[p], ns[0] * 8 + 16, passed)
                    ln_normalise(dve, ln, XN[p], X[p], n, p).then_inc(xn_ready, 1)
                for p, n in enumerate(ns):
                    dve.wait_ge(gs_ready, n + 1)
                    dve.tensor_scalar(GM[p][:, :], GS[p][:, :], 1.0 / SEQ, None, ALU.mult).then_inc(gm_ready, 1)
                    dve.wait_ge(gm_ready, n + 1)
                    dve.tensor_scalar(GR[p][:, :], ones[:, :], GM[p][:, :], None, ALU.mult).then_inc(gr_ready, 1)
                for p, n in enumerate(ns):
                    dve.wait_ge(gb_ready, n + 1)
                    dve.tensor_tensor(BT[p][:, :, :], tb1[:, :, :], GB[p][:, :].unsqueeze(1).broadcast_to([P, FB, TASKS]),
                                      ALU.mult).then_inc(b1_steps, 1)
                    dve.wait_ge(b1_steps, n * 3 + 1)
                    dve.tensor_reduce(BS[p][:, :], BT[p][:, :, :], AX_X, ALU.add).then_inc(b1_steps, 1)
                    dve.wait_ge(b1_steps, n * 3 + 2)
                    dve.tensor_tensor(B1[p][:, :], BS[p][:, :], b1[:, :], ALU.add).then_inc(b1_steps, 1)
                    for e in range(TASKS):
                        if e:
                            dve.wait_ge(wm2_steps, n * TASKS + e)
                        dve.scalar_tensor_tensor(
                            out=WM2[p][:, :], in0=tw2[:, e, :, :].rearrange("p b d -> p (b d)"), scalar=GB[p][:, e:e + 1],
                            in1=WM2[p][:, :] if e else w2[:, :], op0=ALU.mult, op1=ALU.add).then_inc(wm2_steps, 1)
                for p, n in enumerate(ns):
                    dve.wait_ge(w1_ps, n + 1)
                    dve.tensor_tensor(WM1[p][:, :], w1[:, :], B[p][:, 2, :], ALU.add).then_inc(wm1_ready, 1)
                for p, n in enumerate(ns):
                    dve.wait_ge(b1_steps, n * 3 + 3)
                    for fb in range(1, FB, 2):
                        dve.wait_ge(hid_ready, n * FB + fb + 1)
                        dve.tensor_scalar(F[p][:, fb, :], B[p][:, fb, :], B1[p][:, fb:fb + 1], 0.0, ALU.add, ALU.max)\
                           .then_inc(relu_dve, 1)
                for p, n in enumerate(ns):
                    dve.wait_ge(y_ready, n + 1)
                    dve.tensor_tensor(XN[p][:, :, :], XN[p][:, :, :],
                                      B[p][:, 0, :].rearrange("p (c d) -> p c d", c=CH), ALU.add)\
                       .then_inc(r_ready, 1)
                    dve.wait_ge(r_ready, n + 1)
                    ln_measure(dve, ln_out, XN[p], n, p)
                for p, n in enumerate(ns):
                    ln_normalise(dve, ln_out, XN[p], XN[p], n, p).then_inc(nr_ready, 1)
                    dve.wait_ge(nr_ready, n + 1)
                    dve.tensor_tensor(XN[p][:, :, :], XN[p][:, :, :],
                                      lnp[:, 0, :].unsqueeze(1).broadcast_to([P, CH, P]), ALU.mult)\
                       .then_inc(gain_done, 1)
                    dve.wait_ge(gain_done, n + 1)
                    dve.wait_ge(xb_ready, n + 1)
                    dve.tensor_tensor(XN[p][:, :, :], XN[p][:, :, :], X[p][:, :, :], ALU.add).then_inc(out_ready, 1)

        @block.tensor
        def _(pe):
            pe.wait_ge(tln_ready, 1)
            for j in range(2):
                last = pe.matmul(B[0][:, 0, chunk(j)], merge[:, :], tln[:, j, :], start=(j == 0), stop=(j == 1),
                                 skip_group_check=True)
            last.then_inc(lnp_ps, 1)
            pe.wait_ge(lnp_ready, 1)
            for ns in pairs(pe):
                for p, n in enumerate(ns):
                    pe.wait_ge(xn_ready, n + 1)
                    for c in range(CH):
                        last = pe.transpose(B[p][:, 0, chunk(c)], XN[p][:, c, :], ident)
                    last.then_inc(xnT_ready, 1)
                for p, n in enumerate(ns):
                    pe.wait_ge(xt_ready, n + 1)
                    pe.matmul(B[p][:, 1, :], wg1[:, :], XT[p][:, :], start=True, stop=True).then_inc(gh_ps, 1)
                for p, n in enumerate(ns):
                    pe.wait_ge(gr_ready, n + 1)
                    pe.matmul(B[p][:, 1, 0:TASKS], GR[p][:, :], wg2[:, :], start=True, stop=False, skip_group_check=True)
                    pe.matmul(B[p][:, 1, 0:TASKS], ones_row, gb2[:, :], start=False, stop=True, skip_group_check=True)
                    pe.matmul(B[p][0:TASKS, 1, P:2 * P], wg2[:, :], GR[p][:, :], start=False, stop=False,
                              skip_group_check=True)
                    pe.matmul(B[p][0:TASKS, 1, P:2 * P], gb2[:, :], ones_row, start=False, stop=True,
                              skip_group_check=True).then_inc(g_ps, 1)
                for p, n in enumerate(ns):
                    pe.wait_ge(dg_ready, n + 1)
                    for e in range(TASKS):
                        last = pe.matmul(B[p][:, 2, :], DG[p][:, e, :], tw1[:, e, :], start=(e == 0),
                                         stop=(e == TASKS - 1))
                    last.then_inc(w1_ps, 1)
                for p, n in enumerate(ns):
                    pe.wait_ge(wm1_ready, n + 1)
                    pe.wait_ge(gc_ready, n + 1)
                    for fb in range(FB):
                        pe.matmul(B[p][:, fb, :], WM1[p][:, chunk(fb)], XT[p][:, :], start=True, stop=True)\
                          .then_inc(hid_ready, 1)
                for p, n in enumerate(ns):
                    pe.wait_ge(relu_act, n * FB // 2 + FB // 2)
                    pe.wait_ge(relu_dve, n * FB // 2 + FB // 2)
                    pe.wait_ge(wm2_steps, n * TASKS + TASKS)
                    pe.matmul(B[p][:, 0, :], ones_row, b2[:, :, :].rearrange("o c d -> o (c d)"),
                              start=True, stop=False, skip_group_check=True)
                    pe.matmul(B[p][:, 0, :], GC[p][:, :], tb2[:, :, :].rearrange("o c d -> o (c d)"),
                              start=False, stop=False, skip_group_check=True)
                    for c in range(CH):
                        for fb in range(FB):
                            last = pe.matmul(B[p][:, 0, chunk(c)], F[p][:, fb, chunk(c)], WM2[p][:, chunk(fb)],
                                             start=False, stop=(c == CH - 1 and fb == FB - 1),
                                             skip_group_check=True)
                    last.then_inc(y_ready, 1)


TRANSPOSED = ("L0_ffn_gate_w", "L0_ffn_shared_gate_up", "L0_ffn_shared_down", "L0_ffn_expert_gate_up",
              "L0_ffn_expert_down", "L1_attn_q_w", "L1_attn_kv_w", "L1_ffn_gfc1_w", "L1_ffn_gfc2_w",
              "L1_ffn_W1", "L1_ffn_W2", "L1_ffn_tv_W1", "L1_ffn_tv_W2")
IN_COLUMNS = ("L0_attn_b1", "L1_ffn_b1")


def build(nc, a, out):
    with ExitStack() as ctx:
        sb, ps, sem = makers(nc, ctx)
        passed = sem("waits_passed")
        H = sb("H", [P, SEQS, SEQ])
        ident = sb("ident", [P, P])
        half = sb("minus_half", [P, CH])
        ones = sb("ones_row", [1, P])
        set_ = sem("consts_set")
        ident_done = sem("ident_done")
        with nc.Block() as block:
            @block.gpsimd
            def _(pool):
                pool.memset(ident[:, :], 0.0).then_inc(set_, 1)
                pool.memset(half[:, :], -0.5).then_inc(set_, 1)
                pool.memset(ones[:, :], 1.0).then_inc(set_, 1)
                pool.wait_ge(set_, 3)
                pool.affine_select(out=ident[:, :], in_=ident[:, :], compare_op=ALU.not_equal, fill=1.0, base=0,
                                   pattern=[[-1, P]], channel_multiplier=1).then_inc(ident_done, 1)
                pool.wait_ge(ident_done, 1)
        consts = {"ident": ident[:, :], "minus_half": half[:, :], "ones_row": ones[:, :],
                  "passed": passed}
        linear_attention_phase(nc, a, H, consts)
        expert_phase(nc, a, H, consts)
        cross_attention_phase(nc, a, H, consts)
        merged_ffn_phase(nc, a, H, out, consts)


def positions():
    pos = np.arange(1, SEQ + 1, dtype=np.float32)[:, None]
    i = np.arange(P)
    exponent = np.where(i % 2 == 0, i, i + 1).astype(np.float32) / np.float32(P)
    angle = pos / np.power(np.float32(10000.0), exponent)
    return np.where(i % 2 == 0, np.cos(angle), np.sin(angle)).astype(np.float32)


def kernel(**inputs):
    import concourse.bacc as bacc
    from concourse.bass_utils import run_bass_kernel_spmd as run

    nc = bacc.Bacc("TRN2", target_bir_lowering=False, num_devices=1)
    given = {k: np.asarray(v) for k, v in inputs.items()}
    x = given.pop("x")
    arrays = {"ids": x.reshape(SEQS * CH, P).T, "table": given.pop("L0_tok_W").T, "pos": positions()}
    for name in TRANSPOSED:
        w = given.pop(name)
        arrays[name] = w.swapaxes(-1, -2)
    for name in IN_COLUMNS:
        arrays[name] = given.pop(name).reshape(-1, P).T
    arrays["L1_ffn_tv_b1"] = given.pop("L1_ffn_tv_b1").reshape(TASKS, FB, P).T
    arrays.update(given)
    arrays = {f"in_{k}": np.ascontiguousarray(v) for k, v in arrays.items()}
    a = {k[3:]: nc.dram_tensor(k, v.shape, mybir.dt.from_np(v.dtype), kind="ExternalInput").ap()
         for k, v in arrays.items()}
    out = nc.dram_tensor("out_0", (SEQS, SEQ, P), F32, kind="ExternalOutput").ap()
    build(nc, a, out)
    r = run(nc, [arrays], core_ids=[0])
    return r.results[0]["out_0"]
```

```python
from contextlib import ExitStack

import numpy as np

import concourse.bass as bass
from concourse import mybir

F32 = mybir.dt.float32
I32 = mybir.dt.int32
BF16 = mybir.dt.bfloat16
U32 = mybir.dt.uint32
F32R = mybir.dt.float32r
ALU = mybir.AluOpType
ACT = mybir.ActivationFunctionType
AX_X = mybir.AxisListType.X

P = 128
SEQS, SEQ = 32, 512
CH = SEQ // P
HEADS, DH = 8, 16
STRIPS = 4
GROUPS = HEADS // STRIPS
VW = DH + 1
FF = 512
FB = FF // P
EXPERTS, TOP_K = 16, 3
TASKS = 8
EPS = 1e-5
DEN_MIN = 1e-6
GATE_EPS = 1e-9
MERGE = 0.03


def makers(nc, ctx):
    def sb(name, shape, dt=F32):
        return ctx.enter_context(nc.sbuf_tensor(name, shape, dt))

    def ps(name, shape):
        return ctx.enter_context(nc.psum_tensor(name, shape, F32))

    def sem(name):
        return ctx.enter_context(nc.semaphore(name))

    return sb, ps, sem


def wait_apart(engine, sem, value, passed):
    engine.wait_ge(sem, value)
    engine.sem_inc(passed, 1)


def chunk(c):
    return slice(c * P, (c + 1) * P)


def layer_norm(sb, sem, name, passed):
    return {
        "stats": [sb(f"{name}_stats{p}", [P, CH, 6]) for p in range(2)],
        "mv": [sb(f"{name}_mv{p}", [P, CH, 2]) for p in range(2)],
        "ve": [sb(f"{name}_ve{p}", [P, CH]) for p in range(2)],
        "rstd": [sb(f"{name}_rstd{p}", [P, CH]) for p in range(2)],
        "stats_done": sem(f"{name}_stats_done"),
        "mv_done": sem(f"{name}_mv_done"),
        "ve_done": sem(f"{name}_ve_done"),
        "rstd_done": sem(f"{name}_rstd_done"),
        "passed": passed,
    }


def ln_measure(dve, ln, x, n, p):
    for c in range(CH):
        last = dve.bn_stats(ln["stats"][p][:, c, :], x[:, c, :])
    last.then_inc(ln["stats_done"], 1)
    wait_apart(dve, ln["stats_done"], n + 1, ln["passed"])
    for c in range(CH):
        last = dve.bn_aggr(ln["mv"][p][:, c, :], ln["stats"][p][:, c, :])
    last.then_inc(ln["mv_done"], 1)


def ln_power(pool, ln, minus_half, n, p):
    wait_apart(pool, ln["mv_done"], n + 1, ln["passed"])
    pool.tensor_scalar(ln["ve"][p][:, :], ln["mv"][p][:, :, 1], EPS, None, ALU.add).then_inc(ln["ve_done"], 1)
    pool.wait_ge(ln["ve_done"], n + 1)
    pool.tensor_tensor(ln["rstd"][p][:, :], ln["ve"][p][:, :], minus_half, ALU.pow).then_inc(ln["rstd_done"], 1)


def ln_normalise(dve, ln, out, x, n, p):
    dve.wait_ge(ln["rstd_done"], n + 1)
    return ln_scale(dve, ln, out, x, p)


def ln_scale(engine, ln, out, x, p):
    for c in range(CH):
        last = engine.tensor_scalar(out[:, c, :], x[:, c, :], ln["mv"][p][:, c, 0:1], ln["rstd"][p][:, c:c + 1],
                                 ALU.subtract, ALU.mult)
    return last


def pairs(engine):
    with engine.Fori(0, SEQS // 2) as i:
        yield [2 * i, 2 * i + 1]


def linear_attention_phase(nc, a, H, consts):
    ident, minus_half, ones_row = consts["ident"], consts["minus_half"], consts["ones_row"]
    with ExitStack() as ctx:
        sb, ps, sem = makers(nc, ctx)
        passed = consts["passed"]
        two = lambda name, shape: [sb(f"a_{name}_{p}", shape) for p in range(2)]
        w4 = sb("a_w4", [P, 4, P])
        w1 = sb("a_w1", [P, FF])
        w2 = sb("a_w2", [P, FB, P])
        cols = sb("a_cols", [P, 6 + FB])
        BQ, BK, G1, B1, G2, B2, BF = range(7)
        rows = sb("a_rows", [1, 3, CH, P])
        tok_ids = sb("a_tok_ids", [P, SEQS * CH], I32)
        posb = sb("a_posb", [P, CH, P])
        tokb = sb("a_tokb", [P, P])
        even = sb("a_even", [P, 2])
        causal = sb("a_causal", [P, P])
        bdiag = sb("a_bdiag", [P, HEADS * VW])

        ids = two("ids", [P, CH])
        ids = [sb(f"a_idx{p}", [P, CH], I32) for p in range(2)]
        E = two("emb", [P, CH, P])
        X0 = two("x0", [P, CH, P])
        X1 = two("x1", [P, CH, P])
        XN = two("xn", [P, CH, P])
        HT = two("ht", [P, SEQ])
        TE = two("te", [P, SEQ])
        TK = two("tk", [P, SEQ])
        QT = two("qt", [P, SEQ])
        KT = two("kt", [P, SEQ])
        Q2 = two("q2", [P, 2, SEQ])
        KK = two("kk", [P, CH, P])
        V = two("v", [P, CH, HEADS, VW])
        S = two("s", [P, CH - 1, HEADS * VW])
        AT = two("at", [P, STRIPS, 4 * P])
        DN = two("dn", [P, 2, HEADS])
        RD = two("rd", [P, 2, HEADS])
        AN = two("an", [P, CH, P])
        ANT = two("ant", [P, SEQ])
        r1 = two("r1", [P, CH])
        t1 = two("t1", [P, CH])
        B = [ps(f"a_ps{p}", [P, 4, 512]) for p in range(2)]

        ln1, ln2 = layer_norm(sb, sem, "a_ln1", passed), layer_norm(sb, sem, "a_ln2", passed)
        loaded = sem("a_loaded")
        consts_set = sem("a_consts_set")
        masks_zero = sem("a_masks_zero")
        bdiag_done = sem("a_bdiag_done")
        posb_done = sem("a_posb_done")
        idx_ready = sem("a_idx_ready")
        emb_landed = [sem(f"a_emb_landed{p}") for p in range(2)]
        h_ready = sem("a_h_ready")
        x1_ready = sem("a_x1_ready")
        r1_steps = sem("a_r1_steps")
        xn_ready = sem("a_xn_ready")
        xnT_ready = sem("a_xnT_ready")
        ht_ready = sem("a_ht_ready")
        qkv_ready = sem("a_qkv_ready")
        exp_ready = sem("a_exp_ready")
        pos_ready = sem("a_pos_ready")
        qk_done = sem("a_qk_done")
        q2_ready = sem("a_q2_ready")
        v_ready = sem("a_v_ready")
        kT_ready = sem("a_kT_ready")
        kk_ready = sem("a_kk_ready")
        state_ready = sem("a_state_ready")
        s_ready = sem("a_s_ready")
        at_ready = [sem(f"a_at_ready{half}") for half in range(2)]
        mask_done = [sem(f"a_mask_done{half}") for half in range(2)]
        o_ready = [sem(f"a_o_ready{half}") for half in range(2)]
        dn_ready = [sem(f"a_dn_ready{half}") for half in range(2)]
        rd_ready = [sem(f"a_rd_ready{half}") for half in range(2)]
        an_ready = [sem(f"a_an_ready{half}") for half in range(2)]
        anT_ready = sem("a_anT_ready")
        ant_ready = sem("a_ant_ready")
        wo_ready = sem("a_wo_ready")
        x2_ready = sem("a_x2_ready")
        xn2_ready = sem("a_xn2_ready")
        xn2T_ready = sem("a_xn2T_ready")
        h2t_ready = sem("a_h2t_ready")
        hid_ready = sem("a_hid_ready")
        relu_act = sem("a_relu_act")
        relu_dve = sem("a_relu_dve")
        y_ready = sem("a_y_ready")
        x3_ready = sem("a_x3_ready")

        block = ctx.enter_context(nc.Block())

        @block.sync
        def _(sp):
            sp.dma_start(tok_ids[:, :], a["ids"]).then_inc(loaded, 16)
            sp.dma_start(tokb[:, :], a["L0_tok_b"].rearrange("(o d) -> o d", o=1).broadcast_to([P, P]))\
              .then_inc(loaded, 16)
            sp.dma_start(posb[:, :, :], a["pos"].rearrange("(c p) d -> p c d", p=P)).then_inc(loaded, 16)
            for j, name in enumerate(("L0_attn_bq", "L0_attn_bk", "L0_attn_ln1_g", "L0_attn_ln1_b",
                                      "L0_attn_ln2_g", "L0_attn_ln2_b")):
                sp.dma_start(cols[:, j:j + 1], a[name].rearrange("(d o) -> d o", o=1)).then_inc(loaded, 16)
            for j, name in enumerate(("L0_attn_Wq", "L0_attn_Wk", "L0_attn_Wv", "L0_attn_Wo")):
                sp.dma_start(w4[:, j, :], a[name]).then_inc(loaded, 16)
            sp.dma_start(w1[:, :], a["L0_attn_W1"]).then_inc(loaded, 16)
            sp.dma_start(w2[:, :, :], a["L0_attn_W2"].rearrange("(b p) d -> p b d", p=P)).then_inc(loaded, 16)
            sp.wait_ge(loaded, 16 * 19)

        @block.gpsimd
        def _(pool):
            pool.memset(causal[:, :], 1.0).then_inc(masks_zero, 1)
            pool.memset(bdiag[:, :], 1.0).then_inc(masks_zero, 1)
            pool.memset(even[:, :], 0.0).then_inc(masks_zero, 1)
            pool.wait_ge(masks_zero, 3)
            pool.affine_select(out=causal[:, :], in_=causal[:, :], compare_op=ALU.is_ge, fill=0.0, base=0,
                               pattern=[[1, P]], channel_multiplier=-1).then_inc(consts_set, 1)
            heads_view = bdiag[:, :].rearrange("p (h v) -> p h v", h=HEADS)
            pool.affine_select(out=heads_view, in_=heads_view, compare_op=ALU.is_ge, fill=0.0, base=0,
                               pattern=[[-DH, HEADS], [0, VW]], channel_multiplier=1).then_inc(bdiag_done, 1)
            pool.wait_ge(bdiag_done, 1)
            pool.affine_select(out=heads_view, in_=heads_view, compare_op=ALU.is_ge, fill=0.0, base=DH - 1,
                               pattern=[[DH, HEADS], [0, VW]], channel_multiplier=-1).then_inc(bdiag_done, 1)
            pool.wait_ge(bdiag_done, 2)
            for odd in range(2):
                for i in range(STRIPS):
                    pool.wait_ge(bdiag_done, 2 + odd * STRIPS + i)
                    h = 2 * i + odd
                    pool.tensor_tensor(even[:, odd:odd + 1], even[:, odd:odd + 1],
                                       bdiag[:, h * VW:h * VW + 1], ALU.add).then_inc(bdiag_done, 1)
            pool.wait_ge(bdiag_done, 2 + HEADS)
            pool.wait_ge(loaded, 16 * 19)
            for ns in pairs(pool):
                for p, n in enumerate(ns):
                    pool.wait_ge(h_ready, n + 1)
                    pool.tensor_copy(ids[p][:, :], tok_ids[:, bass.ds(n * CH, CH)]).then_inc(idx_ready, 1)
                    wait_apart(pool, idx_ready, n + 1, passed)
                    for c in range(CH):
                        pool.indirect_dma_start(
                            out=E[p][:, c, :], out_offset=None, in_=a["table"],
                            in_offset=bass.IndirectOffsetOnAxis(ap=ids[p][:, c:c + 1], axis=0),
                        ).then_inc(emb_landed[p], 16)
                for p, n in enumerate(ns):
                    ln_power(pool, ln1, minus_half, n, p)
                    pool.wait_ge(ln1["rstd_done"], n + 1)
                    pool.tensor_tensor(t1[p][:, :], ln1["rstd"][p][:, :], ln1["rstd"][p][:, :], ALU.mult)\
                        .then_inc(r1_steps, 1)
                    pool.wait_ge(r1_steps, n * 4 + 1)
                    pool.tensor_tensor(t1[p][:, :], t1[p][:, :], ln1["mv"][p][:, :, 1], ALU.mult)\
                        .then_inc(r1_steps, 1)
                    wait_apart(pool, r1_steps, n * 4 + 2, passed)
                    pool.tensor_scalar(t1[p][:, :], t1[p][:, :], EPS, None, ALU.add).then_inc(r1_steps, 1)
                    pool.wait_ge(r1_steps, n * 4 + 3)
                    pool.tensor_tensor(r1[p][:, :], t1[p][:, :], minus_half, ALU.pow).then_inc(r1_steps, 1)
                for p, n in enumerate(ns):
                    ln_power(pool, ln2, minus_half, n, p)

        @block.scalar
        def _(act):
            for j, name in enumerate(("L0_attn_bv", "L0_attn_bo", "L0_attn_b2")):
                act.dma_start(rows[:, j, :, :],
                              a[name].rearrange("(o c d) -> o c d", o=1, c=1).broadcast_to([1, CH, P]))\
                    .then_inc(loaded, 16)
            act.dma_start(cols[:, BF:BF + FB], a["L0_attn_b1"]).then_inc(loaded, 16)
            act.wait_ge(loaded, 16 * 19)
            act.activation(TE[0][:, 0:1], cols[:, 0:1], ACT.Exp, scale=0.0)
            for ns in pairs(act):
                for p, n in enumerate(ns):
                    act.wait_ge(x1_ready, n + 1)
                    act.wait_ge(r1_steps, n * 4 + 4)
                    for c in range(CH):
                        last = act.activation(XN[p][:, c, :], X1[p][:, c, :], ACT.Copy, scale=r1[p][:, c:c + 1])
                    last.then_inc(xn_ready, 1)
                for p, n in enumerate(ns):
                    act.wait_ge(xnT_ready, n + 1)
                    act.activation(HT[p][:, :], B[p][:, 0, :], ACT.Identity, bias=cols[:, B1:B1 + 1],
                                   scale=cols[:, G1:G1 + 1]).then_inc(ht_ready, 1)
                for p, n in enumerate(ns):
                    act.wait_ge(qkv_ready, n * 3 + 1)
                    act.activation(TE[p][:, :], B[p][:, 1, :], ACT.Exp, bias=cols[:, BQ:BQ + 1])\
                        .then_inc(exp_ready, 1)
                    act.wait_ge(qkv_ready, n * 3 + 2)
                    act.activation(TK[p][:, :], B[p][:, 2, :], ACT.Exp, bias=cols[:, BK:BK + 1])\
                        .then_inc(exp_ready, 1)
                    act.wait_ge(qkv_ready, n * 3 + 3)
                    act.activation(V[p][:, :, :, 0:DH],
                                   B[p][:, 3, :].rearrange("p (c h d) -> p c h d", c=CH, h=HEADS), ACT.Copy)\
                        .then_inc(v_ready, 1)
                for p, n in enumerate(ns):
                    act.wait_ge(kT_ready, n + 1)
                    act.activation(KK[p][:, :, :], B[p][:, 0, :].rearrange("p (c d) -> p c d", c=CH), ACT.Copy)\
                        .then_inc(kk_ready, 1)
                for p, n in enumerate(ns):
                    act.wait_ge(anT_ready, n + 1)
                    act.activation(ANT[p][:, :], B[p][:, 1, :], ACT.Copy).then_inc(ant_ready, 1)
                for p, n in enumerate(ns):
                    act.wait_ge(xn2T_ready, n + 1)
                    act.activation(HT[p][:, :], B[p][:, 3, :], ACT.Identity, bias=cols[:, B2:B2 + 1],
                                   scale=cols[:, G2:G2 + 1]).then_inc(h2t_ready, 1)
                for p, n in enumerate(ns):
                    for fb in range(0, FB, 2):
                        act.wait_ge(hid_ready, n * FB + fb + 1)
                        act.activation(AT[p][:, fb, :], B[p][:, fb, :], ACT.Relu, bias=cols[:, BF + fb:BF + fb + 1])\
                            .then_inc(relu_act, 1)

        @block.vector
        def _(dve):
            for p in range(2):
                dve.memset(V[p][:, :, :, DH:VW], 1.0)
            dve.sem_inc(h_ready, 2)
            dve.wait_ge(loaded, 16 * 19)
            dve.tensor_tensor(posb[:, :, :], posb[:, :, :], tokb[:, :].unsqueeze(1).broadcast_to([P, CH, P]), ALU.add)\
               .then_inc(posb_done, 1)
            dve.wait_ge(posb_done, 1)
            dve.wait_ge(consts_set, 1)
            dve.wait_ge(bdiag_done, 2 + HEADS)
            for ns in pairs(dve):
                for p, n in enumerate(ns):
                    dve.wait_ge(emb_landed[p], (ns[0] + 1) * 8 * CH + 8 * CH)
                    dve.tensor_tensor(X0[p][:, :, :], E[p][:, :, :], posb[:, :, :], ALU.add)\
                       .then_inc(h_ready, 1)
                    dve.wait_ge(h_ready, n + 3)
                    ln_measure(dve, ln1, X0[p], n, p)
                for p, n in enumerate(ns):
                    ln_normalise(dve, ln1, X1[p], X0[p], n, p).then_inc(x1_ready, 1)
                for p, n in enumerate(ns):
                    for j, (out, e, b) in enumerate(((QT, TE, BQ), (KT, TK, BK))):
                        dve.wait_ge(exp_ready, n * 2 + j + 1)
                        dve.tensor_scalar(out[p][:, :], B[p][:, 1 + j, :], cols[:, b:b + 1], 0.0, ALU.add, ALU.max)\
                           .then_inc(pos_ready, 1)
                    for j, (out, e) in enumerate(((QT, TE), (KT, TK))):
                        dve.wait_ge(pos_ready, n * 2 + j + 1)
                        dve.scalar_tensor_tensor(out=out[p][:, :], in0=e[p][:, :], scalar=1.0, in1=out[p][:, :],
                                                 op0=ALU.min, op1=ALU.add).then_inc(qk_done, 1)
                    dve.wait_ge(qk_done, n * 2 + 1)
                    for odd in range(2):
                        last = dve.tensor_scalar(Q2[p][:, odd, :], QT[p][:, :], even[:, odd:odd + 1], None, ALU.mult)
                    last.then_inc(q2_ready, 1)
                for p, n in enumerate(ns):
                    dve.wait_ge(state_ready, n + 1)
                    dve.tensor_tensor(
                        S[p][:, :, :], B[p][:, 1, 0:(CH - 1) * HEADS * VW].rearrange("p (c v) -> p c v", c=CH - 1),
                        bdiag[:, :].unsqueeze(1).broadcast_to([P, CH - 1, HEADS * VW]), ALU.mult)\
                       .then_inc(s_ready, 1)
                for half in range(2):
                    for p, n in enumerate(ns):
                        dve.wait_ge(at_ready[half], n + 1)
                        dve.tensor_tensor(
                            AT[p][:, :, :].rearrange("p i (k t) -> p (i k) t", k=4),
                            B[p][:, :, :].rearrange("p i (k t) -> p (i k) t", k=4),
                            causal[:, :].unsqueeze(1).broadcast_to([P, 16, P]), ALU.mult)\
                           .then_inc(mask_done[half], 1)
                    for p, n in enumerate(ns):
                        dve.wait_ge(o_ready[half], n + 1)
                        o = B[p][:, 0, 0:2 * HEADS * VW].rearrange("p (c h v) -> p c h v", c=2, h=HEADS)
                        dve.tensor_scalar(DN[p][:, :, :], o[:, :, :, DH], DEN_MIN, None, ALU.max)\
                           .then_inc(dn_ready[half], 1)
                        dve.wait_ge(dn_ready[half], n + 1)
                        dve.reciprocal(RD[p][:, :, :], DN[p][:, :, :]).then_inc(rd_ready[half], 1)
                        dve.wait_ge(rd_ready[half], n + 1)
                        dve.tensor_tensor(
                            AN[p][:, 2 * half:2 * half + 2, :].rearrange("p c (h d) -> p c h d", h=HEADS),
                            o[:, :, :, 0:DH],
                            RD[p][:, :, :].unsqueeze(3).broadcast_to([P, 2, HEADS, DH]), ALU.mult)\
                           .then_inc(an_ready[half], 1)
                for p, n in enumerate(ns):
                    dve.wait_ge(wo_ready, n + 1)
                    dve.tensor_tensor(X1[p][:, :, :], X1[p][:, :, :],
                                      B[p][:, 2, :].rearrange("p (c d) -> p c d", c=CH), ALU.add)\
                       .then_inc(x2_ready, 1)
                    dve.wait_ge(x2_ready, n + 1)
                    ln_measure(dve, ln2, X1[p], n, p)
                for p, n in enumerate(ns):
                    ln_normalise(dve, ln2, XN[p], X1[p], n, p).then_inc(xn2_ready, 1)
                for p, n in enumerate(ns):
                    for fb in range(1, FB, 2):
                        dve.wait_ge(hid_ready, n * FB + fb + 1)
                        dve.tensor_scalar(AT[p][:, fb, :], B[p][:, fb, :], cols[:, BF + fb:BF + fb + 1], 0.0,
                                          ALU.add, ALU.max).then_inc(relu_dve, 1)
                for p, n in enumerate(ns):
                    dve.wait_ge(y_ready, n + 1)
                    dve.tensor_tensor(X1[p][:, :, :], X1[p][:, :, :],
                                      B[p][:, 0, :].rearrange("p (c d) -> p c d", c=CH), ALU.add)\
                       .then_inc(x3_ready, 1)
                    dve.wait_ge(x3_ready, n + 1)
                    dve.tensor_tensor(H[:, bass.ds(n, 1), :], X1[p][:, :, :].rearrange("p c d -> p (c d)").unsqueeze(1),
                                      X0[p][:, :, :].rearrange("p c d -> p (c d)").unsqueeze(1), ALU.add)

        @block.tensor
        def _(pe):
            pe.wait_ge(loaded, 16 * 19)
            for ns in pairs(pe):
                for p, n in enumerate(ns):
                    pe.wait_ge(xn_ready, n + 1)
                    for c in range(CH):
                        last = pe.transpose(B[p][:, 0, chunk(c)], XN[p][:, c, :], ident)
                    last.then_inc(xnT_ready, 1)
                for p, n in enumerate(ns):
                    pe.wait_ge(ht_ready, n + 1)
                    for j in range(2):
                        pe.matmul(B[p][:, 1 + j, :], w4[:, j, :], HT[p][:, :], start=True, stop=True)\
                          .then_inc(qkv_ready, 1)
                    pe.matmul(B[p][:, 3, :], ones_row, rows[:, 0, :, :].rearrange("o c d -> o (c d)"),
                              start=True, stop=False, skip_group_check=True)
                    for c in range(CH):
                        last = pe.matmul(B[p][:, 3, chunk(c)], HT[p][:, chunk(c)], w4[:, 2, :], start=False,
                                         stop=(c == CH - 1), skip_group_check=True)
                    last.then_inc(qkv_ready, 1)
                for p, n in enumerate(ns):
                    pe.wait_ge(qk_done, n * 2 + 2)
                    for c in range(CH):
                        last = pe.transpose(B[p][:, 0, chunk(c)], KT[p][:, chunk(c)], ident)
                    last.then_inc(kT_ready, 1)
                for p, n in enumerate(ns):
                    pe.wait_ge(kk_ready, n + 1)
                    pe.wait_ge(v_ready, n + 1)
                    for c in range(1, CH):
                        for b in range(c):
                            last = pe.matmul(B[p][:, 1, (c - 1) * HEADS * VW:c * HEADS * VW], KK[p][:, b, :],
                                             V[p][:, b, :, :].rearrange("p h v -> p (h v)"),
                                             start=(c == 1 and b == 0), stop=(b == c - 1), skip_group_check=True)
                    last.then_inc(state_ready, 1)
                for half in range(2):
                    for p, n in enumerate(ns):
                        if half == 0:
                            pe.wait_ge(s_ready, n + 1)
                            pe.wait_ge(q2_ready, n + 1)
                        else:
                            pe.wait_ge(an_ready[0], n + 1)
                        for odd in range(2):
                            for cc in range(2):
                                c = 2 * half + cc
                                for i in range(STRIPS):
                                    rows32 = slice(32 * i, 32 * i + 32)
                                    last = pe.matmul(B[p][:, i, (2 * odd + cc) * P:(2 * odd + cc + 1) * P],
                                                     KT[p][rows32, chunk(c)], Q2[p][rows32, odd, chunk(c)],
                                                     start=True, stop=True)
                        last.then_inc(at_ready[half], 1)
                    for p, n in enumerate(ns):
                        pe.wait_ge(mask_done[half], n + 1)
                        for cc in range(2):
                            c = 2 * half + cc
                            first = cc == 0
                            if c:
                                pe.matmul(B[p][:, 0, cc * HEADS * VW:(cc + 1) * HEADS * VW], QT[p][:, chunk(c)],
                                          S[p][:, c - 1, :], start=first, stop=False, skip_group_check=True)
                                first = False
                            for h in range(HEADS):
                                i, odd = h // 2, h % 2
                                at = (cc * HEADS + h) * VW
                                last = pe.matmul(B[p][:, 0, at:at + VW],
                                                 AT[p][:, i, (2 * odd + cc) * P:(2 * odd + cc + 1) * P],
                                                 V[p][:, c, h, :], start=first, stop=True, skip_group_check=True)
                                first = False
                        last.then_inc(o_ready[half], 1)
                for p, n in enumerate(ns):
                    pe.wait_ge(an_ready[1], n + 1)
                    for c in range(CH):
                        last = pe.transpose(B[p][:, 1, chunk(c)], AN[p][:, c, :], ident)
                    last.then_inc(anT_ready, 1)
                for p, n in enumerate(ns):
                    pe.wait_ge(ant_ready, n + 1)
                    pe.matmul(B[p][:, 2, :], ones_row, rows[:, 1, :, :].rearrange("o c d -> o (c d)"),
                              start=True, stop=False, skip_group_check=True)
                    for c in range(CH):
                        last = pe.matmul(B[p][:, 2, chunk(c)], ANT[p][:, chunk(c)], w4[:, 3, :], start=False,
                                         stop=(c == CH - 1), skip_group_check=True)
                    last.then_inc(wo_ready, 1)
                for p, n in enumerate(ns):
                    pe.wait_ge(xn2_ready, n + 1)
                    for c in range(CH):
                        last = pe.transpose(B[p][:, 3, chunk(c)], XN[p][:, c, :], ident)
                    last.then_inc(xn2T_ready, 1)
                for p, n in enumerate(ns):
                    pe.wait_ge(h2t_ready, n + 1)
                    for fb in range(FB):
                        pe.matmul(B[p][:, fb, :], w1[:, chunk(fb)], HT[p][:, :], start=True, stop=True)\
                          .then_inc(hid_ready, 1)
                for p, n in enumerate(ns):
                    pe.wait_ge(relu_act, n * FB // 2 + FB // 2)
                    pe.wait_ge(relu_dve, n * FB // 2 + FB // 2)
                    pe.matmul(B[p][:, 0, :], ones_row, rows[:, 2, :, :].rearrange("o c d -> o (c d)"),
                              start=True, stop=False, skip_group_check=True)
                    for c in range(CH):
                        for fb in range(FB):
                            last = pe.matmul(B[p][:, 0, chunk(c)], AT[p][:, fb, chunk(c)], w2[:, fb, :],
                                             start=False, stop=(c == CH - 1 and fb == FB - 1),
                                             skip_group_check=True)
                    last.then_inc(y_ready, 1)


def expert_phase(nc, a, H, consts):
    ident, minus_half = consts["ident"], consts["minus_half"]
    LAST = EXPERTS
    UNITS = EXPERTS + 1
    with ExitStack() as ctx:
        sb, ps, sem = makers(nc, ctx)
        passed = consts["passed"]
        two = lambda name, shape, dt=F32: [sb(f"e_{name}_{p}", shape, dt) for p in range(2)]
        wgu = sb("e_wgu", [P, UNITS, 2 * P])
        wgu_hi = sb("e_wgu_hi", [P, UNITS, 2 * P], F32R)
        wgu_lo = sb("e_wgu_lo", [P, UNITS, 2 * P], F32R)
        wdn = sb("e_wdn", [P, UNITS, P])
        wr = sb("e_wr", [P, EXPERTS])
        ebias = sb("e_bias", [P, EXPERTS])
        iota = sb("e_iota", [P, EXPERTS])
        XN = two("xn", [P, CH, P])
        XT = two("xt", [P, SEQ])
        XH = two("xh", [P, SEQ], F32R)
        XL = two("xl", [P, SEQ], F32R)
        EX = two("ex", [P, CH, EXPERTS])
        AF = two("af", [P, CH, EXPERTS])
        SC = two("sc", [P, CH, EXPERTS])
        T8 = two("t8", [P, CH, 8])
        I8 = two("i8", [P, CH, 8], U32)
        IF = two("if", [P, CH, 8])
        OH = two("oh", [P, CH, EXPERTS, TOP_K])
        GS = two("gs", [P, CH])
        GATE = two("gate", [P, CH, EXPERTS])
        ACC = two("acc", [P, CH, P])
        SIL = two("sil", [P, SEQ])
        HID = [sb(f"e_hid_{j}", [P, SEQ]) for j in range(3)]
        GP = [ps(f"e_gp{p}", [P, 512]) for p in range(2)]
        UP = [ps(f"e_up{p}", [P, 512]) for p in range(2)]
        DP = [ps(f"e_dp{p}", [P, 512]) for p in range(2)]
        TP = [ps(f"e_tp{p}", [P, 512]) for p in range(2)]

        ln = layer_norm(sb, sem, "e_ln", passed)
        loaded = sem("e_loaded")
        iota_done = sem("e_iota_done")
        w_split = sem("e_w_split")
        x_split = sem("e_x_split")
        xn_ready = sem("e_xn_ready")
        xnT_ready = sem("e_xnT_ready")
        xt_ready = sem("e_xt_ready")
        logit_ready = sem("e_logit_ready")
        ex_ready = sem("e_ex_ready")
        steps = sem("e_route_steps")
        gate_steps = sem("e_gate_steps")
        gu_ready = sem("e_gu_ready")
        sil_ready = sem("e_sil_ready")
        hid_ready = sem("e_hid_ready")
        dn_ready = sem("e_dn_ready")
        acc_ready = sem("e_acc_ready")
        h_ready = sem("e_h_ready")
        LOADS = 16 * 6

        block = ctx.enter_context(nc.Block())

        @block.sync
        def _(sp):
            sp.dma_start(wr[:, :], a["L0_ffn_gate_w"]).then_inc(loaded, 16)
            sp.dma_start(ebias[:, :], a["L0_ffn_expert_bias"].rearrange("(o d) -> o d", o=1)
                         .broadcast_to([P, EXPERTS])).then_inc(loaded, 16)
            sp.dma_start(wgu[:, 0, :], a["L0_ffn_shared_gate_up"]).then_inc(loaded, 16)
            sp.dma_start(wdn[:, 0, :], a["L0_ffn_shared_down"]).then_inc(loaded, 16)
            sp.dma_start(wgu[:, 1:UNITS, :], a["L0_ffn_expert_gate_up"].rearrange("e d f -> d e f"))\
              .then_inc(loaded, 16)
            sp.dma_start(wdn[:, 1:UNITS, :], a["L0_ffn_expert_down"].rearrange("e f d -> f e d"))\
              .then_inc(loaded, 16)
            sp.wait_ge(loaded, LOADS)

        @block.gpsimd
        def _(pool):
            pool.sem_inc(h_ready, 1)
            pool.iota(iota[:, :], pattern=[[1, EXPERTS]], base=0, channel_multiplier=0,
                      allow_small_or_imprecise_dtypes=True).then_inc(iota_done, 1)
            for ns in pairs(pool):
                for p, n in enumerate(ns):
                    ln_power(pool, ln, minus_half, n, p)
                for p, n in enumerate(ns):
                    pool.wait_ge(acc_ready, n * UNITS + UNITS + 1)
                    pool.tensor_copy(H[:, bass.ds(n, 1), :],
                                     ACC[p][:, :, :].rearrange("p c d -> p (c d)").unsqueeze(1)).then_inc(h_ready, 1)

        @block.scalar
        def _(act):
            for ns in pairs(act):
                for p, n in enumerate(ns):
                    act.wait_ge(xnT_ready, n + 1)
                    act.activation(XT[p][:, :], TP[p][:, :], ACT.Copy).then_inc(xt_ready, 1)
                for p, n in enumerate(ns):
                    act.wait_ge(logit_ready, n + 1)
                    act.activation(EX[p][:, :, :], TP[p][:, 0:CH * EXPERTS].rearrange("p (c e) -> p c e", c=CH),
                                   ACT.Exp, scale=-1.0).then_inc(ex_ready, 1)
                for p, n in enumerate(ns):
                    for e in range(UNITS):
                        act.wait_ge(gu_ready, n * UNITS + e + 1)
                        act.wait_ge(hid_ready, n * UNITS + max(e - 1, 0) + 1)
                        act.activation(SIL[e % 2][:, :], GP[e % 2][:, :], ACT.Silu).then_inc(sil_ready, 1)

        @block.vector
        def _(dve):
            dve.sem_inc(hid_ready, 1)
            dve.sem_inc(acc_ready, 1)
            dve.wait_ge(loaded, LOADS)
            dve.wait_ge(iota_done, 1)
            dve.tensor_copy(wgu_hi[:, :, :], wgu[:, :, :]).then_inc(w_split, 1)
            dve.wait_ge(w_split, 1)
            dve.tensor_tensor(wgu_lo[:, :, :], wgu[:, :, :], wgu_hi[:, :, :], ALU.subtract).then_inc(w_split, 1)
            for ns in pairs(dve):
                for p, n in enumerate(ns):
                    x = H[:, bass.ds(n, 1), :].rearrange("p o (c d) -> p (o c) d", c=CH)
                    wait_apart(dve, h_ready, ns[0] + 1, passed)
                    dve.tensor_copy(ACC[p][:, :, :], x).then_inc(steps, 1)
                    dve.wait_ge(steps, ns[0] * 10 + p + 1)
                    ln_measure(dve, ln, ACC[p], n, p)
                for p, n in enumerate(ns):
                    ln_normalise(dve, ln, XN[p], ACC[p], n, p).then_inc(xn_ready, 1)
                for p, n in enumerate(ns):
                    dve.wait_ge(xt_ready, n + 1)
                    dve.tensor_copy(XH[p][:, :], XT[p][:, :]).then_inc(x_split, 1)
                    dve.wait_ge(x_split, n * 2 + 1)
                    dve.tensor_tensor(XL[p][:, :], XT[p][:, :], XH[p][:, :], ALU.subtract).then_inc(x_split, 1)
                for p, n in enumerate(ns):
                    done = [2 + 9 * p]

                    def step(ins):
                        ins.then_inc(steps, 1)
                        done[0] += 1
                        wait_apart(dve, steps, ns[0] * 10 + done[0], passed)

                    dve.wait_ge(ex_ready, n + 1)
                    step(dve.tensor_scalar(EX[p][:, :, :], EX[p][:, :, :], 1.0, None, ALU.add))
                    step(dve.reciprocal(AF[p][:, :, :], EX[p][:, :, :]))
                    step(dve.tensor_tensor(SC[p][:, :, :], AF[p][:, :, :],
                                           ebias[:, :].unsqueeze(1).broadcast_to([P, CH, EXPERTS]), ALU.add))
                    for c in range(CH):
                        last = dve.max(T8[p][:, c, :], SC[p][:, c, :])
                    last.then_inc(steps, 1)
                    done[0] += 1
                    wait_apart(dve, steps, ns[0] * 10 + done[0], passed)
                    for c in range(CH):
                        last = dve.max_index(I8[p][:, c, :], T8[p][:, c, :], SC[p][:, c, :])
                    step(last)
                    step(dve.tensor_copy(IF[p][:, :, :], I8[p][:, :, :]))
                    step(dve.tensor_tensor(
                        OH[p][:, :, :, :], IF[p][:, :, 0:TOP_K].unsqueeze(2).broadcast_to([P, CH, EXPERTS, TOP_K]),
                        iota[:, :].unsqueeze(1).unsqueeze(3).broadcast_to([P, CH, EXPERTS, TOP_K]), ALU.is_equal))
                    step(dve.tensor_reduce(SC[p][:, :, :], OH[p][:, :, :, :], AX_X, ALU.add))
                    step(dve.tensor_tensor(AF[p][:, :, :], AF[p][:, :, :], SC[p][:, :, :], ALU.mult))
                for p, n in enumerate(ns):
                    dve.tensor_reduce(GS[p][:, :], AF[p][:, :, :], AX_X, ALU.add).then_inc(gate_steps, 1)
                    dve.wait_ge(gate_steps, n * 4 + 1)
                    dve.tensor_scalar(GS[p][:, :], GS[p][:, :], GATE_EPS, None, ALU.add).then_inc(gate_steps, 1)
                    dve.wait_ge(gate_steps, n * 4 + 2)
                    dve.reciprocal(GS[p][:, :], GS[p][:, :]).then_inc(gate_steps, 1)
                    dve.wait_ge(gate_steps, n * 4 + 3)
                    dve.tensor_tensor(GATE[p][:, :, :], AF[p][:, :, :],
                                      GS[p][:, :].unsqueeze(2).broadcast_to([P, CH, EXPERTS]), ALU.mult)\
                       .then_inc(gate_steps, 1)
                for p, n in enumerate(ns):
                    def add(e):
                        dve.wait_ge(dn_ready, n * UNITS + e + 1 + 1)
                        if e == 0:
                            dve.tensor_tensor(ACC[p][:, :, :], ACC[p][:, :, :],
                                              DP[0][:, :].rearrange("p (c d) -> p c d", c=CH), ALU.add)\
                               .then_inc(acc_ready, 1)
                            return
                        dve.wait_ge(acc_ready, n * UNITS + e + 1)
                        if e == 1:
                            dve.wait_ge(gate_steps, n * 4 + 4)
                        for c in range(CH):
                            last = dve.scalar_tensor_tensor(
                                out=ACC[p][:, c, :], in0=DP[e % 2][:, chunk(c)], scalar=GATE[p][:, c, e - 1:e],
                                in1=ACC[p][:, c, :], op0=ALU.mult, op1=ALU.add)
                        last.then_inc(acc_ready, 1)

                    for e in range(UNITS):
                        dve.wait_ge(sil_ready, n * UNITS + e + 1)
                        dve.wait_ge(dn_ready, n * UNITS + max(e - 2, 0) + 1)
                        dve.tensor_tensor(HID[e % 3][:, :], SIL[e % 2][:, :], UP[e % 2][:, :], ALU.mult)\
                           .then_inc(hid_ready, 1)
                        if e >= 2:
                            add(e - 2)
                    add(LAST - 1)
                    add(LAST)

        @block.tensor
        def _(pe):
            pe.sem_inc(dn_ready, 1)
            pe.wait_ge(loaded, LOADS)
            pe.wait_ge(w_split, 2)
            for ns in pairs(pe):
                for p, n in enumerate(ns):
                    pe.wait_ge(xn_ready, n + 1)
                    for c in range(CH):
                        last = pe.transpose(TP[p][:, chunk(c)], XN[p][:, c, :], ident)
                    last.then_inc(xnT_ready, 1)
                for p, n in enumerate(ns):
                    pe.wait_ge(xt_ready, n + 1)
                    for c in range(CH):
                        last = pe.matmul(TP[p][:, c * EXPERTS:(c + 1) * EXPERTS], XT[p][:, chunk(c)], wr[:, :],
                                         start=(c == 0), stop=(c == CH - 1), skip_group_check=True)
                    last.then_inc(logit_ready, 1)
                for p, n in enumerate(ns):
                    def down(e):
                        pe.wait_ge(hid_ready, n * UNITS + e + 1 + 1)
                        pe.wait_ge(acc_ready, n * UNITS + max(e - 1, 0) + 1)
                        for c in range(CH):
                            last = pe.matmul(DP[e % 2][:, chunk(c)], HID[e % 3][:, chunk(c)], wdn[:, e, :],
                                             start=(c == 0), stop=(c == CH - 1), skip_group_check=True)
                        last.then_inc(dn_ready, 1)

                    pe.wait_ge(x_split, n * 2 + 2)
                    for e in range(UNITS):
                        pe.wait_ge(hid_ready, n * UNITS + max(e - 1, 0) + 1)
                        for out, cols in ((GP, slice(0, P)), (UP, slice(P, 2 * P))):
                            for k, (w, x) in enumerate(((wgu_hi, XH), (wgu_hi, XL), (wgu_lo, XH))):
                                last = pe.matmul(out[e % 2][:, :], w[:, e, cols], x[p][:, :],
                                                 start=(k == 0), stop=(k == 2))
                        last.then_inc(gu_ready, 1)
                        if e >= 2:
                            down(e - 2)
                    down(LAST - 1)
                    down(LAST)


def cross_attention_phase(nc, a, H, consts):
    ident, minus_half = consts["ident"], consts["minus_half"]
    SCALE = float(P) ** -0.5
    TILES = CH * GROUPS * STRIPS
    ROUNDS = TILES // 2
    PARTS = 3
    Q_PARTS, K_PARTS = (0, 0, 1, 0, 2, 1), (0, 1, 0, 2, 0, 1)
    ROWS = DH * len(Q_PARTS)
    PAIRS = SEQS // 2
    TURN = 11
    FIRST_TILE = 7
    tiles = [(c, g, i) for c in range(CH) for g in range(GROUPS) for i in range(STRIPS)]
    with ExitStack() as ctx:
        sb, ps, sem = makers(nc, ctx)
        passed = consts["passed"]
        two = lambda name, shape, dt=F32: [sb(f"c_{name}_{p}", shape, dt) for p in range(2)]
        wq = sb("c_wq", [P, P])
        wk = sb("c_wk", [P, P])
        wv = sb("c_wv", [P, P])
        X = two("x", [P, CH, P])
        XN = two("xn", [P, CH, P])
        XT = two("xt", [P, SEQ])
        SPLIT = two("split", [P, 2, PARTS, SEQ], BF16)
        R1 = two("r1", [P, 2, SEQ])
        QS_A, KS_A = sb("c_qs_a", [P, HEADS, SEQ], BF16), sb("c_ks_a", [P, HEADS, SEQ], BF16)
        QS_B, KS_B = two("qs_b", [P, HEADS, SEQ], BF16), two("ks_b", [P, HEADS, SEQ], BF16)
        MF = sb("c_mf", [HEADS, SEQ])
        MR = sb("c_mr", [HEADS, SEQ])
        MS = two("ms", [HEADS, PARTS, SEQ], BF16)
        VT = two("vt", [P, SEQ])
        V = two("v", [P, CH, HEADS, 32])
        NM = two("nm", [P, CH, HEADS])
        PT = two("pt", [P, 2, SEQ])
        OS = sb("c_os", [P, GROUPS, SEQ])
        RD = sb("c_rd", [P, GROUPS, CH, STRIPS])
        AO = two("ao", [P, CH, P])
        S1 = ps("c_s1", [P, 2, 512])
        S2 = [ps(f"c_s2_{p}", [P, 2, 512]) for p in range(2)]
        O = ps("c_o", [P, GROUPS, 512])

        ln = layer_norm(sb, sem, "c_ln", passed)
        split_dram = [nc.dram_tensor(f"c_split_dram{p}", (P, 2, PARTS, SEQ), BF16).ap() for p in range(2)]
        max_dram = [nc.dram_tensor(f"c_max_dram{p}", (HEADS, PARTS, SEQ), BF16).ap() for p in range(2)]
        zeroed = sem("c_zeroed")
        loaded = sem("c_loaded")
        ones_set = sem("c_ones_set")
        x_ready = sem("c_x_ready")
        xn_ready = sem("c_xn_ready")
        xnT_ready = sem("c_xnT_ready")
        xt_ready = sem("c_xt_ready")
        qk_ps = sem("c_qk_ps")
        v_ps = sem("c_v_ps")
        part1_ready = sem("c_part1_ready")
        rest_ready = sem("c_rest_ready")
        part2_ready = sem("c_part2_ready")
        part3_ready = sem("c_part3_ready")
        v_ready = sem("c_v_ready")
        v_placed = sem("c_v_placed")
        to_dram = [sem(f"c_to_dram{p}") for p in range(2)]
        stacked = [sem(f"c_stacked{p}") for p in range(2)]
        max_in = [sem(f"c_max_in{p}") for p in range(2)]
        STACKED = 16 * 2 * len(Q_PARTS)
        mf_ready = sem("c_mf_ready")
        m_steps = sem("c_m_steps")
        s1_ready = sem("c_s1_ready")
        s1_read = sem("c_s1_read")
        nmT_ready = sem("c_nmT_ready")
        s2_ready = sem("c_s2_ready")
        pt_ready = sem("c_pt_ready")
        pv_done = sem("c_pv_done")
        os_ready = sem("c_os_ready")
        oT_ready = sem("c_oT_ready")
        rd_ready = sem("c_rd_ready")
        ao_ready = sem("c_ao_ready")
        LOADS = 16 * 3

        def stack_q(p, b):
            return QS_B[b] if p else QS_A

        def stack_k(p, b):
            return KS_B[b] if p else KS_A

        def twins(engine):
            with engine.Fori(0, PAIRS // 2 - 1) as j:
                for b in range(2):
                    yield 4 * j + 2 * b, 2 * j + b, b, True
            yield SEQS - 4, PAIRS - 2, 0, True
            yield SEQS - 2, PAIRS - 1, 1, False

        block = ctx.enter_context(nc.Block())

        @block.sync
        def _(sp):
            sp.dma_start(wq[:, :], a["L1_attn_q_w"]).then_inc(loaded, 16)
            sp.dma_start(wk[:, :], a["L1_attn_kv_w"][:, 0:P]).then_inc(loaded, 16)
            sp.dma_start(wv[:, :], a["L1_attn_kv_w"][:, P:2 * P]).then_inc(loaded, 16)
            sp.wait_ge(loaded, LOADS)

            def parts_out(m, i):
                for p in range(2):
                    sp.wait_ge(part3_ready, m + p + 1)
                    sp.dma_start(split_dram[p], SPLIT[p][:, :, :, :]).then_inc(to_dram[p], 16)
                for p in range(2):
                    wait_apart(sp, to_dram[p], 32 * i + 16, passed)

            def stacks_in(p, b):
                for stack, place, qk, parts in ((stack_q(p, b), p, 0, Q_PARTS), (stack_k(p, b), 1 - p, 1, K_PARTS)):
                    for k, part in enumerate(parts):
                        sp.dma_start(stack[DH * k:DH * (k + 1), :, :],
                                     split_dram[place][:, qk, part, :].rearrange("(h d) n -> d h n", h=HEADS))\
                          .then_inc(stacked[p], 16)

            def maxima_round(p, n, i, b):
                sp.wait_ge(m_steps, n * 4 + 4)
                sp.dma_start(max_dram[p], MS[p][:, :, :]).then_inc(to_dram[p], 16)
                sp.wait_ge(to_dram[p], 32 * i + 32)
                sp.dma_start(stack_q(p, b)[ROWS:ROWS + PARTS, :, :], max_dram[p].rearrange("h j n -> j h n"))\
                  .then_inc(max_in[p], 16)

            parts_out(0, 0)
            stacks_in(0, 0)
            stacks_in(1, 0)
            maxima_round(0, 0, 0, 0)
            for n, i, b, more in twins(sp):
                maxima_round(1, n + 1, i, b)
                if more:
                    parts_out(n + 2, i + 1)
                    wait_apart(sp, s2_ready, (n + 1) * ROUNDS, passed)
                    stacks_in(0, 1 - b)
                    stacks_in(1, 1 - b)
                    maxima_round(0, n + 2, i + 1, 1 - b)

        @block.gpsimd
        def _(pool):
            for p in range(2):
                pool.memset(V[p][:, :, :, :], 0.0).then_inc(zeroed, 1)
            for p in range(2):
                pool.wait_ge(zeroed, 1 + p)
                pool.memset(V[p][:, :, :, DH:VW], 1.0).then_inc(ones_set, 1)

            def normalise(n, i):
                for p in range(2):
                    pool.tensor_copy(X[p][:, :, :], H[:, bass.ds(i + PAIRS * p, 1), :]
                                     .rearrange("p o (c d) -> p (o c) d", c=CH)).then_inc(x_ready, 1)
                for p in range(2):
                    ln_power(pool, ln, minus_half, n + p, p)
                for p in range(2):
                    wait_apart(pool, ln["rstd_done"], n + p + 1, passed)
                    ln_scale(pool, ln, XN[p], X[p], p).then_inc(xn_ready, 1)

            def place_values(p, n):
                wait_apart(pool, v_ready, n + 2, passed)
                pool.tensor_copy(V[p][:, :, :, 0:DH], VT[p][:, :].rearrange("p (c h d) -> p c h d", c=CH, h=HEADS))\
                    .then_inc(v_placed, 1)

            pool.wait_ge(ones_set, 5)
            normalise(0, 0)
            place_values(1, 0)
            place_values(0, 0)
            for n, i, b, more in twins(pool):
                if more:
                    normalise(n + 2, i + 1)
                    wait_apart(pool, pv_done, (n + 1) * ROUNDS, passed)
                    place_values(1, n + 2)
                    wait_apart(pool, pv_done, (n + 2) * ROUNDS, passed)
                    place_values(0, n + 2)

        @block.scalar
        def _(act):
            act.wait_ge(ones_set, 5)
            act.activation(RD[:, 0, 0, 0:1], ident[:, 0:1], ACT.Exp)

            def copy_rows(p, n):
                act.wait_ge(xnT_ready, n + p + 1)
                act.activation(XT[p][:, :], S1[:, 1 - p, :], ACT.Copy).then_inc(xt_ready, 1)

            def first_part(p, n):
                act.wait_ge(qk_ps, n + p + 1)
                act.activation(SPLIT[p][:, :, 0, :], S1[:, :, :], ACT.Copy).then_inc(part1_ready, 1)

            def second_part(p, n):
                act.wait_ge(rest_ready, n + p + 1)
                act.activation(SPLIT[p][:, :, 1, :], R1[p][:, :, :], ACT.Copy).then_inc(part2_ready, 1)

            def copy_values(n):
                act.wait_ge(v_ps, n + 2)
                for p in range(2):
                    act.activation(VT[p][:, :], S1[:, p, :], ACT.Copy).then_inc(v_ready, 1)

            def copy_maxima(p, n):
                act.wait_ge(nmT_ready, n + 1)
                act.activation(MF[:, :], S1[0:HEADS, 0, :], ACT.Copy).then_inc(mf_ready, 1)
                act.wait_ge(mf_ready, n + 1)
                act.activation(MS[p][:, 0, :], MF[:, :], ACT.Copy).then_inc(m_steps, 1)

            def second_part_of_maxima(p, n):
                act.wait_ge(m_steps, n * 4 + 2)
                act.activation(MS[p][:, 1, :], MR[:, :], ACT.Copy).then_inc(m_steps, 1)

            def exponentials(n, r):
                act.wait_ge(s2_ready, n * ROUNDS + r + 1)
                if r >= 2:
                    act.wait_ge(pv_done, n * ROUNDS + r - 1)
                act.activation(PT[r % 2][:, :, :], S2[r % 2][:, :, :], ACT.Exp, scale=SCALE).then_inc(pt_ready, 1)

            def copy_output(n):
                act.wait_ge(pv_done, n * ROUNDS + ROUNDS)
                act.activation(OS[:, :, :], O[:, :, :], ACT.Copy).then_inc(os_ready, 1)

            for p in range(2):
                copy_rows(p, 0)
            for p in range(2):
                first_part(p, 0)
                second_part(p, 0)
            copy_values(0)
            copy_maxima(0, 0)
            second_part_of_maxima(0, 0)
            for n, i, b, more in twins(act):
                for r in range(ROUNDS):
                    exponentials(n, r)
                    if r == TURN:
                        copy_maxima(1, n + 1)
                        if more:
                            copy_rows(0, n + 2)
                    if r == TURN + 1:
                        second_part_of_maxima(1, n + 1)
                        if more:
                            copy_rows(1, n + 2)
                    if r == TURN + 2 and more:
                        first_part(0, n + 2)
                    if r == TURN + 3 and more:
                        second_part(0, n + 2)
                        first_part(1, n + 2)
                copy_output(n)
                if more:
                    second_part(1, n + 2)
                    copy_values(n + 2)
                for r in range(ROUNDS):
                    exponentials(n + 1, r)
                if more:
                    copy_maxima(0, n + 2)
                copy_output(n + 1)
                if more:
                    second_part_of_maxima(0, n + 2)

        @block.vector
        def _(dve):
            for tile in (KS_A, KS_B[0], KS_B[1]):
                dve.memset(tile[ROWS:ROWS + PARTS, :, :], 1.0).then_inc(ones_set, 1)
            dve.sem_inc(ao_ready, 1)

            def measure(n):
                for p in range(2):
                    wait_apart(dve, x_ready, n + p + 1, passed)
                    ln_measure(dve, ln, X[p], n + p, p)

            def rests(n):
                for p in range(2):
                    dve.wait_ge(part1_ready, n + p + 1)
                    dve.tensor_tensor(R1[p][:, :, :], S1[:, :, :], SPLIT[p][:, :, 0, :], ALU.subtract)\
                       .then_inc(rest_ready, 1)
                for p in range(2):
                    dve.wait_ge(part2_ready, n + p + 1)
                    dve.tensor_tensor(SPLIT[p][:, :, 2, :], R1[p][:, :, :], SPLIT[p][:, :, 1, :], ALU.subtract)\
                       .then_inc(part3_ready, 1)

            def maxima(p, n):
                for r, (c, g, k) in enumerate(tiles):
                    h = g * STRIPS + k
                    dve.wait_ge(s1_ready, n * TILES + r + 1)
                    dve.tensor_reduce(NM[p][:, c, h:h + 1], S1[:, r % 2, :], AX_X, ALU.max, negate=True)\
                       .then_inc(s1_read, 1)

            def split_maxima(p, n):
                dve.wait_ge(m_steps, n * 4 + 1)
                dve.tensor_tensor(MR[:, :], MF[:, :], MS[p][:, 0, :], ALU.subtract).then_inc(m_steps, 1)
                dve.wait_ge(m_steps, n * 4 + 3)
                dve.tensor_tensor(MS[p][:, 2, :], MR[:, :], MS[p][:, 1, :], ALU.subtract).then_inc(m_steps, 1)

            def finish(p, n, place):
                dve.wait_ge(oT_ready, n + 1)
                for g in range(GROUPS):
                    sums = S1[:, g, :].rearrange("p (c i v) -> p c i v", c=CH, i=STRIPS)
                    last = dve.reciprocal(RD[:, g, :, :], sums[:, :, :, DH])
                last.then_inc(rd_ready, 1)
                dve.wait_ge(rd_ready, n + 1)
                for g in range(GROUPS):
                    o = S1[:, g, :].rearrange("p (c i v) -> p c i v", c=CH, i=STRIPS)
                    out = AO[p][:, :, :].rearrange("p c (d h) -> p c h d", h=HEADS)[:, :, g * STRIPS:(g + 1) * STRIPS, :]
                    last = dve.tensor_tensor(out, o[:, :, :, 0:DH],
                                             RD[:, g, :, :].unsqueeze(3).broadcast_to([P, CH, STRIPS, DH]), ALU.mult)
                last.then_inc(ao_ready, 1)
                dve.wait_ge(ao_ready, n + 2)
                h = H[:, bass.ds(place, 1), :]
                dve.tensor_tensor(h, h, AO[p][:, :, :].rearrange("p c d -> p (c d)").unsqueeze(1), ALU.add)

            measure(0)
            rests(0)
            maxima(0, 0)
            split_maxima(0, 0)
            for n, i, b, more in twins(dve):
                if more:
                    measure(n + 2)
                maxima(1, n + 1)
                split_maxima(1, n + 1)
                if more:
                    rests(n + 2)
                finish(0, n, i)
                if more:
                    maxima(0, n + 2)
                    split_maxima(0, n + 2)
                finish(1, n + 1, i + PAIRS)

        @block.tensor
        def _(pe):
            pe.wait_ge(loaded, LOADS)

            def turn_rows(p, n):
                pe.wait_ge(xn_ready, n + p + 1)
                for c in range(CH):
                    last = pe.transpose(S1[:, 1 - p, chunk(c)], XN[p][:, c, :], ident)
                last.then_inc(xnT_ready, 1)

            def queries_and_keys(p, n):
                pe.wait_ge(xt_ready, n + 2)
                if p:
                    pe.wait_ge(rest_ready, n + 1)
                pe.matmul(S1[:, 0, :], wq[:, :], XT[p][:, :], start=True, stop=True)
                pe.matmul(S1[:, 1, :], wk[:, :], XT[p][:, :], start=True, stop=True).then_inc(qk_ps, 1)

            def values_of_both(n):
                pe.wait_ge(rest_ready, n + 2)
                for p in range(2):
                    for c in range(CH):
                        last = pe.matmul(S1[:, p, chunk(c)], XT[p][:, chunk(c)], wv[:, :], start=(c == 0),
                                         stop=(c == CH - 1), skip_group_check=True)
                last.then_inc(v_ps, 2)

            def score_for_max(p, n, b, r):
                c, g, k = tiles[r]
                h = g * STRIPS + k
                if r >= 2:
                    pe.wait_ge(s1_read, n * TILES + r - 1)
                pe.matmul(S1[:, r % 2, :], stack_q(p, b)[0:ROWS, h, chunk(c)], stack_k(p, b)[0:ROWS, h, :],
                          start=True, stop=True).then_inc(s1_ready, 1)

            def turn_maxima(p, n):
                pe.wait_ge(s1_read, (n + 1) * TILES)
                for c in range(CH):
                    last = pe.transpose(S1[0:HEADS, 0, chunk(c)], NM[p][:, c, :], ident)
                last.then_inc(nmT_ready, 1)

            def scores(p, n, b, r):
                for j in range(2):
                    c, g, k = tiles[2 * r + j]
                    h = g * STRIPS + k
                    last = pe.matmul(S2[r % 2][:, j, :], stack_k(p, b)[0:ROWS + PARTS, h, chunk(c)],
                                     stack_q(p, b)[0:ROWS + PARTS, h, :], start=True, stop=True)
                last.then_inc(s2_ready, 1)

            def values(p, n, r, j):
                c, g, k = tiles[2 * r + j]
                if j == 0:
                    pe.wait_ge(pt_ready, n * ROUNDS + r + 1)
                ins = pe.matmul(O[32 * k:32 * k + 32, g, :], V[1 - p][:, c, g * STRIPS + k, :], PT[r % 2][:, j, :],
                                start=(c == 0), stop=(c == CH - 1), skip_group_check=True)
                if j == 1:
                    ins.then_inc(pv_done, 1)

            def turn_output(n):
                pe.wait_ge(os_ready, n + 1)
                for g in range(GROUPS):
                    for c in range(CH):
                        last = pe.transpose(S1[:, g, chunk(c)], OS[:, g, chunk(c)], ident)
                last.then_inc(oT_ready, 1)

            for p in range(2):
                turn_rows(p, 0)
            for p in range(2):
                queries_and_keys(p, 0)
            values_of_both(0)
            pe.wait_ge(v_ready, 2)
            pe.wait_ge(stacked[0], STACKED)
            for r in range(TILES):
                score_for_max(0, 0, 0, r)
            turn_maxima(0, 0)
            pe.wait_ge(mf_ready, 1)
            for n, i, b, more in twins(pe):
                pe.wait_ge(stacked[1], i * STACKED + STACKED)
                pe.wait_ge(max_in[0], i * 16 + 16)
                pe.wait_ge(v_placed, n + 1)
                pe.wait_ge(ao_ready, n + 1)
                for r in range(ROUNDS):
                    if 3 * r < TILES:
                        score_for_max(1, n + 1, b, 3 * r)
                    scores(0, n, b, r)
                    for j in range(2):
                        if 3 * r + 1 + j < TILES:
                            score_for_max(1, n + 1, b, 3 * r + 1 + j)
                        if r:
                            values(0, n, r - 1, j)
                    if r == TURN:
                        turn_maxima(1, n + 1)
                        if more:
                            turn_rows(0, n + 2)
                    if r == TURN + 1:
                        pe.wait_ge(mf_ready, n + 2)
                        if more:
                            turn_rows(1, n + 2)
                    if r == TURN + 2 and more:
                        queries_and_keys(0, n + 2)
                    if r == TURN + 3 and more:
                        queries_and_keys(1, n + 2)
                    if r == TURN + 4 and more:
                        values_of_both(n + 2)
                for j in range(2):
                    values(0, n, ROUNDS - 1, j)
                pe.wait_ge(max_in[1], i * 16 + 16)
                pe.wait_ge(v_placed, n + 2)
                for r in range(ROUNDS):
                    if r == FIRST_TILE and more:
                        pe.wait_ge(ao_ready, n + 2)
                        pe.wait_ge(stacked[0], (i + 1) * STACKED + STACKED)
                    t = 4 * (r - FIRST_TILE)
                    if 0 <= t < TILES and more:
                        score_for_max(0, n + 2, 1 - b, t)
                    scores(1, n + 1, b, r)
                    if r == 1:
                        if more:
                            pe.wait_ge(v_ready, n + 4)
                        turn_output(n)
                    if 0 <= t < TILES and more:
                        score_for_max(0, n + 2, 1 - b, t + 1)
                    for j in range(2):
                        if 0 <= t < TILES and more:
                            score_for_max(0, n + 2, 1 - b, t + 2 + j)
                        if r:
                            values(1, n + 1, r - 1, j)
                if more:
                    turn_maxima(0, n + 2)
                for j in range(2):
                    values(1, n + 1, ROUNDS - 1, j)
                if more:
                    pe.wait_ge(mf_ready, n + 3)
                else:
                    pe.wait_ge(ao_ready, n + 2)
                turn_output(n + 1)


def merged_ffn_phase(nc, a, H, out, consts):
    ident, minus_half, ones_row = consts["ident"], consts["minus_half"], consts["ones_row"]
    with ExitStack() as ctx:
        sb, ps, sem = makers(nc, ctx)
        passed = consts["passed"]
        two = lambda name, shape, dt=F32: [sb(f"f_{name}_{p}", shape, dt) for p in range(2)]
        wg1 = sb("f_wg1", [P, P])
        wg2 = sb("f_wg2", [P, TASKS])
        gb1 = sb("f_gb1", [P, 1])
        gb2 = sb("f_gb2", [1, TASKS])
        w1 = sb("f_w1", [P, FF])
        w2 = sb("f_w2", [P, FB * P])
        tw1 = sb("f_tw1", [P, TASKS, FF])
        tw2 = sb("f_tw2", [P, TASKS, FB, P])
        b1 = sb("f_b1", [P, FB])
        tb1 = sb("f_tb1", [P, FB, TASKS])
        b2 = sb("f_b2", [1, CH, P])
        tb2 = sb("f_tb2", [TASKS, CH, P])
        tln = sb("f_tln", [TASKS, 2, P])
        ln8 = sb("f_ln8", [TASKS, 2, P])
        lnp = sb("f_lnp", [P, 2, P])
        merge = sb("f_merge", [TASKS, P])
        ones = sb("f_ones", [P, P])
        X = two("x", [P, CH, P])
        XN = two("xn", [P, CH, P])
        XT = two("xt", [P, SEQ])
        GH = two("gh", [P, SEQ])
        GS = two("gs", [P, 1])
        GM = two("gm", [P, 1])
        GR = two("gr", [P, P])
        GB = two("gb", [P, TASKS])
        GC = two("gc", [TASKS, P])
        DG = two("dg", [P, TASKS, P])
        WM1 = two("wm1", [P, FF])
        WM2 = two("wm2", [P, FB * P])
        BT = two("bt", [P, FB, TASKS])
        BS = two("bs", [P, FB])
        B1 = two("b1m", [P, FB])
        F = two("hid", [P, FB, SEQ])
        B = [ps(f"f_ps{p}", [P, 4, 512]) for p in range(2)]

        ln, ln_out = layer_norm(sb, sem, "f_ln", passed), layer_norm(sb, sem, "f_lno", passed)
        loaded = sem("f_loaded")
        set_ = sem("f_set")
        tln_ready = sem("f_tln_ready")
        lnp_ps = sem("f_lnp_ps")
        lnp_ready = sem("f_lnp_ready")
        stored = [sem(f"f_stored{p}") for p in range(2)]
        x_ready = sem("f_x_ready")
        xn_ready = sem("f_xn_ready")
        xnT_ready = sem("f_xnT_ready")
        xt_ready = sem("f_xt_ready")
        gh_ps = sem("f_gh_ps")
        gs_ready = sem("f_gs_ready")
        gm_ready = sem("f_gm_ready")
        gr_ready = sem("f_gr_ready")
        g_ps = sem("f_g_ps")
        gb_ready = sem("f_gb_ready")
        gc_ready = sem("f_gc_ready")
        dg_ready = sem("f_dg_ready")
        w1_ps = sem("f_w1_ps")
        wm1_ready = sem("f_wm1_ready")
        wm2_steps = sem("f_wm2_steps")
        b1_steps = sem("f_b1_steps")
        hid_ready = sem("f_hid_ready")
        relu_act = sem("f_relu_act")
        relu_dve = sem("f_relu_dve")
        y_ready = sem("f_y_ready")
        r_ready = sem("f_r_ready")
        nr_ready = sem("f_nr_ready")
        gain_done = sem("f_gain_done")
        xb_ready = sem("f_xb_ready")
        out_ready = sem("f_out_ready")
        LOADS = 16 * 16

        block = ctx.enter_context(nc.Block())

        @block.sync
        def _(sp):
            row = lambda name: a[name].rearrange("(o d) -> o d", o=1)
            for tile, src in (
                (wg1[:, :], a["L1_ffn_gfc1_w"]),
                (wg2[:, :], a["L1_ffn_gfc2_w"]),
                (gb1[:, :], a["L1_ffn_gfc1_b"].rearrange("(d o) -> d o", o=1)),
                (gb2[:, :], row("L1_ffn_gfc2_b")),
                (tln[:, 0, :], a["L1_ffn_tv_ln_g"]),
                (tln[:, 1, :], a["L1_ffn_tv_ln_b"]),
                (ln8[:, 0, :], row("L1_ffn_ln_g").broadcast_to([TASKS, P])),
                (ln8[:, 1, :], row("L1_ffn_ln_b").broadcast_to([TASKS, P])),
                (lnp[:, 0, :], row("L1_ffn_ln_g").broadcast_to([P, P])),
                (lnp[:, 1, :], row("L1_ffn_ln_b").broadcast_to([P, P])),
                (tw1[:, :, :], a["L1_ffn_tv_W1"].rearrange("e d f -> d e f")),
                (w1[:, :], a["L1_ffn_W1"]),
                (b1[:, :], a["L1_ffn_b1"]),
                (tb1[:, :, :], a["L1_ffn_tv_b1"]),
                (b2[:, :, :], a["L1_ffn_b2"].rearrange("(o c d) -> o c d", o=1, c=1).broadcast_to([1, CH, P])),
                (tb2[:, :, :], a["L1_ffn_tv_b2"].unsqueeze(1).broadcast_to([TASKS, CH, P])),
            ):
                sp.dma_start(tile, src).then_inc(loaded, 16)
            for ns in pairs(sp):
                for p, n in enumerate(ns):
                    sp.wait_ge(out_ready, n + 1)
                    sp.dma_start(out[bass.ds(n, 1), :, :].rearrange("o (c p) d -> p (o c) d", p=P), XN[p][:, :, :])\
                      .then_inc(stored[p], 16)
            for p in range(2):
                sp.wait_ge(stored[p], SEQS * 8 + 16)

        @block.gpsimd
        def _(pool):
            pool.memset(ones[:, :], 1.0).then_inc(set_, 1)
            pool.memset(merge[:, :], MERGE).then_inc(set_, 1)
            pool.wait_ge(lnp_ready, 1)
            for ns in pairs(pool):
                for p, n in enumerate(ns):
                    ln_power(pool, ln, minus_half, n, p)
                for p, n in enumerate(ns):
                    pool.wait_ge(xn_ready, n + 1)
                    pool.tensor_tensor(X[p][:, :, :], X[p][:, :, :],
                                       lnp[:, 1, :].unsqueeze(1).broadcast_to([P, CH, P]), ALU.add)\
                        .then_inc(xb_ready, 1)
                for p, n in enumerate(ns):
                    ln_power(pool, ln_out, minus_half, n, p)

        @block.scalar
        def _(act):
            act.dma_start(tw2[:, :, :, :], a["L1_ffn_tv_W2"].rearrange("e (b p) d -> p e b d", p=P))\
               .then_inc(loaded, 16)
            act.dma_start(w2[:, :].rearrange("p (b d) -> p b d", b=FB), a["L1_ffn_W2"].rearrange("(b p) d -> p b d", p=P))\
               .then_inc(loaded, 16)
            act.wait_ge(loaded, LOADS + 32)
            for ns in pairs(act):
                for p, n in enumerate(ns):
                    act.wait_ge(xnT_ready, n + 1)
                    act.activation(XT[p][:, :], B[p][:, 0, :], ACT.Copy).then_inc(xt_ready, 1)
                for p, n in enumerate(ns):
                    act.wait_ge(gh_ps, n + 1)
                    act.activation(GH[p][:, :], B[p][:, 1, :], ACT.Relu, bias=gb1[:, :], accum_out=GS[p][:, :])\
                       .then_inc(gs_ready, 1)
                for p, n in enumerate(ns):
                    act.wait_ge(g_ps, n + 1)
                    act.activation(GB[p][:, :], B[p][:, 1, 0:TASKS], ACT.Copy).then_inc(gb_ready, 1)
                    act.activation(GC[p][:, :], B[p][0:TASKS, 1, P:2 * P], ACT.Copy).then_inc(gc_ready, 1)
                for p, n in enumerate(ns):
                    act.wait_ge(gb_ready, n + 1)
                    for e in range(TASKS):
                        last = act.activation(DG[p][:, e, :], ident, ACT.Copy, scale=GB[p][:, e:e + 1])
                    last.then_inc(dg_ready, 1)
                for p, n in enumerate(ns):
                    act.wait_ge(b1_steps, n * 3 + 3)
                    for fb in range(0, FB, 2):
                        act.wait_ge(hid_ready, n * FB + fb + 1)
                        act.activation(F[p][:, fb, :], B[p][:, fb, :], ACT.Relu, bias=B1[p][:, fb:fb + 1])\
                           .then_inc(relu_act, 1)

        @block.vector
        def _(dve):
            for p in range(2):
                dve.sem_inc(stored[p], 16)
            dve.wait_ge(loaded, LOADS + 32)
            dve.wait_ge(set_, 2)
            dve.tensor_tensor(tln[:, :, :], tln[:, :, :], ln8[:, :, :], ALU.subtract).then_inc(tln_ready, 1)
            dve.wait_ge(lnp_ps, 1)
            dve.tensor_tensor(lnp[:, :, :], lnp[:, :, :], B[0][:, 0, 0:2 * P].rearrange("p (o d) -> p o d", o=2), ALU.add)\
               .then_inc(lnp_ready, 1)
            dve.wait_ge(lnp_ready, 1)
            for ns in pairs(dve):
                for p, n in enumerate(ns):
                    x = H[:, bass.ds(n, 1), :].rearrange("p o (c d) -> p (o c) d", c=CH)
                    dve.tensor_copy(X[p][:, :, :], x).then_inc(x_ready, 1)
                    dve.wait_ge(x_ready, n + 1)
                    ln_measure(dve, ln, X[p], n, p)
                for p, n in enumerate(ns):
                    wait_apart(dve, stored[p], ns[0] * 8 + 16, passed)
                    ln_normalise(dve, ln, XN[p], X[p], n, p).then_inc(xn_ready, 1)
                for p, n in enumerate(ns):
                    dve.wait_ge(gs_ready, n + 1)
                    dve.tensor_scalar(GM[p][:, :], GS[p][:, :], 1.0 / SEQ, None, ALU.mult).then_inc(gm_ready, 1)
                    dve.wait_ge(gm_ready, n + 1)
                    dve.tensor_scalar(GR[p][:, :], ones[:, :], GM[p][:, :], None, ALU.mult).then_inc(gr_ready, 1)
                for p, n in enumerate(ns):
                    dve.wait_ge(gb_ready, n + 1)
                    dve.tensor_tensor(BT[p][:, :, :], tb1[:, :, :], GB[p][:, :].unsqueeze(1).broadcast_to([P, FB, TASKS]),
                                      ALU.mult).then_inc(b1_steps, 1)
                    dve.wait_ge(b1_steps, n * 3 + 1)
                    dve.tensor_reduce(BS[p][:, :], BT[p][:, :, :], AX_X, ALU.add).then_inc(b1_steps, 1)
                    dve.wait_ge(b1_steps, n * 3 + 2)
                    dve.tensor_tensor(B1[p][:, :], BS[p][:, :], b1[:, :], ALU.add).then_inc(b1_steps, 1)
                    for e in range(TASKS):
                        if e:
                            dve.wait_ge(wm2_steps, n * TASKS + e)
                        dve.scalar_tensor_tensor(
                            out=WM2[p][:, :], in0=tw2[:, e, :, :].rearrange("p b d -> p (b d)"), scalar=GB[p][:, e:e + 1],
                            in1=WM2[p][:, :] if e else w2[:, :], op0=ALU.mult, op1=ALU.add).then_inc(wm2_steps, 1)
                for p, n in enumerate(ns):
                    dve.wait_ge(w1_ps, n + 1)
                    dve.tensor_tensor(WM1[p][:, :], w1[:, :], B[p][:, 2, :], ALU.add).then_inc(wm1_ready, 1)
                for p, n in enumerate(ns):
                    dve.wait_ge(b1_steps, n * 3 + 3)
                    for fb in range(1, FB, 2):
                        dve.wait_ge(hid_ready, n * FB + fb + 1)
                        dve.tensor_scalar(F[p][:, fb, :], B[p][:, fb, :], B1[p][:, fb:fb + 1], 0.0, ALU.add, ALU.max)\
                           .then_inc(relu_dve, 1)
                for p, n in enumerate(ns):
                    dve.wait_ge(y_ready, n + 1)
                    dve.tensor_tensor(XN[p][:, :, :], XN[p][:, :, :],
                                      B[p][:, 0, :].rearrange("p (c d) -> p c d", c=CH), ALU.add)\
                       .then_inc(r_ready, 1)
                    dve.wait_ge(r_ready, n + 1)
                    ln_measure(dve, ln_out, XN[p], n, p)
                for p, n in enumerate(ns):
                    ln_normalise(dve, ln_out, XN[p], XN[p], n, p).then_inc(nr_ready, 1)
                    dve.wait_ge(nr_ready, n + 1)
                    dve.tensor_tensor(XN[p][:, :, :], XN[p][:, :, :],
                                      lnp[:, 0, :].unsqueeze(1).broadcast_to([P, CH, P]), ALU.mult)\
                       .then_inc(gain_done, 1)
                    dve.wait_ge(gain_done, n + 1)
                    dve.wait_ge(xb_ready, n + 1)
                    dve.tensor_tensor(XN[p][:, :, :], XN[p][:, :, :], X[p][:, :, :], ALU.add).then_inc(out_ready, 1)

        @block.tensor
        def _(pe):
            pe.wait_ge(tln_ready, 1)
            for j in range(2):
                last = pe.matmul(B[0][:, 0, chunk(j)], merge[:, :], tln[:, j, :], start=(j == 0), stop=(j == 1),
                                 skip_group_check=True)
            last.then_inc(lnp_ps, 1)
            pe.wait_ge(lnp_ready, 1)
            for ns in pairs(pe):
                for p, n in enumerate(ns):
                    pe.wait_ge(xn_ready, n + 1)
                    for c in range(CH):
                        last = pe.transpose(B[p][:, 0, chunk(c)], XN[p][:, c, :], ident)
                    last.then_inc(xnT_ready, 1)
                for p, n in enumerate(ns):
                    pe.wait_ge(xt_ready, n + 1)
                    pe.matmul(B[p][:, 1, :], wg1[:, :], XT[p][:, :], start=True, stop=True).then_inc(gh_ps, 1)
                for p, n in enumerate(ns):
                    pe.wait_ge(gr_ready, n + 1)
                    pe.matmul(B[p][:, 1, 0:TASKS], GR[p][:, :], wg2[:, :], start=True, stop=False, skip_group_check=True)
                    pe.matmul(B[p][:, 1, 0:TASKS], ones_row, gb2[:, :], start=False, stop=True, skip_group_check=True)
                    pe.matmul(B[p][0:TASKS, 1, P:2 * P], wg2[:, :], GR[p][:, :], start=False, stop=False,
                              skip_group_check=True)
                    pe.matmul(B[p][0:TASKS, 1, P:2 * P], gb2[:, :], ones_row, start=False, stop=True,
                              skip_group_check=True).then_inc(g_ps, 1)
                for p, n in enumerate(ns):
                    pe.wait_ge(dg_ready, n + 1)
                    for e in range(TASKS):
                        last = pe.matmul(B[p][:, 2, :], DG[p][:, e, :], tw1[:, e, :], start=(e == 0),
                                         stop=(e == TASKS - 1))
                    last.then_inc(w1_ps, 1)
                for p, n in enumerate(ns):
                    pe.wait_ge(wm1_ready, n + 1)
                    pe.wait_ge(gc_ready, n + 1)
                    for fb in range(FB):
                        pe.matmul(B[p][:, fb, :], WM1[p][:, chunk(fb)], XT[p][:, :], start=True, stop=True)\
                          .then_inc(hid_ready, 1)
                for p, n in enumerate(ns):
                    pe.wait_ge(relu_act, n * FB // 2 + FB // 2)
                    pe.wait_ge(relu_dve, n * FB // 2 + FB // 2)
                    pe.wait_ge(wm2_steps, n * TASKS + TASKS)
                    pe.matmul(B[p][:, 0, :], ones_row, b2[:, :, :].rearrange("o c d -> o (c d)"),
                              start=True, stop=False, skip_group_check=True)
                    pe.matmul(B[p][:, 0, :], GC[p][:, :], tb2[:, :, :].rearrange("o c d -> o (c d)"),
                              start=False, stop=False, skip_group_check=True)
                    for c in range(CH):
                        for fb in range(FB):
                            last = pe.matmul(B[p][:, 0, chunk(c)], F[p][:, fb, chunk(c)], WM2[p][:, chunk(fb)],
                                             start=False, stop=(c == CH - 1 and fb == FB - 1),
                                             skip_group_check=True)
                    last.then_inc(y_ready, 1)


TRANSPOSED = ("L0_ffn_gate_w", "L0_ffn_shared_gate_up", "L0_ffn_shared_down", "L0_ffn_expert_gate_up",
              "L0_ffn_expert_down", "L1_attn_q_w", "L1_attn_kv_w", "L1_ffn_gfc1_w", "L1_ffn_gfc2_w",
              "L1_ffn_W1", "L1_ffn_W2", "L1_ffn_tv_W1", "L1_ffn_tv_W2")
IN_COLUMNS = ("L0_attn_b1", "L1_ffn_b1")


def build(nc, a, out):
    with ExitStack() as ctx:
        sb, ps, sem = makers(nc, ctx)
        passed = sem("waits_passed")
        H = sb("H", [P, SEQS, SEQ])
        ident = sb("ident", [P, P])
        half = sb("minus_half", [P, CH])
        ones = sb("ones_row", [1, P])
        set_ = sem("consts_set")
        ident_done = sem("ident_done")
        with nc.Block() as block:
            @block.gpsimd
            def _(pool):
                pool.memset(ident[:, :], 0.0).then_inc(set_, 1)
                pool.memset(half[:, :], -0.5).then_inc(set_, 1)
                pool.memset(ones[:, :], 1.0).then_inc(set_, 1)
                pool.wait_ge(set_, 3)
                pool.affine_select(out=ident[:, :], in_=ident[:, :], compare_op=ALU.not_equal, fill=1.0, base=0,
                                   pattern=[[-1, P]], channel_multiplier=1).then_inc(ident_done, 1)
                pool.wait_ge(ident_done, 1)
        consts = {"ident": ident[:, :], "minus_half": half[:, :], "ones_row": ones[:, :],
                  "passed": passed}
        linear_attention_phase(nc, a, H, consts)
        expert_phase(nc, a, H, consts)
        cross_attention_phase(nc, a, H, consts)
        merged_ffn_phase(nc, a, H, out, consts)


def positions():
    pos = np.arange(1, SEQ + 1, dtype=np.float32)[:, None]
    i = np.arange(P)
    exponent = np.where(i % 2 == 0, i, i + 1).astype(np.float32) / np.float32(P)
    angle = pos / np.power(np.float32(10000.0), exponent)
    return np.where(i % 2 == 0, np.cos(angle), np.sin(angle)).astype(np.float32)


def kernel(**inputs):
    import concourse.bacc as bacc
    from concourse.bass_utils import run_bass_kernel_spmd as run

    nc = bacc.Bacc("TRN2", target_bir_lowering=False, num_devices=1)
    given = {k: np.asarray(v) for k, v in inputs.items()}
    x = given.pop("x")
    arrays = {"ids": x.reshape(SEQS * CH, P).T, "table": given.pop("L0_tok_W").T, "pos": positions()}
    for name in TRANSPOSED:
        w = given.pop(name)
        arrays[name] = w.swapaxes(-1, -2)
    for name in IN_COLUMNS:
        arrays[name] = given.pop(name).reshape(-1, P).T
    arrays["L1_ffn_tv_b1"] = given.pop("L1_ffn_tv_b1").reshape(TASKS, FB, P).T
    arrays.update(given)
    arrays = {f"in_{k}": np.ascontiguousarray(v) for k, v in arrays.items()}
    a = {k[3:]: nc.dram_tensor(k, v.shape, mybir.dt.from_np(v.dtype), kind="ExternalInput").ap()
         for k, v in arrays.items()}
    out = nc.dram_tensor("out_0", (SEQS, SEQ, P), F32, kind="ExternalOutput").ap()
    build(nc, a, out)
    r = run(nc, [arrays], core_ids=[0])
    return r.results[0]["out_0"]
```

```python
from contextlib import ExitStack

import numpy as np

import concourse.bass as bass
from concourse import mybir

F32 = mybir.dt.float32
I32 = mybir.dt.int32
BF16 = mybir.dt.bfloat16
U32 = mybir.dt.uint32
F32R = mybir.dt.float32r
ALU = mybir.AluOpType
ACT = mybir.ActivationFunctionType
AX_X = mybir.AxisListType.X

P = 128
SEQS, SEQ = 32, 512
CH = SEQ // P
HEADS, DH = 8, 16
STRIPS = 4
GROUPS = HEADS // STRIPS
VW = DH + 1
FF = 512
FB = FF // P
EXPERTS, TOP_K = 16, 3
TASKS = 8
EPS = 1e-5
DEN_MIN = 1e-6
GATE_EPS = 1e-9
MERGE = 0.03


def makers(nc, ctx):
    def sb(name, shape, dt=F32):
        return ctx.enter_context(nc.sbuf_tensor(name, shape, dt))

    def ps(name, shape):
        return ctx.enter_context(nc.psum_tensor(name, shape, F32))

    def sem(name):
        return ctx.enter_context(nc.semaphore(name))

    return sb, ps, sem


def wait_apart(engine, sem, value, passed):
    engine.wait_ge(sem, value)
    engine.sem_inc(passed, 1)


def chunk(c):
    return slice(c * P, (c + 1) * P)


def layer_norm(sb, sem, name, passed):
    return {
        "stats": [sb(f"{name}_stats{p}", [P, CH, 6]) for p in range(2)],
        "mv": [sb(f"{name}_mv{p}", [P, CH, 2]) for p in range(2)],
        "ve": [sb(f"{name}_ve{p}", [P, CH]) for p in range(2)],
        "rstd": [sb(f"{name}_rstd{p}", [P, CH]) for p in range(2)],
        "stats_done": sem(f"{name}_stats_done"),
        "mv_done": sem(f"{name}_mv_done"),
        "ve_done": sem(f"{name}_ve_done"),
        "rstd_done": sem(f"{name}_rstd_done"),
        "passed": passed,
    }


def ln_measure(dve, ln, x, n, p):
    for c in range(CH):
        last = dve.bn_stats(ln["stats"][p][:, c, :], x[:, c, :])
    last.then_inc(ln["stats_done"], 1)
    wait_apart(dve, ln["stats_done"], n + 1, ln["passed"])
    for c in range(CH):
        last = dve.bn_aggr(ln["mv"][p][:, c, :], ln["stats"][p][:, c, :])
    last.then_inc(ln["mv_done"], 1)


def ln_power(pool, ln, minus_half, n, p):
    wait_apart(pool, ln["mv_done"], n + 1, ln["passed"])
    pool.tensor_scalar(ln["ve"][p][:, :], ln["mv"][p][:, :, 1], EPS, None, ALU.add).then_inc(ln["ve_done"], 1)
    pool.wait_ge(ln["ve_done"], n + 1)
    pool.tensor_tensor(ln["rstd"][p][:, :], ln["ve"][p][:, :], minus_half, ALU.pow).then_inc(ln["rstd_done"], 1)


def ln_normalise(dve, ln, out, x, n, p):
    dve.wait_ge(ln["rstd_done"], n + 1)
    return ln_scale(dve, ln, out, x, p)


def ln_scale(engine, ln, out, x, p):
    for c in range(CH):
        last = engine.tensor_scalar(out[:, c, :], x[:, c, :], ln["mv"][p][:, c, 0:1], ln["rstd"][p][:, c:c + 1],
                                 ALU.subtract, ALU.mult)
    return last


def turns(engine):
    with engine.Fori(0, SEQS // 4 - 1) as j:
        for b in range(2):
            yield 4 * j + 2 * b, 2 * j + b, b, True, True
    yield SEQS - 4, SEQS // 2 - 2, 0, True, False
    yield SEQS - 2, SEQS // 2 - 1, 1, False, False


def linear_attention_phase(nc, a, H, consts):
    ident, minus_half, ones_row = consts["ident"], consts["minus_half"], consts["ones_row"]
    with ExitStack() as ctx:
        sb, ps, sem = makers(nc, ctx)
        passed = consts["passed"]
        two = lambda name, shape: [sb(f"a_{name}_{p}", shape) for p in range(2)]
        w4 = sb("a_w4", [P, 4, P])
        w1 = sb("a_w1", [P, FF])
        w2 = sb("a_w2", [P, FB, P])
        cols = sb("a_cols", [P, 6 + FB])
        BQ, BK, G1, B1, G2, B2, BF = range(7)
        rows = sb("a_rows", [1, 3, CH, P])
        tok_ids = sb("a_tok_ids", [P, SEQS * CH], I32)
        posb = sb("a_posb", [P, CH, P])
        tokb = sb("a_tokb", [P, P])
        causal = sb("a_causal", [P, P])
        bdiag = sb("a_bdiag", [P, HEADS * VW])

        ids = [sb(f"a_idx{p}", [P, CH], I32) for p in range(2)]
        E = two("emb", [P, CH, P])
        X0 = [two(f"x0{b}", [P, CH, P]) for b in range(2)]
        X1 = [two(f"x1{b}", [P, CH, P]) for b in range(2)]
        XN = [two(f"xn{b}", [P, CH, P]) for b in range(2)]
        HT = two("ht", [P, SEQ])
        TE = two("te", [P, SEQ])
        TK = two("tk", [P, SEQ])
        QT = two("qt", [P, SEQ])
        KT = two("kt", [P, SEQ])
        Q8 = two("q8", [P, HEADS, SEQ])
        KK = two("kk", [P, CH, P])
        V = two("v", [P, CH, HEADS, VW])
        S = two("s", [P, CH - 1, HEADS * VW])
        AT = two("at", [P, STRIPS, 4 * P])
        DN = two("dn", [P, 2, HEADS])
        RD = two("rd", [P, 2, HEADS])
        AN = two("an", [P, CH, P])
        ANT = two("ant", [P, SEQ])
        r1 = two("r1", [P, CH])
        t1 = two("t1", [P, CH])
        B = [ps(f"a_ps{p}", [P, 4, 512]) for p in range(2)]

        ln1, ln2 = layer_norm(sb, sem, "a_ln1", passed), layer_norm(sb, sem, "a_ln2", passed)
        loaded = sem("a_loaded")
        consts_set = sem("a_consts_set")
        masks_zero = sem("a_masks_zero")
        bdiag_done = sem("a_bdiag_done")
        posb_done = sem("a_posb_done")
        idx_ready = sem("a_idx_ready")
        emb_landed = [sem(f"a_emb_landed{p}") for p in range(2)]
        h_ready = sem("a_h_ready")
        x1_ready = sem("a_x1_ready")
        r1_steps = sem("a_r1_steps")
        xn_ready = sem("a_xn_ready")
        xnT_ready = sem("a_xnT_ready")
        ht_ready = sem("a_ht_ready")
        qkv_ready = sem("a_qkv_ready")
        exp_ready = sem("a_exp_ready")
        pos_ready = sem("a_pos_ready")
        qk_done = sem("a_qk_done")
        q8_ready = sem("a_q8_ready")
        v_ready = sem("a_v_ready")
        kT_ready = sem("a_kT_ready")
        kk_ready = sem("a_kk_ready")
        state_ready = sem("a_state_ready")
        s_ready = sem("a_s_ready")
        at_ready = [sem(f"a_at_ready{half}") for half in range(2)]
        mask_done = [sem(f"a_mask_done{half}") for half in range(2)]
        o_ready = [sem(f"a_o_ready{half}") for half in range(2)]
        dn_ready = [sem(f"a_dn_ready{half}") for half in range(2)]
        rd_ready = [sem(f"a_rd_ready{half}") for half in range(2)]
        an_ready = [sem(f"a_an_ready{half}") for half in range(2)]
        anT_ready = sem("a_anT_ready")
        ant_ready = sem("a_ant_ready")
        wo_ready = sem("a_wo_ready")
        x2_ready = sem("a_x2_ready")
        xn2_ready = sem("a_xn2_ready")
        xn2T_ready = sem("a_xn2T_ready")
        h2t_ready = sem("a_h2t_ready")
        hid_ready = sem("a_hid_ready")
        relu_act = sem("a_relu_act")
        relu_dve = sem("a_relu_dve")
        y_ready = sem("a_y_ready")
        x3_ready = sem("a_x3_ready")

        block = ctx.enter_context(nc.Block())

        @block.sync
        def _(sp):
            sp.dma_start(tok_ids[:, :], a["ids"]).then_inc(loaded, 16)
            sp.dma_start(tokb[:, :], a["L0_tok_b"].rearrange("(o d) -> o d", o=1).broadcast_to([P, P]))\
              .then_inc(loaded, 16)
            sp.dma_start(posb[:, :, :], a["pos"].rearrange("(c p) d -> p c d", p=P)).then_inc(loaded, 16)
            for j, name in enumerate(("L0_attn_bq", "L0_attn_bk", "L0_attn_ln1_g", "L0_attn_ln1_b",
                                      "L0_attn_ln2_g", "L0_attn_ln2_b")):
                sp.dma_start(cols[:, j:j + 1], a[name].rearrange("(d o) -> d o", o=1)).then_inc(loaded, 16)
            for j, name in enumerate(("L0_attn_Wq", "L0_attn_Wk", "L0_attn_Wv", "L0_attn_Wo")):
                sp.dma_start(w4[:, j, :], a[name]).then_inc(loaded, 16)
            sp.dma_start(w1[:, :], a["L0_attn_W1"]).then_inc(loaded, 16)
            sp.dma_start(w2[:, :, :], a["L0_attn_W2"].rearrange("(b p) d -> p b d", p=P)).then_inc(loaded, 16)
            sp.wait_ge(loaded, 16 * 19)

        @block.gpsimd
        def _(pool):
            pool.memset(causal[:, :], 1.0).then_inc(masks_zero, 1)
            pool.memset(bdiag[:, :], 1.0).then_inc(masks_zero, 1)
            pool.wait_ge(masks_zero, 2)
            pool.affine_select(out=causal[:, :], in_=causal[:, :], compare_op=ALU.is_ge, fill=0.0, base=0,
                               pattern=[[1, P]], channel_multiplier=-1).then_inc(consts_set, 1)
            heads_view = bdiag[:, :].rearrange("p (h v) -> p h v", h=HEADS)
            pool.affine_select(out=heads_view, in_=heads_view, compare_op=ALU.is_ge, fill=0.0, base=0,
                               pattern=[[-DH, HEADS], [0, VW]], channel_multiplier=1).then_inc(bdiag_done, 1)
            pool.wait_ge(bdiag_done, 1)
            pool.affine_select(out=heads_view, in_=heads_view, compare_op=ALU.is_ge, fill=0.0, base=DH - 1,
                               pattern=[[DH, HEADS], [0, VW]], channel_multiplier=-1).then_inc(bdiag_done, 1)
            pool.wait_ge(bdiag_done, 2)
            pool.wait_ge(loaded, 16 * 19)

            def gather(n0):
                for p, n in enumerate((n0, n0 + 1)):
                    pool.wait_ge(h_ready, n + 1)
                    pool.tensor_copy(ids[p][:, :], tok_ids[:, bass.ds(n * CH, CH)]).then_inc(idx_ready, 1)
                    wait_apart(pool, idx_ready, n + 1, passed)
                    for c in range(CH):
                        pool.indirect_dma_start(
                            out=E[p][:, c, :], out_offset=None, in_=a["table"],
                            in_offset=bass.IndirectOffsetOnAxis(ap=ids[p][:, c:c + 1], axis=0),
                        ).then_inc(emb_landed[p], 16)

            def first_powers(n0):
                for p, n in enumerate((n0, n0 + 1)):
                    ln_power(pool, ln1, minus_half, n, p)
                    pool.wait_ge(ln1["rstd_done"], n + 1)
                    pool.tensor_tensor(t1[p][:, :], ln1["rstd"][p][:, :], ln1["rstd"][p][:, :], ALU.mult)\
                        .then_inc(r1_steps, 1)
                    pool.wait_ge(r1_steps, n * 4 + 1)
                    pool.tensor_tensor(t1[p][:, :], t1[p][:, :], ln1["mv"][p][:, :, 1], ALU.mult)\
                        .then_inc(r1_steps, 1)
                    wait_apart(pool, r1_steps, n * 4 + 2, passed)
                    pool.tensor_scalar(t1[p][:, :], t1[p][:, :], EPS, None, ALU.add).then_inc(r1_steps, 1)
                    pool.wait_ge(r1_steps, n * 4 + 3)
                    pool.tensor_tensor(r1[p][:, :], t1[p][:, :], minus_half, ALU.pow).then_inc(r1_steps, 1)

            gather(0)
            first_powers(0)
            gather(2)
            for n0, _, b, more, two_more in turns(pool):
                if more:
                    first_powers(n0 + 2)
                if two_more:
                    gather(n0 + 4)
                for p in range(2):
                    ln_power(pool, ln2, minus_half, n0 + p, p)

        @block.scalar
        def _(act):
            for j, name in enumerate(("L0_attn_bv", "L0_attn_bo", "L0_attn_b2")):
                act.dma_start(rows[:, j, :, :],
                              a[name].rearrange("(o c d) -> o c d", o=1, c=1).broadcast_to([1, CH, P]))\
                    .then_inc(loaded, 16)
            act.dma_start(cols[:, BF:BF + FB], a["L0_attn_b1"]).then_inc(loaded, 16)
            act.wait_ge(loaded, 16 * 19)
            act.activation(TE[0][:, 0:1], cols[:, 0:1], ACT.Exp, scale=0.0)

            def normalise_again(n0, b):
                for p, n in enumerate((n0, n0 + 1)):
                    act.wait_ge(x1_ready, n + 1)
                    act.wait_ge(r1_steps, n * 4 + 4)
                    for c in range(CH):
                        last = act.activation(XN[b][p][:, c, :], X1[b][p][:, c, :], ACT.Copy, scale=r1[p][:, c:c + 1])
                    last.then_inc(xn_ready, 1)

            normalise_again(0, 0)
            for n0, _, b, more, _ in turns(act):
                ns = (n0, n0 + 1)
                for p, n in enumerate(ns):
                    act.wait_ge(xnT_ready, n + 1)
                    act.activation(HT[p][:, :], B[p][:, 0, :], ACT.Identity, bias=cols[:, B1:B1 + 1],
                                   scale=cols[:, G1:G1 + 1]).then_inc(ht_ready, 1)
                for p, n in enumerate(ns):
                    act.wait_ge(qkv_ready, n * 3 + 1)
                    act.activation(TE[p][:, :], B[p][:, 1, :], ACT.Exp, bias=cols[:, BQ:BQ + 1])\
                        .then_inc(exp_ready, 1)
                    act.wait_ge(qkv_ready, n * 3 + 2)
                    act.activation(TK[p][:, :], B[p][:, 2, :], ACT.Exp, bias=cols[:, BK:BK + 1])\
                        .then_inc(exp_ready, 1)
                    act.wait_ge(qkv_ready, n * 3 + 3)
                    act.activation(V[p][:, :, :, 0:DH],
                                   B[p][:, 3, :].rearrange("p (c h d) -> p c h d", c=CH, h=HEADS), ACT.Copy)\
                        .then_inc(v_ready, 1)
                for p, n in enumerate(ns):
                    act.wait_ge(kT_ready, n + 1)
                    act.activation(KK[p][:, :, :], B[p][:, 0, :].rearrange("p (c d) -> p c d", c=CH), ACT.Copy)\
                        .then_inc(kk_ready, 1)
                if more:
                    normalise_again(n0 + 2, 1 - b)
                for p, n in enumerate(ns):
                    act.wait_ge(anT_ready, n + 1)
                    act.activation(ANT[p][:, :], B[p][:, 1, :], ACT.Copy).then_inc(ant_ready, 1)
                for p, n in enumerate(ns):
                    act.wait_ge(xn2T_ready, n + 1)
                    act.activation(HT[p][:, :], B[p][:, 3, :], ACT.Identity, bias=cols[:, B2:B2 + 1],
                                   scale=cols[:, G2:G2 + 1]).then_inc(h2t_ready, 1)
                for p, n in enumerate(ns):
                    for fb in range(0, FB, 2):
                        act.wait_ge(hid_ready, n * FB + fb + 1)
                        act.activation(AT[p][:, fb, :], B[p][:, fb, :], ACT.Relu, bias=cols[:, BF + fb:BF + fb + 1])\
                            .then_inc(relu_act, 1)

        @block.vector
        def _(dve):
            for p in range(2):
                dve.memset(V[p][:, :, :, DH:VW], 1.0)
            dve.sem_inc(h_ready, 2)
            dve.sem_inc(x3_ready, 2)
            dve.wait_ge(loaded, 16 * 19)
            dve.tensor_tensor(posb[:, :, :], posb[:, :, :], tokb[:, :].unsqueeze(1).broadcast_to([P, CH, P]), ALU.add)\
               .then_inc(posb_done, 1)
            dve.wait_ge(posb_done, 1)
            dve.wait_ge(consts_set, 1)
            dve.wait_ge(bdiag_done, 2)

            def embed(n0, b):
                for p, n in enumerate((n0, n0 + 1)):
                    dve.wait_ge(emb_landed[p], (n0 + 1) * 8 * CH + 8 * CH)
                    dve.tensor_tensor(X0[b][p][:, :, :], E[p][:, :, :], posb[:, :, :], ALU.add)\
                       .then_inc(h_ready, 1)
                    dve.wait_ge(h_ready, n + 3)
                    ln_measure(dve, ln1, X0[b][p], n, p)

            def normalise(n0, b):
                for p, n in enumerate((n0, n0 + 1)):
                    ln_normalise(dve, ln1, X1[b][p], X0[b][p], n, p).then_inc(x1_ready, 1)

            embed(0, 0)
            normalise(0, 0)
            for n0, _, b, more, _ in turns(dve):
                ns = (n0, n0 + 1)
                for p, n in enumerate(ns):
                    for j, (out, bias) in enumerate(((QT, BQ), (KT, BK))):
                        dve.wait_ge(exp_ready, n * 2 + j + 1)
                        dve.tensor_scalar(out[p][:, :], B[p][:, 1 + j, :], cols[:, bias:bias + 1], 0.0, ALU.add, ALU.max)\
                           .then_inc(pos_ready, 1)
                    for j, (out, e) in enumerate(((QT, TE), (KT, TK))):
                        dve.wait_ge(pos_ready, n * 2 + j + 1)
                        dve.scalar_tensor_tensor(out=out[p][:, :], in0=e[p][:, :], scalar=1.0, in1=out[p][:, :],
                                                 op0=ALU.min, op1=ALU.add).then_inc(qk_done, 1)
                    dve.wait_ge(qk_done, n * 2 + 1)
                    for h in range(HEADS):
                        last = dve.tensor_scalar(Q8[p][:, h, :], QT[p][:, :], bdiag[:, h * VW:h * VW + 1], None, ALU.mult)
                    last.then_inc(q8_ready, 1)
                for p, n in enumerate(ns):
                    dve.wait_ge(state_ready, n + 1)
                    dve.tensor_tensor(
                        S[p][:, :, :], B[p][:, 1, 0:(CH - 1) * HEADS * VW].rearrange("p (c v) -> p c v", c=CH - 1),
                        bdiag[:, :].unsqueeze(1).broadcast_to([P, CH - 1, HEADS * VW]), ALU.mult)\
                       .then_inc(s_ready, 1)
                for half in range(2):
                    for p, n in enumerate(ns):
                        dve.wait_ge(at_ready[half], n + 1)
                        dve.tensor_tensor(
                            AT[p][:, :, :].rearrange("p i (k t) -> p (i k) t", k=4),
                            B[p][:, :, :].rearrange("p i (k t) -> p (i k) t", k=4),
                            causal[:, :].unsqueeze(1).broadcast_to([P, 16, P]), ALU.mult)\
                           .then_inc(mask_done[half], 1)
                    if more:
                        (embed if half == 0 else normalise)(n0 + 2, 1 - b)
                    for p, n in enumerate(ns):
                        dve.wait_ge(o_ready[half], n + 1)
                        o = B[p][:, 0, 0:2 * HEADS * VW].rearrange("p (c h v) -> p c h v", c=2, h=HEADS)
                        dve.tensor_scalar(DN[p][:, :, :], o[:, :, :, DH], DEN_MIN, None, ALU.max)\
                           .then_inc(dn_ready[half], 1)
                        dve.wait_ge(dn_ready[half], n + 1)
                        dve.reciprocal(RD[p][:, :, :], DN[p][:, :, :]).then_inc(rd_ready[half], 1)
                        dve.wait_ge(rd_ready[half], n + 1)
                        dve.tensor_tensor(
                            AN[p][:, 2 * half:2 * half + 2, :].rearrange("p c (h d) -> p c h d", h=HEADS),
                            o[:, :, :, 0:DH],
                            RD[p][:, :, :].unsqueeze(3).broadcast_to([P, 2, HEADS, DH]), ALU.mult)\
                           .then_inc(an_ready[half], 1)
                for p, n in enumerate(ns):
                    dve.wait_ge(wo_ready, n + 1)
                    dve.tensor_tensor(X1[b][p][:, :, :], X1[b][p][:, :, :],
                                      B[p][:, 2, :].rearrange("p (c d) -> p c d", c=CH), ALU.add)\
                       .then_inc(x2_ready, 1)
                    dve.wait_ge(x2_ready, n + 1)
                    ln_measure(dve, ln2, X1[b][p], n, p)
                for p, n in enumerate(ns):
                    ln_normalise(dve, ln2, XN[b][p], X1[b][p], n, p).then_inc(xn2_ready, 1)
                for p, n in enumerate(ns):
                    for fb in range(1, FB, 2):
                        dve.wait_ge(hid_ready, n * FB + fb + 1)
                        dve.tensor_scalar(AT[p][:, fb, :], B[p][:, fb, :], cols[:, BF + fb:BF + fb + 1], 0.0,
                                          ALU.add, ALU.max).then_inc(relu_dve, 1)
                for p, n in enumerate(ns):
                    dve.wait_ge(y_ready, n + 1)
                    dve.tensor_tensor(X1[b][p][:, :, :], X1[b][p][:, :, :],
                                      B[p][:, 0, :].rearrange("p (c d) -> p c d", c=CH), ALU.add)\
                       .then_inc(x3_ready, 1)
                    dve.wait_ge(x3_ready, n + 3)
                    dve.tensor_tensor(H[:, bass.ds(n, 1), :], X1[b][p][:, :, :].rearrange("p c d -> p (c d)").unsqueeze(1),
                                      X0[b][p][:, :, :].rearrange("p c d -> p (c d)").unsqueeze(1), ALU.add)

        @block.tensor
        def _(pe):
            pe.wait_ge(loaded, 16 * 19)
            for n0, _, b, more, _ in turns(pe):
                ns = (n0, n0 + 1)
                for p, n in enumerate(ns):
                    pe.wait_ge(xn_ready, n + 1)
                    pe.wait_ge(x3_ready, n + 1)
                    for c in range(CH):
                        last = pe.transpose(B[p][:, 0, chunk(c)], XN[b][p][:, c, :], ident)
                    last.then_inc(xnT_ready, 1)
                for p, n in enumerate(ns):
                    pe.wait_ge(ht_ready, n + 1)
                    for j in range(2):
                        pe.matmul(B[p][:, 1 + j, :], w4[:, j, :], HT[p][:, :], start=True, stop=True)\
                          .then_inc(qkv_ready, 1)
                    pe.matmul(B[p][:, 3, :], ones_row, rows[:, 0, :, :].rearrange("o c d -> o (c d)"),
                              start=True, stop=False, skip_group_check=True)
                    for c in range(CH):
                        last = pe.matmul(B[p][:, 3, chunk(c)], HT[p][:, chunk(c)], w4[:, 2, :], start=False,
                                         stop=(c == CH - 1), skip_group_check=True)
                    last.then_inc(qkv_ready, 1)
                for p, n in enumerate(ns):
                    pe.wait_ge(qk_done, n * 2 + 2)
                    for c in range(CH):
                        last = pe.transpose(B[p][:, 0, chunk(c)], KT[p][:, chunk(c)], ident)
                    last.then_inc(kT_ready, 1)
                for p, n in enumerate(ns):
                    pe.wait_ge(kk_ready, n + 1)
                    pe.wait_ge(v_ready, n + 1)
                    for c in range(1, CH):
                        for before in range(c):
                            last = pe.matmul(B[p][:, 1, (c - 1) * HEADS * VW:c * HEADS * VW], KK[p][:, before, :],
                                             V[p][:, before, :, :].rearrange("p h v -> p (h v)"),
                                             start=(c == 1 and before == 0), stop=(before == c - 1), skip_group_check=True)
                    last.then_inc(state_ready, 1)
                for half in range(2):
                    for p, n in enumerate(ns):
                        if half == 0:
                            pe.wait_ge(s_ready, n + 1)
                            pe.wait_ge(q8_ready, n + 1)
                        else:
                            pe.wait_ge(an_ready[0], n + 1)
                        for odd in range(2):
                            for cc in range(2):
                                c = 2 * half + cc
                                for i in range(STRIPS):
                                    last = pe.matmul(B[p][:, i, (2 * odd + cc) * P:(2 * odd + cc + 1) * P],
                                                     KT[p][:, chunk(c)], Q8[p][:, 2 * i + odd, chunk(c)],
                                                     start=True, stop=True)
                        last.then_inc(at_ready[half], 1)
                    for p, n in enumerate(ns):
                        pe.wait_ge(mask_done[half], n + 1)
                        for cc in range(2):
                            c = 2 * half + cc
                            first = cc == 0
                            if c:
                                pe.matmul(B[p][:, 0, cc * HEADS * VW:(cc + 1) * HEADS * VW], QT[p][:, chunk(c)],
                                          S[p][:, c - 1, :], start=first, stop=False, skip_group_check=True)
                                first = False
                            for h in range(HEADS):
                                i, odd = h // 2, h % 2
                                at = (cc * HEADS + h) * VW
                                last = pe.matmul(B[p][:, 0, at:at + VW],
                                                 AT[p][:, i, (2 * odd + cc) * P:(2 * odd + cc + 1) * P],
                                                 V[p][:, c, h, :], start=first, stop=True, skip_group_check=True)
                                first = False
                        last.then_inc(o_ready[half], 1)
                for p, n in enumerate(ns):
                    pe.wait_ge(an_ready[1], n + 1)
                    for c in range(CH):
                        last = pe.transpose(B[p][:, 1, chunk(c)], AN[p][:, c, :], ident)
                    last.then_inc(anT_ready, 1)
                for p, n in enumerate(ns):
                    pe.wait_ge(ant_ready, n + 1)
                    pe.matmul(B[p][:, 2, :], ones_row, rows[:, 1, :, :].rearrange("o c d -> o (c d)"),
                              start=True, stop=False, skip_group_check=True)
                    for c in range(CH):
                        last = pe.matmul(B[p][:, 2, chunk(c)], ANT[p][:, chunk(c)], w4[:, 3, :], start=False,
                                         stop=(c == CH - 1), skip_group_check=True)
                    last.then_inc(wo_ready, 1)
                for p, n in enumerate(ns):
                    pe.wait_ge(xn2_ready, n + 1)
                    for c in range(CH):
                        last = pe.transpose(B[p][:, 3, chunk(c)], XN[b][p][:, c, :], ident)
                    last.then_inc(xn2T_ready, 1)
                for p, n in enumerate(ns):
                    pe.wait_ge(h2t_ready, n + 1)
                    for fb in range(FB):
                        pe.matmul(B[p][:, fb, :], w1[:, chunk(fb)], HT[p][:, :], start=True, stop=True)\
                          .then_inc(hid_ready, 1)
                for p, n in enumerate(ns):
                    pe.wait_ge(relu_act, n * FB // 2 + FB // 2)
                    pe.wait_ge(relu_dve, n * FB // 2 + FB // 2)
                    pe.matmul(B[p][:, 0, :], ones_row, rows[:, 2, :, :].rearrange("o c d -> o (c d)"),
                              start=True, stop=False, skip_group_check=True)
                    for c in range(CH):
                        for fb in range(FB):
                            last = pe.matmul(B[p][:, 0, chunk(c)], AT[p][:, fb, chunk(c)], w2[:, fb, :],
                                             start=False, stop=(c == CH - 1 and fb == FB - 1),
                                             skip_group_check=True)
                    last.then_inc(y_ready, 1)


def expert_phase(nc, a, H, consts):
    ident, minus_half = consts["ident"], consts["minus_half"]
    UNITS = EXPERTS + 1
    STEPS = 13
    MEASURE, NORMALISE, TURN, COPY, SPLIT, LOGITS, EXP, ROUTE = 4, 8, 12, 13, 14, 14, 15, 17
    with ExitStack() as ctx:
        sb, ps, sem = makers(nc, ctx)
        passed = consts["passed"]
        two = lambda name, shape, dt=F32: [sb(f"e_{name}_{p}", shape, dt) for p in range(2)]
        wgu = sb("e_wgu", [P, UNITS, 2 * P])
        wgu_hi = sb("e_wgu_hi", [P, UNITS, 2 * P], F32R)
        wgu_lo = sb("e_wgu_lo", [P, UNITS, 2 * P], F32R)
        wdn = sb("e_wdn", [P, UNITS, P])
        wr = sb("e_wr", [P, EXPERTS])
        ebias = sb("e_bias", [P, EXPERTS])
        iota = sb("e_iota", [P, EXPERTS])
        X = two("x", [P, CH, P])
        XN = two("xn", [P, CH, P])
        XT = two("xt", [P, SEQ])
        XH = [two(f"xh{b}", [P, SEQ], F32R) for b in range(2)]
        XL = [two(f"xl{b}", [P, SEQ], F32R) for b in range(2)]
        GATE = two("gate", [P, 2 * CH, EXPERTS])
        EX = sb("e_ex", [P, 2 * CH, EXPERTS])
        AF = sb("e_af", [P, 2 * CH, EXPERTS])
        SC = sb("e_sc", [P, 2 * CH, EXPERTS])
        T8 = sb("e_t8", [P, 2 * CH, 8])
        I8 = sb("e_i8", [P, 2 * CH, 8], U32)
        IF = sb("e_if", [P, 2 * CH, 8])
        OH = sb("e_oh", [P, 2 * CH, EXPERTS, TOP_K])
        GS = sb("e_gs", [P, 2 * CH])
        ACC = two("acc", [P, CH, P])
        SIL = two("sil", [P, SEQ])
        HID = [sb(f"e_hid_{j}", [P, SEQ]) for j in range(3)]
        GP = [ps(f"e_gp{p}", [P, 512]) for p in range(2)]
        UP = [ps(f"e_up{p}", [P, 512]) for p in range(2)]
        DP = [ps(f"e_dp{p}", [P, 512]) for p in range(2)]
        TP = [ps(f"e_tp{p}", [P, 512]) for p in range(2)]

        ln = layer_norm(sb, sem, "e_ln", passed)
        loaded = sem("e_loaded")
        iota_done = sem("e_iota_done")
        w_split = sem("e_w_split")
        x_split = sem("e_x_split")
        xn_ready = sem("e_xn_ready")
        xnT_ready = sem("e_xnT_ready")
        xt_ready = sem("e_xt_ready")
        logit_ready = sem("e_logit_ready")
        ex_ready = sem("e_ex_ready")
        steps = sem("e_route_steps")
        x_ready = sem("e_x_ready")
        gu_ready = sem("e_gu_ready")
        sil_ready = sem("e_sil_ready")
        hid_ready = sem("e_hid_ready")
        dn_ready = sem("e_dn_ready")
        acc_ready = sem("e_acc_ready")
        h_ready = sem("e_h_ready")
        LOADS = 16 * 6

        block = ctx.enter_context(nc.Block())

        @block.sync
        def _(sp):
            sp.dma_start(wr[:, :], a["L0_ffn_gate_w"]).then_inc(loaded, 16)
            sp.dma_start(ebias[:, :], a["L0_ffn_expert_bias"].rearrange("(o d) -> o d", o=1)
                         .broadcast_to([P, EXPERTS])).then_inc(loaded, 16)
            sp.dma_start(wgu[:, 0, :], a["L0_ffn_shared_gate_up"]).then_inc(loaded, 16)
            sp.dma_start(wdn[:, 0, :], a["L0_ffn_shared_down"]).then_inc(loaded, 16)
            sp.dma_start(wgu[:, 1:UNITS, :], a["L0_ffn_expert_gate_up"].rearrange("e d f -> d e f"))\
              .then_inc(loaded, 16)
            sp.dma_start(wdn[:, 1:UNITS, :], a["L0_ffn_expert_down"].rearrange("e f d -> f e d"))\
              .then_inc(loaded, 16)
            sp.wait_ge(loaded, LOADS)

        @block.gpsimd
        def _(pool):
            pool.sem_inc(h_ready, 2)
            pool.iota(iota[:, :], pattern=[[1, EXPERTS]], base=0, channel_multiplier=0,
                      allow_small_or_imprecise_dtypes=True).then_inc(iota_done, 1)

            def prepare(n):
                for p in range(2):
                    pool.tensor_copy(X[p][:, :, :], H[:, bass.ds(n + p, 1), :]
                                     .rearrange("p o (c d) -> p (o c) d", c=CH)).then_inc(x_ready, 1)
                for p in range(2):
                    ln_power(pool, ln, minus_half, n + p, p)

            prepare(0)
            for n, i, b, more, _ in turns(pool):
                if more:
                    wait_apart(pool, xn_ready, n + 2, passed)
                    prepare(n + 2)
                for p in range(2):
                    wait_apart(pool, acc_ready, n * UNITS + p * UNITS + UNITS + 1, passed)
                    pool.tensor_copy(H[:, bass.ds(n + p, 1), :],
                                     ACC[p][:, :, :].rearrange("p c d -> p (c d)").unsqueeze(1)).then_inc(h_ready, 1)

        @block.scalar
        def _(act):
            def prepare(u, n):
                if u == COPY:
                    for p in range(2):
                        act.wait_ge(xnT_ready, n + p + 1)
                        act.activation(XT[p][:, :], TP[p][:, :], ACT.Copy).then_inc(xt_ready, 1)
                if u == EXP:
                    for p in range(2):
                        act.wait_ge(logit_ready, n + p + 1)
                        act.activation(EX[:, p * CH:(p + 1) * CH, :],
                                       TP[p][:, 0:CH * EXPERTS].rearrange("p (c e) -> p c e", c=CH),
                                       ACT.Exp, scale=-1.0).then_inc(ex_ready, 1)

            for u in range(2 * UNITS):
                prepare(u, 0)
            for n, i, b, more, _ in turns(act):
                for u in range(2 * UNITS):
                    act.wait_ge(gu_ready, n * UNITS + u + 1)
                    act.wait_ge(hid_ready, n * UNITS + max(u - 1, 0) + 1)
                    act.activation(SIL[u % 2][:, :], GP[u % 2][:, :], ACT.Silu).then_inc(sil_ready, 1)
                    if more:
                        prepare(u, n + 2)

        @block.vector
        def _(dve):
            dve.sem_inc(hid_ready, 1)
            dve.sem_inc(acc_ready, 1)
            dve.wait_ge(loaded, LOADS)
            dve.wait_ge(iota_done, 1)
            dve.tensor_copy(wgu_hi[:, :, :], wgu[:, :, :]).then_inc(w_split, 1)
            dve.wait_ge(w_split, 1)
            dve.tensor_tensor(wgu_lo[:, :, :], wgu[:, :, :], wgu_hi[:, :, :], ALU.subtract).then_inc(w_split, 1)

            def route(s, n, i, b):
                if s == 0:
                    wait_apart(dve, ex_ready, n + 2, passed)
                else:
                    wait_apart(dve, steps, i * STEPS + s, passed)
                if s == 0:
                    last = dve.tensor_scalar(EX[:, :, :], EX[:, :, :], 1.0, None, ALU.add)
                elif s == 1:
                    last = dve.reciprocal(AF[:, :, :], EX[:, :, :])
                elif s == 2:
                    last = dve.tensor_tensor(SC[:, :, :], AF[:, :, :],
                                             ebias[:, :].unsqueeze(1).broadcast_to([P, 2 * CH, EXPERTS]), ALU.add)
                elif s == 3:
                    for c in range(2 * CH):
                        last = dve.max(T8[:, c, :], SC[:, c, :])
                elif s == 4:
                    for c in range(2 * CH):
                        last = dve.max_index(I8[:, c, :], T8[:, c, :], SC[:, c, :])
                elif s == 5:
                    last = dve.tensor_copy(IF[:, :, :], I8[:, :, :])
                elif s == 6:
                    last = dve.tensor_tensor(
                        OH[:, :, :, :], IF[:, :, 0:TOP_K].unsqueeze(2).broadcast_to([P, 2 * CH, EXPERTS, TOP_K]),
                        iota[:, :].unsqueeze(1).unsqueeze(3).broadcast_to([P, 2 * CH, EXPERTS, TOP_K]), ALU.is_equal)
                elif s == 7:
                    last = dve.tensor_reduce(SC[:, :, :], OH[:, :, :, :], AX_X, ALU.add)
                elif s == 8:
                    last = dve.tensor_tensor(AF[:, :, :], AF[:, :, :], SC[:, :, :], ALU.mult)
                elif s == 9:
                    last = dve.tensor_reduce(GS[:, :], AF[:, :, :], AX_X, ALU.add)
                elif s == 10:
                    last = dve.tensor_scalar(GS[:, :], GS[:, :], GATE_EPS, None, ALU.add)
                elif s == 11:
                    last = dve.reciprocal(GS[:, :], GS[:, :])
                else:
                    last = dve.tensor_tensor(GATE[b][:, :, :], AF[:, :, :],
                                             GS[:, :].unsqueeze(2).broadcast_to([P, 2 * CH, EXPERTS]), ALU.mult)
                last.then_inc(steps, 1)

            def prepare(u, n, i, b):
                for p in range(2):
                    if u == MEASURE + 2 * p:
                        wait_apart(dve, x_ready, n + p + 1, passed)
                        ln_measure(dve, ln, X[p], n + p, p)
                    if u == NORMALISE + 2 * p:
                        ln_normalise(dve, ln, XN[p], X[p], n + p, p).then_inc(xn_ready, 1)
                    if u == SPLIT + p:
                        dve.wait_ge(xt_ready, n + p + 1)
                        dve.tensor_copy(XH[b][p][:, :], XT[p][:, :]).then_inc(x_split, 1)
                        dve.wait_ge(x_split, (n + p) * 2 + 1)
                        dve.tensor_tensor(XL[b][p][:, :], XT[p][:, :], XH[b][p][:, :], ALU.subtract)\
                           .then_inc(x_split, 1)
                if ROUTE <= u < ROUTE + STEPS:
                    route(u - ROUTE, n, i, b)

            def add(u, n, i, b):
                p, e = divmod(u, UNITS)
                dve.wait_ge(dn_ready, n * UNITS + u + 1 + 1)
                if e == 0:
                    wait_apart(dve, h_ready, n + p + 1, passed)
                    dve.tensor_tensor(ACC[p][:, :, :].rearrange("p c d -> p (c d)").unsqueeze(1),
                                      H[:, bass.ds(n + p, 1), :], DP[u % 2][:, :].unsqueeze(1), ALU.add)\
                       .then_inc(acc_ready, 1)
                    return
                dve.wait_ge(acc_ready, n * UNITS + u + 1)
                if u == 1:
                    wait_apart(dve, steps, i * STEPS + STEPS, passed)
                for c in range(CH):
                    last = dve.scalar_tensor_tensor(
                        out=ACC[p][:, c, :], in0=DP[u % 2][:, chunk(c)], scalar=GATE[b][:, p * CH + c, e - 1:e],
                        in1=ACC[p][:, c, :], op0=ALU.mult, op1=ALU.add)
                last.then_inc(acc_ready, 1)

            for u in range(2 * UNITS):
                prepare(u, 0, 0, 0)
            for n, i, b, more, _ in turns(dve):
                for u in range(2 * UNITS):
                    dve.wait_ge(sil_ready, n * UNITS + u + 1)
                    dve.wait_ge(dn_ready, n * UNITS + max(u - 2, 0) + 1)
                    dve.tensor_tensor(HID[u % 3][:, :], SIL[u % 2][:, :], UP[u % 2][:, :], ALU.mult)\
                       .then_inc(hid_ready, 1)
                    if u >= 2:
                        add(u - 2, n, i, b)
                    if more:
                        prepare(u, n + 2, i + 1, 1 - b)
                add(2 * UNITS - 2, n, i, b)
                add(2 * UNITS - 1, n, i, b)

        @block.tensor
        def _(pe):
            pe.sem_inc(dn_ready, 1)
            pe.wait_ge(loaded, LOADS)
            pe.wait_ge(w_split, 2)

            def prepare(u, n):
                if u == TURN:
                    for p in range(2):
                        pe.wait_ge(xn_ready, n + p + 1)
                        for c in range(CH):
                            last = pe.transpose(TP[p][:, chunk(c)], XN[p][:, c, :], ident)
                        last.then_inc(xnT_ready, 1)
                if u == LOGITS:
                    for p in range(2):
                        pe.wait_ge(xt_ready, n + p + 1)
                        for c in range(CH):
                            last = pe.matmul(TP[p][:, c * EXPERTS:(c + 1) * EXPERTS], XT[p][:, chunk(c)], wr[:, :],
                                             start=(c == 0), stop=(c == CH - 1), skip_group_check=True)
                        last.then_inc(logit_ready, 1)

            def down(u, n):
                pe.wait_ge(hid_ready, n * UNITS + u + 1 + 1)
                pe.wait_ge(acc_ready, n * UNITS + max(u - 1, 0) + 1)
                for c in range(CH):
                    last = pe.matmul(DP[u % 2][:, chunk(c)], HID[u % 3][:, chunk(c)], wdn[:, u % UNITS, :],
                                     start=(c == 0), stop=(c == CH - 1), skip_group_check=True)
                last.then_inc(dn_ready, 1)

            for u in range(2 * UNITS):
                prepare(u, 0)
            for n, i, b, more, _ in turns(pe):
                pe.wait_ge(x_split, n * 2 + 4)
                for u in range(2 * UNITS):
                    p, e = divmod(u, UNITS)
                    pe.wait_ge(hid_ready, n * UNITS + max(u - 1, 0) + 1)
                    for out, cols in ((GP, slice(0, P)), (UP, slice(P, 2 * P))):
                        for k, (w, x) in enumerate(((wgu_hi, XH), (wgu_hi, XL), (wgu_lo, XH))):
                            last = pe.matmul(out[u % 2][:, :], w[:, e, cols], x[b][p][:, :],
                                             start=(k == 0), stop=(k == 2))
                    last.then_inc(gu_ready, 1)
                    if u >= 2:
                        down(u - 2, n)
                    if more:
                        prepare(u, n + 2)
                down(2 * UNITS - 2, n)
                down(2 * UNITS - 1, n)


def cross_attention_phase(nc, a, H, consts):
    ident, minus_half = consts["ident"], consts["minus_half"]
    SCALE = float(P) ** -0.5
    TILES = CH * GROUPS * STRIPS
    ROUNDS = TILES // 2
    PARTS = 3
    Q_PARTS, K_PARTS = (0, 0, 1, 0, 2, 1), (0, 1, 0, 2, 0, 1)
    ROWS = DH * len(Q_PARTS)
    PAIRS = SEQS // 2
    TURN = 11
    FIRST_TILE = 8
    tiles = [(c, g, i) for c in range(CH) for g in range(GROUPS) for i in range(STRIPS)]
    with ExitStack() as ctx:
        sb, ps, sem = makers(nc, ctx)
        passed = consts["passed"]
        two = lambda name, shape, dt=F32: [sb(f"c_{name}_{p}", shape, dt) for p in range(2)]
        wq = sb("c_wq", [P, P])
        wk = sb("c_wk", [P, P])
        wv = sb("c_wv", [P, P])
        X = two("x", [P, CH, P])
        XN = two("xn", [P, CH, P])
        XT = two("xt", [P, SEQ])
        SPLIT = two("split", [P, 2, PARTS, SEQ], BF16)
        R1 = two("r1", [P, 2, SEQ])
        QS_A, KS_A = sb("c_qs_a", [P, HEADS, SEQ], BF16), sb("c_ks_a", [P, HEADS, SEQ], BF16)
        QS_B, KS_B = two("qs_b", [P, HEADS, SEQ], BF16), two("ks_b", [P, HEADS, SEQ], BF16)
        MF = sb("c_mf", [HEADS, SEQ])
        MR = sb("c_mr", [HEADS, SEQ])
        MS = two("ms", [HEADS, PARTS, SEQ], BF16)
        VT = two("vt", [P, SEQ])
        V = two("v", [P, CH, HEADS, 32])
        NM = two("nm", [P, CH, HEADS])
        PT = two("pt", [P, 2, SEQ])
        OS = sb("c_os", [P, GROUPS, SEQ])
        RD = sb("c_rd", [P, GROUPS, CH, STRIPS])
        AO = two("ao", [P, CH, P])
        S1 = ps("c_s1", [P, 2, 512])
        S2 = [ps(f"c_s2_{p}", [P, 2, 512]) for p in range(2)]
        O = ps("c_o", [P, GROUPS, 512])

        ln = layer_norm(sb, sem, "c_ln", passed)
        split_dram = [nc.dram_tensor(f"c_split_dram{p}", (P, 2, PARTS, SEQ), BF16).ap() for p in range(2)]
        zeroed = sem("c_zeroed")
        loaded = sem("c_loaded")
        ones_set = sem("c_ones_set")
        x_ready = sem("c_x_ready")
        xn_ready = sem("c_xn_ready")
        xnT_ready = sem("c_xnT_ready")
        xt_ready = sem("c_xt_ready")
        qk_ps = sem("c_qk_ps")
        v_ps = sem("c_v_ps")
        part1_ready = sem("c_part1_ready")
        rest_ready = sem("c_rest_ready")
        part2_ready = sem("c_part2_ready")
        part3_ready = sem("c_part3_ready")
        v_ready = sem("c_v_ready")
        v_placed = sem("c_v_placed")
        to_dram = [sem(f"c_to_dram{p}") for p in range(2)]
        stacked = [sem(f"c_stacked{p}") for p in range(2)]
        max_in = [sem(f"c_max_in{p}") for p in range(2)]
        STACKED = 16 * 2 * len(Q_PARTS)
        UNDER = 16 * PARTS
        mf_ready = sem("c_mf_ready")
        m_steps = sem("c_m_steps")
        s1_ready = sem("c_s1_ready")
        s1_read = sem("c_s1_read")
        nmT_ready = sem("c_nmT_ready")
        s2_ready = sem("c_s2_ready")
        pt_ready = sem("c_pt_ready")
        pv_done = sem("c_pv_done")
        os_ready = sem("c_os_ready")
        oT_ready = sem("c_oT_ready")
        rd_ready = sem("c_rd_ready")
        ao_ready = sem("c_ao_ready")
        LOADS = 16 * 3

        def stack_q(p, b):
            return QS_B[b] if p else QS_A

        def stack_k(p, b):
            return KS_B[b] if p else KS_A

        def twins(engine):
            with engine.Fori(0, PAIRS // 2 - 1) as j:
                for b in range(2):
                    yield 4 * j + 2 * b, 2 * j + b, b, True
            yield SEQS - 4, PAIRS - 2, 0, True
            yield SEQS - 2, PAIRS - 1, 1, False

        block = ctx.enter_context(nc.Block())

        @block.sync
        def _(sp):
            sp.dma_start(wq[:, :], a["L1_attn_q_w"]).then_inc(loaded, 16)
            sp.dma_start(wk[:, :], a["L1_attn_kv_w"][:, 0:P]).then_inc(loaded, 16)
            sp.dma_start(wv[:, :], a["L1_attn_kv_w"][:, P:2 * P]).then_inc(loaded, 16)
            sp.wait_ge(loaded, LOADS)

            def parts_out(m, i):
                for p in range(2):
                    sp.wait_ge(part3_ready, m + p + 1)
                    sp.dma_start(split_dram[p], SPLIT[p][:, :, :, :]).then_inc(to_dram[p], 16)
                for p in range(2):
                    wait_apart(sp, to_dram[p], 16 * i + 16, passed)

            def stacks_in(p, b):
                for stack, place, qk, parts in ((stack_q(p, b), p, 0, Q_PARTS), (stack_k(p, b), 1 - p, 1, K_PARTS)):
                    for k, part in enumerate(parts):
                        sp.dma_start(stack[DH * k:DH * (k + 1), :, :],
                                     split_dram[place][:, qk, part, :].rearrange("(h d) n -> d h n", h=HEADS))\
                          .then_inc(stacked[p], 16)

            def maxima_round(p, n, i, b):
                sp.wait_ge(m_steps, n * 4 + 4)
                for j in range(PARTS):
                    sp.dma_start(stack_q(p, b)[ROWS + j:ROWS + j + 1, :, :], MS[p][:, j, :]).then_inc(max_in[p], 16)

            parts_out(0, 0)
            stacks_in(0, 0)
            stacks_in(1, 0)
            maxima_round(0, 0, 0, 0)
            for n, i, b, more in twins(sp):
                maxima_round(1, n + 1, i, b)
                if more:
                    parts_out(n + 2, i + 1)
                    wait_apart(sp, s2_ready, (n + 1) * ROUNDS, passed)
                    stacks_in(0, 1 - b)
                    stacks_in(1, 1 - b)
                    maxima_round(0, n + 2, i + 1, 1 - b)

        @block.gpsimd
        def _(pool):
            for p in range(2):
                pool.memset(V[p][:, :, :, :], 0.0).then_inc(zeroed, 1)
            for p in range(2):
                pool.wait_ge(zeroed, 1 + p)
                pool.memset(V[p][:, :, :, DH:VW], 1.0).then_inc(ones_set, 1)

            def normalise(n, i):
                for p in range(2):
                    pool.tensor_copy(X[p][:, :, :], H[:, bass.ds(i + PAIRS * p, 1), :]
                                     .rearrange("p o (c d) -> p (o c) d", c=CH)).then_inc(x_ready, 1)
                for p in range(2):
                    ln_power(pool, ln, minus_half, n + p, p)
                for p in range(2):
                    wait_apart(pool, ln["rstd_done"], n + p + 1, passed)
                    ln_scale(pool, ln, XN[p], X[p], p).then_inc(xn_ready, 1)

            def place_values(p, n):
                wait_apart(pool, v_ready, n + 2, passed)
                pool.tensor_copy(V[p][:, :, :, 0:DH], VT[p][:, :].rearrange("p (c h d) -> p c h d", c=CH, h=HEADS))\
                    .then_inc(v_placed, 1)

            pool.wait_ge(ones_set, 5)
            normalise(0, 0)
            place_values(1, 0)
            place_values(0, 0)
            for n, i, b, more in twins(pool):
                if more:
                    normalise(n + 2, i + 1)
                    wait_apart(pool, pv_done, (n + 1) * ROUNDS, passed)
                    place_values(1, n + 2)
                    wait_apart(pool, pv_done, (n + 2) * ROUNDS, passed)
                    place_values(0, n + 2)

        @block.scalar
        def _(act):
            act.wait_ge(ones_set, 5)
            act.activation(RD[:, 0, 0, 0:1], ident[:, 0:1], ACT.Exp)

            def copy_rows(p, n):
                act.wait_ge(xnT_ready, n + p + 1)
                act.activation(XT[p][:, :], S1[:, 1 - p, :], ACT.Copy).then_inc(xt_ready, 1)

            def first_part(p, n):
                act.wait_ge(qk_ps, n + p + 1)
                act.activation(SPLIT[p][:, :, 0, :], S1[:, :, :], ACT.Copy).then_inc(part1_ready, 1)

            def second_part(p, n):
                act.wait_ge(rest_ready, n + p + 1)
                act.activation(SPLIT[p][:, :, 1, :], R1[p][:, :, :], ACT.Copy).then_inc(part2_ready, 1)

            def copy_values(n):
                act.wait_ge(v_ps, n + 2)
                for p in range(2):
                    act.activation(VT[p][:, :], S1[:, p, :], ACT.Copy).then_inc(v_ready, 1)

            def copy_maxima(p, n):
                act.wait_ge(nmT_ready, n + 1)
                act.activation(MF[:, :], S1[0:HEADS, 0, :], ACT.Copy).then_inc(mf_ready, 1)
                act.wait_ge(mf_ready, n + 1)
                act.activation(MS[p][:, 0, :], MF[:, :], ACT.Copy).then_inc(m_steps, 1)

            def second_part_of_maxima(p, n):
                act.wait_ge(m_steps, n * 4 + 2)
                act.activation(MS[p][:, 1, :], MR[:, :], ACT.Copy).then_inc(m_steps, 1)

            def exponentials(n, r):
                act.wait_ge(s2_ready, n * ROUNDS + r + 1)
                if r >= 2:
                    act.wait_ge(pv_done, n * ROUNDS + r - 1)
                act.activation(PT[r % 2][:, :, :], S2[r % 2][:, :, :], ACT.Exp, scale=SCALE).then_inc(pt_ready, 1)

            def copy_output(n):
                act.wait_ge(pv_done, n * ROUNDS + ROUNDS)
                act.activation(OS[:, :, :], O[:, :, :], ACT.Copy).then_inc(os_ready, 1)

            for p in range(2):
                copy_rows(p, 0)
            for p in range(2):
                first_part(p, 0)
                second_part(p, 0)
            copy_values(0)
            copy_maxima(0, 0)
            second_part_of_maxima(0, 0)
            for n, i, b, more in twins(act):
                for r in range(ROUNDS):
                    exponentials(n, r)
                    if r == TURN:
                        copy_maxima(1, n + 1)
                        if more:
                            copy_rows(0, n + 2)
                    if r == TURN + 1:
                        second_part_of_maxima(1, n + 1)
                        if more:
                            copy_rows(1, n + 2)
                    if r == TURN + 2 and more:
                        first_part(0, n + 2)
                    if r == TURN + 3 and more:
                        second_part(0, n + 2)
                        first_part(1, n + 2)
                copy_output(n)
                if more:
                    second_part(1, n + 2)
                    copy_values(n + 2)
                for r in range(ROUNDS):
                    exponentials(n + 1, r)
                if more:
                    copy_maxima(0, n + 2)
                copy_output(n + 1)
                if more:
                    second_part_of_maxima(0, n + 2)

        @block.vector
        def _(dve):
            for tile in (KS_A, KS_B[0], KS_B[1]):
                dve.memset(tile[ROWS:ROWS + PARTS, :, :], 1.0).then_inc(ones_set, 1)
            dve.sem_inc(ao_ready, 1)

            def measure(n):
                for p in range(2):
                    wait_apart(dve, x_ready, n + p + 1, passed)
                    ln_measure(dve, ln, X[p], n + p, p)

            def rests(n):
                for p in range(2):
                    dve.wait_ge(part1_ready, n + p + 1)
                    dve.tensor_tensor(R1[p][:, :, :], S1[:, :, :], SPLIT[p][:, :, 0, :], ALU.subtract)\
                       .then_inc(rest_ready, 1)
                for p in range(2):
                    dve.wait_ge(part2_ready, n + p + 1)
                    dve.tensor_tensor(SPLIT[p][:, :, 2, :], R1[p][:, :, :], SPLIT[p][:, :, 1, :], ALU.subtract)\
                       .then_inc(part3_ready, 1)

            def maxima(p, n):
                for r, (c, g, k) in enumerate(tiles):
                    h = g * STRIPS + k
                    dve.wait_ge(s1_ready, n * TILES + r + 1)
                    dve.tensor_reduce(NM[p][:, c, h:h + 1], S1[:, r % 2, :], AX_X, ALU.max, negate=True)\
                       .then_inc(s1_read, 1)

            def split_maxima(p, n):
                dve.wait_ge(m_steps, n * 4 + 1)
                dve.tensor_tensor(MR[:, :], MF[:, :], MS[p][:, 0, :], ALU.subtract).then_inc(m_steps, 1)
                dve.wait_ge(m_steps, n * 4 + 3)
                dve.tensor_tensor(MS[p][:, 2, :], MR[:, :], MS[p][:, 1, :], ALU.subtract).then_inc(m_steps, 1)

            def finish(p, n, place):
                dve.wait_ge(oT_ready, n + 1)
                for g in range(GROUPS):
                    sums = S1[:, g, :].rearrange("p (c i v) -> p c i v", c=CH, i=STRIPS)
                    last = dve.reciprocal(RD[:, g, :, :], sums[:, :, :, DH])
                last.then_inc(rd_ready, 1)
                dve.wait_ge(rd_ready, n + 1)
                for g in range(GROUPS):
                    o = S1[:, g, :].rearrange("p (c i v) -> p c i v", c=CH, i=STRIPS)
                    out = AO[p][:, :, :].rearrange("p c (d h) -> p c h d", h=HEADS)[:, :, g * STRIPS:(g + 1) * STRIPS, :]
                    last = dve.tensor_tensor(out, o[:, :, :, 0:DH],
                                             RD[:, g, :, :].unsqueeze(3).broadcast_to([P, CH, STRIPS, DH]), ALU.mult)
                last.then_inc(ao_ready, 1)
                dve.wait_ge(ao_ready, n + 2)
                h = H[:, bass.ds(place, 1), :]
                dve.tensor_tensor(h, h, AO[p][:, :, :].rearrange("p c d -> p (c d)").unsqueeze(1), ALU.add)

            measure(0)
            rests(0)
            maxima(0, 0)
            split_maxima(0, 0)
            for n, i, b, more in twins(dve):
                if more:
                    measure(n + 2)
                maxima(1, n + 1)
                split_maxima(1, n + 1)
                if more:
                    rests(n + 2)
                finish(0, n, i)
                if more:
                    maxima(0, n + 2)
                    split_maxima(0, n + 2)
                finish(1, n + 1, i + PAIRS)

        @block.tensor
        def _(pe):
            pe.wait_ge(loaded, LOADS)

            def turn_rows(p, n):
                pe.wait_ge(xn_ready, n + p + 1)
                for c in range(CH):
                    last = pe.transpose(S1[:, 1 - p, chunk(c)], XN[p][:, c, :], ident)
                last.then_inc(xnT_ready, 1)

            def queries_and_keys(p, n):
                pe.wait_ge(xt_ready, n + 2)
                if p:
                    pe.wait_ge(rest_ready, n + 1)
                pe.matmul(S1[:, 0, :], wq[:, :], XT[p][:, :], start=True, stop=True)
                pe.matmul(S1[:, 1, :], wk[:, :], XT[p][:, :], start=True, stop=True).then_inc(qk_ps, 1)

            def values_of_both(n):
                pe.wait_ge(rest_ready, n + 2)
                for p in range(2):
                    for c in range(CH):
                        last = pe.matmul(S1[:, p, chunk(c)], XT[p][:, chunk(c)], wv[:, :], start=(c == 0),
                                         stop=(c == CH - 1), skip_group_check=True)
                last.then_inc(v_ps, 2)

            def score_for_max(p, n, b, r):
                c, g, k = tiles[r]
                h = g * STRIPS + k
                if r >= 2:
                    pe.wait_ge(s1_read, n * TILES + r - 1)
                pe.matmul(S1[:, r % 2, :], stack_q(p, b)[0:ROWS, h, chunk(c)], stack_k(p, b)[0:ROWS, h, :],
                          start=True, stop=True).then_inc(s1_ready, 1)

            def turn_maxima(p, n):
                pe.wait_ge(s1_read, (n + 1) * TILES)
                for c in range(CH):
                    last = pe.transpose(S1[0:HEADS, 0, chunk(c)], NM[p][:, c, :], ident)
                last.then_inc(nmT_ready, 1)

            def scores(p, n, b, r):
                for j in range(2):
                    c, g, k = tiles[2 * r + j]
                    h = g * STRIPS + k
                    last = pe.matmul(S2[r % 2][:, j, :], stack_k(p, b)[0:ROWS + PARTS, h, chunk(c)],
                                     stack_q(p, b)[0:ROWS + PARTS, h, :], start=True, stop=True)
                last.then_inc(s2_ready, 1)

            def values(p, n, r, j):
                c, g, k = tiles[2 * r + j]
                if j == 0:
                    pe.wait_ge(pt_ready, n * ROUNDS + r + 1)
                ins = pe.matmul(O[32 * k:32 * k + 32, g, :], V[1 - p][:, c, g * STRIPS + k, :], PT[r % 2][:, j, :],
                                start=(c == 0), stop=(c == CH - 1), skip_group_check=True)
                if j == 1:
                    ins.then_inc(pv_done, 1)

            def turn_output(n):
                pe.wait_ge(os_ready, n + 1)
                for g in range(GROUPS):
                    for c in range(CH):
                        last = pe.transpose(S1[:, g, chunk(c)], OS[:, g, chunk(c)], ident)
                last.then_inc(oT_ready, 1)

            for p in range(2):
                turn_rows(p, 0)
            for p in range(2):
                queries_and_keys(p, 0)
            values_of_both(0)
            pe.wait_ge(v_ready, 2)
            pe.wait_ge(stacked[0], STACKED)
            for r in range(TILES):
                score_for_max(0, 0, 0, r)
            turn_maxima(0, 0)
            pe.wait_ge(mf_ready, 1)
            for n, i, b, more in twins(pe):
                pe.wait_ge(stacked[1], i * STACKED + STACKED)
                pe.wait_ge(max_in[0], i * UNDER + UNDER)
                pe.wait_ge(v_placed, n + 1)
                pe.wait_ge(ao_ready, n + 1)
                for r in range(ROUNDS):
                    t = 3 * r
                    if t < TILES:
                        score_for_max(1, n + 1, b, t)
                    scores(0, n, b, r)
                    for j in range(2):
                        if t + 1 + j < TILES:
                            score_for_max(1, n + 1, b, t + 1 + j)
                        if r:
                            values(0, n, r - 1, j)
                    if r == TURN:
                        turn_maxima(1, n + 1)
                        if more:
                            turn_rows(0, n + 2)
                    if r == TURN + 1:
                        pe.wait_ge(mf_ready, n + 2)
                        if more:
                            turn_rows(1, n + 2)
                    if r == TURN + 2 and more:
                        queries_and_keys(0, n + 2)
                    if r == TURN + 3 and more:
                        queries_and_keys(1, n + 2)
                    if r == TURN + 4 and more:
                        values_of_both(n + 2)
                for j in range(2):
                    values(0, n, ROUNDS - 1, j)
                pe.wait_ge(max_in[1], i * UNDER + UNDER)
                pe.wait_ge(v_placed, n + 2)
                for r in range(ROUNDS):
                    if r == FIRST_TILE and more:
                        pe.wait_ge(ao_ready, n + 2)
                        pe.wait_ge(stacked[0], (i + 1) * STACKED + STACKED)
                    t = 4 * (r - FIRST_TILE)
                    if 0 <= t < TILES and more:
                        score_for_max(0, n + 2, 1 - b, t)
                    scores(1, n + 1, b, r)
                    if r == 1:
                        if more:
                            pe.wait_ge(v_ready, n + 4)
                        turn_output(n)
                    if 0 <= t < TILES and more:
                        score_for_max(0, n + 2, 1 - b, t + 1)
                    for j in range(2):
                        if 0 <= t < TILES and more:
                            score_for_max(0, n + 2, 1 - b, t + 2 + j)
                        if r:
                            values(1, n + 1, r - 1, j)
                if more:
                    turn_maxima(0, n + 2)
                for j in range(2):
                    values(1, n + 1, ROUNDS - 1, j)
                if more:
                    pe.wait_ge(mf_ready, n + 3)
                else:
                    pe.wait_ge(ao_ready, n + 2)
                turn_output(n + 1)


def merged_ffn_phase(nc, a, H, out, consts):
    ident, minus_half, ones_row = consts["ident"], consts["minus_half"], consts["ones_row"]
    with ExitStack() as ctx:
        sb, ps, sem = makers(nc, ctx)
        passed = consts["passed"]
        two = lambda name, shape, dt=F32: [sb(f"f_{name}_{p}", shape, dt) for p in range(2)]
        wg1 = sb("f_wg1", [P, P])
        wg2 = sb("f_wg2", [P, TASKS])
        gb1 = sb("f_gb1", [P, 1])
        gb2 = sb("f_gb2", [1, TASKS])
        w1 = sb("f_w1", [P, FF])
        w2 = sb("f_w2", [P, FB * P])
        tw1 = sb("f_tw1", [P, TASKS, FF])
        tw2 = sb("f_tw2", [P, TASKS, FB, P])
        b1 = sb("f_b1", [P, FB])
        tb1 = sb("f_tb1", [P, FB, TASKS])
        b2 = sb("f_b2", [1, CH, P])
        tb2 = sb("f_tb2", [TASKS, CH, P])
        tln = sb("f_tln", [TASKS, 2, P])
        ln8 = sb("f_ln8", [TASKS, 2, P])
        lnp = sb("f_lnp", [P, 2, P])
        merge = sb("f_merge", [TASKS, P])
        ones = sb("f_ones", [P, P])
        X = [two(f"x{b}", [P, CH, P]) for b in range(2)]
        XN = [two(f"xn{b}", [P, CH, P]) for b in range(2)]
        XT = [two(f"xt{b}", [P, SEQ]) for b in range(2)]
        GH = two("gh", [P, SEQ])
        GS = two("gs", [P, 1])
        GM = two("gm", [P, 1])
        GR = two("gr", [P, P])
        GB = two("gb", [P, TASKS])
        GC = two("gc", [TASKS, P])
        DG = two("dg", [P, TASKS, P])
        WM1 = two("wm1", [P, FF])
        WM2 = two("wm2", [P, FB * P])
        BT = two("bt", [P, FB, TASKS])
        BS = two("bs", [P, FB])
        B1 = two("b1m", [P, FB])
        F = two("hid", [P, FB, SEQ])
        TURNED, GATE = 3, 1
        B = [ps(f"f_ps{p}", [P, 4, 512]) for p in range(2)]

        ln, ln_out = layer_norm(sb, sem, "f_ln", passed), layer_norm(sb, sem, "f_lno", passed)
        loaded = sem("f_loaded")
        set_ = sem("f_set")
        tln_ready = sem("f_tln_ready")
        lnp_ps = sem("f_lnp_ps")
        lnp_ready = sem("f_lnp_ready")
        stored = [sem(f"f_stored{p}") for p in range(2)]
        x_ready = sem("f_x_ready")
        xn_ready = sem("f_xn_ready")
        xnT_ready = sem("f_xnT_ready")
        xt_ready = sem("f_xt_ready")
        gh_ps = sem("f_gh_ps")
        gs_ready = sem("f_gs_ready")
        gm_ready = sem("f_gm_ready")
        gr_ready = sem("f_gr_ready")
        g_ps = sem("f_g_ps")
        gb_ready = sem("f_gb_ready")
        gc_ready = sem("f_gc_ready")
        dg_ready = sem("f_dg_ready")
        w1_ps = sem("f_w1_ps")
        wm1_ready = sem("f_wm1_ready")
        wm2_steps = sem("f_wm2_steps")
        b1_steps = sem("f_b1_steps")
        hid_ready = sem("f_hid_ready")
        relu_act = sem("f_relu_act")
        relu_dve = sem("f_relu_dve")
        y_ready = sem("f_y_ready")
        r_ready = sem("f_r_ready")
        nr_ready = sem("f_nr_ready")
        gain_done = sem("f_gain_done")
        xb_ready = sem("f_xb_ready")
        out_ready = sem("f_out_ready")
        LOADS = 16 * 16

        block = ctx.enter_context(nc.Block())

        @block.sync
        def _(sp):
            row = lambda name: a[name].rearrange("(o d) -> o d", o=1)
            for tile, src in (
                (wg1[:, :], a["L1_ffn_gfc1_w"]),
                (wg2[:, :], a["L1_ffn_gfc2_w"]),
                (gb1[:, :], a["L1_ffn_gfc1_b"].rearrange("(d o) -> d o", o=1)),
                (gb2[:, :], row("L1_ffn_gfc2_b")),
                (tln[:, 0, :], a["L1_ffn_tv_ln_g"]),
                (tln[:, 1, :], a["L1_ffn_tv_ln_b"]),
                (ln8[:, 0, :], row("L1_ffn_ln_g").broadcast_to([TASKS, P])),
                (ln8[:, 1, :], row("L1_ffn_ln_b").broadcast_to([TASKS, P])),
                (lnp[:, 0, :], row("L1_ffn_ln_g").broadcast_to([P, P])),
                (lnp[:, 1, :], row("L1_ffn_ln_b").broadcast_to([P, P])),
                (tw1[:, :, :], a["L1_ffn_tv_W1"].rearrange("e d f -> d e f")),
                (w1[:, :], a["L1_ffn_W1"]),
                (b1[:, :], a["L1_ffn_b1"]),
                (tb1[:, :, :], a["L1_ffn_tv_b1"]),
                (b2[:, :, :], a["L1_ffn_b2"].rearrange("(o c d) -> o c d", o=1, c=1).broadcast_to([1, CH, P])),
                (tb2[:, :, :], a["L1_ffn_tv_b2"].unsqueeze(1).broadcast_to([TASKS, CH, P])),
            ):
                sp.dma_start(tile, src).then_inc(loaded, 16)
            for n0, _, b, more, _ in turns(sp):
                ns = (n0, n0 + 1)
                for p, n in enumerate(ns):
                    sp.wait_ge(out_ready, n + 1)
                    sp.dma_start(out[bass.ds(n, 1), :, :].rearrange("o (c p) d -> p (o c) d", p=P), XN[b][p][:, :, :])\
                      .then_inc(stored[p], 16)
            for p in range(2):
                sp.wait_ge(stored[p], SEQS * 8 + 32)

        @block.gpsimd
        def _(pool):
            pool.memset(ones[:, :], 1.0).then_inc(set_, 1)
            pool.memset(merge[:, :], MERGE).then_inc(set_, 1)
            pool.wait_ge(lnp_ready, 1)
            for p in range(2):
                ln_power(pool, ln, minus_half, p, p)
            for n0, _, b, more, _ in turns(pool):
                ns = (n0, n0 + 1)
                for p, n in enumerate(ns):
                    pool.wait_ge(xn_ready, n + 1)
                    pool.tensor_tensor(X[b][p][:, :, :], X[b][p][:, :, :],
                                       lnp[:, 1, :].unsqueeze(1).broadcast_to([P, CH, P]), ALU.add)\
                        .then_inc(xb_ready, 1)
                if more:
                    for p in range(2):
                        ln_power(pool, ln, minus_half, n0 + 2 + p, p)
                for p, n in enumerate(ns):
                    ln_power(pool, ln_out, minus_half, n, p)

        @block.scalar
        def _(act):
            act.dma_start(tw2[:, :, :, :], a["L1_ffn_tv_W2"].rearrange("e (b p) d -> p e b d", p=P))\
               .then_inc(loaded, 16)
            act.dma_start(w2[:, :].rearrange("p (b d) -> p b d", b=FB), a["L1_ffn_W2"].rearrange("(b p) d -> p b d", p=P))\
               .then_inc(loaded, 16)
            act.wait_ge(loaded, LOADS + 32)

            def begin(n0, b):
                for p, n in enumerate((n0, n0 + 1)):
                    act.wait_ge(xnT_ready, n + 1)
                    act.activation(XT[b][p][:, :], B[p][:, TURNED, :], ACT.Copy).then_inc(xt_ready, 1)
                for p, n in enumerate((n0, n0 + 1)):
                    act.wait_ge(gh_ps, n + 1)
                    act.activation(GH[p][:, :], B[p][:, GATE, :], ACT.Relu, bias=gb1[:, :], accum_out=GS[p][:, :])\
                       .then_inc(gs_ready, 1)

            begin(0, 0)
            for n0, _, b, more, _ in turns(act):
                ns = (n0, n0 + 1)
                for p, n in enumerate(ns):
                    act.wait_ge(g_ps, n + 1)
                    act.activation(GB[p][:, :], B[p][:, GATE, 0:TASKS], ACT.Copy).then_inc(gb_ready, 1)
                    act.activation(GC[p][:, :], B[p][0:TASKS, GATE, P:2 * P], ACT.Copy).then_inc(gc_ready, 1)
                for p, n in enumerate(ns):
                    act.wait_ge(gb_ready, n + 1)
                    for e in range(TASKS):
                        last = act.activation(DG[p][:, e, :], ident, ACT.Copy, scale=GB[p][:, e:e + 1])
                    last.then_inc(dg_ready, 1)
                for p, n in enumerate(ns):
                    act.wait_ge(b1_steps, n * 3 + 3)
                    for fb in range(0, FB, 2):
                        act.wait_ge(hid_ready, n * FB + fb + 1)
                        act.activation(F[p][:, fb, :], B[p][:, fb, :], ACT.Relu, bias=B1[p][:, fb:fb + 1])\
                           .then_inc(relu_act, 1)
                if more:
                    begin(n0 + 2, 1 - b)

        @block.vector
        def _(dve):
            for p in range(2):
                dve.sem_inc(stored[p], 32)
            dve.wait_ge(loaded, LOADS + 32)
            dve.wait_ge(set_, 2)
            dve.tensor_tensor(tln[:, :, :], tln[:, :, :], ln8[:, :, :], ALU.subtract).then_inc(tln_ready, 1)
            dve.wait_ge(lnp_ps, 1)
            dve.tensor_tensor(lnp[:, :, :], lnp[:, :, :], B[0][:, 0, 0:2 * P].rearrange("p (o d) -> p o d", o=2), ALU.add)\
               .then_inc(lnp_ready, 1)
            dve.wait_ge(lnp_ready, 1)

            def measure(n0, b):
                for p, n in enumerate((n0, n0 + 1)):
                    x = H[:, bass.ds(n, 1), :].rearrange("p o (c d) -> p (o c) d", c=CH)
                    dve.tensor_copy(X[b][p][:, :, :], x).then_inc(x_ready, 1)
                    dve.wait_ge(x_ready, n + 1)
                    ln_measure(dve, ln, X[b][p], n, p)

            def normalise(n0, b):
                for p, n in enumerate((n0, n0 + 1)):
                    wait_apart(dve, stored[p], n0 * 8 + 16, passed)
                    ln_normalise(dve, ln, XN[b][p], X[b][p], n, p).then_inc(xn_ready, 1)

            def gate_mean(n0):
                for p, n in enumerate((n0, n0 + 1)):
                    dve.wait_ge(gs_ready, n + 1)
                    dve.tensor_scalar(GM[p][:, :], GS[p][:, :], 1.0 / SEQ, None, ALU.mult).then_inc(gm_ready, 1)
                    dve.wait_ge(gm_ready, n + 1)
                    dve.tensor_scalar(GR[p][:, :], ones[:, :], GM[p][:, :], None, ALU.mult).then_inc(gr_ready, 1)

            measure(0, 0)
            normalise(0, 0)
            gate_mean(0)
            for n0, _, b, more, _ in turns(dve):
                ns = (n0, n0 + 1)
                for p, n in enumerate(ns):
                    dve.wait_ge(gb_ready, n + 1)
                    dve.tensor_tensor(BT[p][:, :, :], tb1[:, :, :], GB[p][:, :].unsqueeze(1).broadcast_to([P, FB, TASKS]),
                                      ALU.mult).then_inc(b1_steps, 1)
                    dve.wait_ge(b1_steps, n * 3 + 1)
                    dve.tensor_reduce(BS[p][:, :], BT[p][:, :, :], AX_X, ALU.add).then_inc(b1_steps, 1)
                    dve.wait_ge(b1_steps, n * 3 + 2)
                    dve.tensor_tensor(B1[p][:, :], BS[p][:, :], b1[:, :], ALU.add).then_inc(b1_steps, 1)
                    for e in range(TASKS):
                        if e:
                            dve.wait_ge(wm2_steps, n * TASKS + e)
                        dve.scalar_tensor_tensor(
                            out=WM2[p][:, :], in0=tw2[:, e, :, :].rearrange("p b d -> p (b d)"), scalar=GB[p][:, e:e + 1],
                            in1=WM2[p][:, :] if e else w2[:, :], op0=ALU.mult, op1=ALU.add).then_inc(wm2_steps, 1)
                for p, n in enumerate(ns):
                    dve.wait_ge(w1_ps, n + 1)
                    dve.tensor_tensor(WM1[p][:, :], w1[:, :], B[p][:, 2, :], ALU.add).then_inc(wm1_ready, 1)
                if more:
                    measure(n0 + 2, 1 - b)
                for p, n in enumerate(ns):
                    dve.wait_ge(b1_steps, n * 3 + 3)
                    for fb in range(1, FB, 2):
                        dve.wait_ge(hid_ready, n * FB + fb + 1)
                        dve.tensor_scalar(F[p][:, fb, :], B[p][:, fb, :], B1[p][:, fb:fb + 1], 0.0, ALU.add, ALU.max)\
                           .then_inc(relu_dve, 1)
                if more:
                    normalise(n0 + 2, 1 - b)
                for p, n in enumerate(ns):
                    dve.wait_ge(y_ready, n + 1)
                    dve.tensor_tensor(XN[b][p][:, :, :], XN[b][p][:, :, :],
                                      B[p][:, 0, :].rearrange("p (c d) -> p c d", c=CH), ALU.add)\
                       .then_inc(r_ready, 1)
                    dve.wait_ge(r_ready, n + 1)
                    ln_measure(dve, ln_out, XN[b][p], n, p)
                if more:
                    gate_mean(n0 + 2)
                for p, n in enumerate(ns):
                    ln_normalise(dve, ln_out, XN[b][p], XN[b][p], n, p).then_inc(nr_ready, 1)
                    dve.wait_ge(nr_ready, n + 1)
                    dve.tensor_tensor(XN[b][p][:, :, :], XN[b][p][:, :, :],
                                      lnp[:, 0, :].unsqueeze(1).broadcast_to([P, CH, P]), ALU.mult)\
                       .then_inc(gain_done, 1)
                    dve.wait_ge(gain_done, n + 1)
                    dve.wait_ge(xb_ready, n + 1)
                    dve.tensor_tensor(XN[b][p][:, :, :], XN[b][p][:, :, :], X[b][p][:, :, :], ALU.add).then_inc(out_ready, 1)

        @block.tensor
        def _(pe):
            pe.wait_ge(tln_ready, 1)
            for j in range(2):
                last = pe.matmul(B[0][:, 0, chunk(j)], merge[:, :], tln[:, j, :], start=(j == 0), stop=(j == 1),
                                 skip_group_check=True)
            last.then_inc(lnp_ps, 1)
            pe.wait_ge(lnp_ready, 1)

            def begin(n0, b):
                for p, n in enumerate((n0, n0 + 1)):
                    pe.wait_ge(xn_ready, n + 1)
                    for c in range(CH):
                        last = pe.transpose(B[p][:, TURNED, chunk(c)], XN[b][p][:, c, :], ident)
                    last.then_inc(xnT_ready, 1)
                for p, n in enumerate((n0, n0 + 1)):
                    pe.wait_ge(xt_ready, n + 1)
                    pe.matmul(B[p][:, GATE, :], wg1[:, :], XT[b][p][:, :], start=True, stop=True).then_inc(gh_ps, 1)

            begin(0, 0)
            for n0, _, b, more, _ in turns(pe):
                ns = (n0, n0 + 1)
                for p, n in enumerate(ns):
                    pe.wait_ge(gr_ready, n + 1)
                    pe.matmul(B[p][:, GATE, 0:TASKS], GR[p][:, :], wg2[:, :], start=True, stop=False, skip_group_check=True)
                    pe.matmul(B[p][:, GATE, 0:TASKS], ones_row, gb2[:, :], start=False, stop=True, skip_group_check=True)
                    pe.matmul(B[p][0:TASKS, GATE, P:2 * P], wg2[:, :], GR[p][:, :], start=False, stop=False,
                              skip_group_check=True)
                    pe.matmul(B[p][0:TASKS, GATE, P:2 * P], gb2[:, :], ones_row, start=False, stop=True,
                              skip_group_check=True).then_inc(g_ps, 1)
                for p, n in enumerate(ns):
                    pe.wait_ge(dg_ready, n + 1)
                    for e in range(TASKS):
                        last = pe.matmul(B[p][:, 2, :], DG[p][:, e, :], tw1[:, e, :], start=(e == 0),
                                         stop=(e == TASKS - 1))
                    last.then_inc(w1_ps, 1)
                for p, n in enumerate(ns):
                    pe.wait_ge(wm1_ready, n + 1)
                    pe.wait_ge(gc_ready, n + 1)
                    for fb in range(FB):
                        pe.matmul(B[p][:, fb, :], WM1[p][:, chunk(fb)], XT[b][p][:, :], start=True, stop=True)\
                          .then_inc(hid_ready, 1)
                for p, n in enumerate(ns):
                    pe.wait_ge(relu_act, n * FB // 2 + FB // 2)
                    pe.wait_ge(relu_dve, n * FB // 2 + FB // 2)
                    pe.wait_ge(wm2_steps, n * TASKS + TASKS)
                    pe.matmul(B[p][:, 0, :], ones_row, b2[:, :, :].rearrange("o c d -> o (c d)"),
                              start=True, stop=False, skip_group_check=True)
                    pe.matmul(B[p][:, 0, :], GC[p][:, :], tb2[:, :, :].rearrange("o c d -> o (c d)"),
                              start=False, stop=False, skip_group_check=True)
                    for c in range(CH):
                        for fb in range(FB):
                            last = pe.matmul(B[p][:, 0, chunk(c)], F[p][:, fb, chunk(c)], WM2[p][:, chunk(fb)],
                                             start=False, stop=(c == CH - 1 and fb == FB - 1),
                                             skip_group_check=True)
                    last.then_inc(y_ready, 1)
                if more:
                    begin(n0 + 2, 1 - b)


TRANSPOSED = ("L0_ffn_gate_w", "L0_ffn_shared_gate_up", "L0_ffn_shared_down", "L0_ffn_expert_gate_up",
              "L0_ffn_expert_down", "L1_attn_q_w", "L1_attn_kv_w", "L1_ffn_gfc1_w", "L1_ffn_gfc2_w",
              "L1_ffn_W1", "L1_ffn_W2", "L1_ffn_tv_W1", "L1_ffn_tv_W2")
IN_COLUMNS = ("L0_attn_b1", "L1_ffn_b1")


def build(nc, a, out):
    with ExitStack() as ctx:
        sb, ps, sem = makers(nc, ctx)
        passed = sem("waits_passed")
        H = sb("H", [P, SEQS, SEQ])
        ident = sb("ident", [P, P])
        half = sb("minus_half", [P, CH])
        ones = sb("ones_row", [1, P])
        set_ = sem("consts_set")
        ident_done = sem("ident_done")
        with nc.Block() as block:
            @block.gpsimd
            def _(pool):
                pool.memset(ident[:, :], 0.0).then_inc(set_, 1)
                pool.memset(half[:, :], -0.5).then_inc(set_, 1)
                pool.memset(ones[:, :], 1.0).then_inc(set_, 1)
                pool.wait_ge(set_, 3)
                pool.affine_select(out=ident[:, :], in_=ident[:, :], compare_op=ALU.not_equal, fill=1.0, base=0,
                                   pattern=[[-1, P]], channel_multiplier=1).then_inc(ident_done, 1)
                pool.wait_ge(ident_done, 1)
        consts = {"ident": ident[:, :], "minus_half": half[:, :], "ones_row": ones[:, :],
                  "passed": passed}
        linear_attention_phase(nc, a, H, consts)
        expert_phase(nc, a, H, consts)
        cross_attention_phase(nc, a, H, consts)
        merged_ffn_phase(nc, a, H, out, consts)


def positions():
    pos = np.arange(1, SEQ + 1, dtype=np.float32)[:, None]
    i = np.arange(P)
    exponent = np.where(i % 2 == 0, i, i + 1).astype(np.float32) / np.float32(P)
    angle = pos / np.power(np.float32(10000.0), exponent)
    return np.where(i % 2 == 0, np.cos(angle), np.sin(angle)).astype(np.float32)


def kernel(**inputs):
    import concourse.bacc as bacc
    from concourse.bass_utils import run_bass_kernel_spmd as run

    nc = bacc.Bacc("TRN2", target_bir_lowering=False, num_devices=1)
    given = {k: np.asarray(v) for k, v in inputs.items()}
    x = given.pop("x")
    arrays = {"ids": x.reshape(SEQS * CH, P).T, "table": given.pop("L0_tok_W").T, "pos": positions()}
    for name in TRANSPOSED:
        w = given.pop(name)
        arrays[name] = w.swapaxes(-1, -2)
    for name in IN_COLUMNS:
        arrays[name] = given.pop(name).reshape(-1, P).T
    arrays["L1_ffn_tv_b1"] = given.pop("L1_ffn_tv_b1").reshape(TASKS, FB, P).T
    arrays.update(given)
    arrays = {f"in_{k}": np.ascontiguousarray(v) for k, v in arrays.items()}
    a = {k[3:]: nc.dram_tensor(k, v.shape, mybir.dt.from_np(v.dtype), kind="ExternalInput").ap()
         for k, v in arrays.items()}
    out = nc.dram_tensor("out_0", (SEQS, SEQ, P), F32, kind="ExternalOutput").ap()
    build(nc, a, out)
    r = run(nc, [arrays], core_ids=[0])
    return r.results[0]["out_0"]
```
